# Optimizing a Trainium2 kernel written in Bass

```python
import numpy as np
import jax
import jax.numpy as jnp

def _softmax(x, axis=-1):
    return jax.nn.softmax(x, axis=axis)

def _gelu(x):
    return jax.nn.gelu(x, approximate=True)

def _silu(x):
    return jax.nn.silu(x)

def _sigmoid(x):
    return jax.nn.sigmoid(x)

def _layernorm(x, axis=-1, eps=1e-05):
    m = jnp.mean(x, axis=axis, keepdims=True)
    v = jnp.var(x, axis=axis, keepdims=True)
    return (x - m) / jnp.sqrt(v + eps)

def _scatter_add(tgt, idx, src, axis=0):
    return tgt.at[idx].add(src)

def _segment_sum(src, seg, n):
    return jax.ops.segment_sum(src, seg, n)
kernel_name = 'mk_xattn_ffn_d2_seqx_r8_65f710'

def setup_inputs(seed: int=0):
    np.random.seed(seed)
    _w = jnp.asarray

    def _rec_inputs():
        import jax
        import jax.numpy as jnp
        _rk = jax.random.key(seed)
        x = -0.0002928 + 1 * jax.random.normal(jax.random.fold_in(_rk, 1), (64, 128, 128), jnp.float32)
        _lenS = 128 - jax.random.randint(jax.random.fold_in(_rk, 7), (64,), 0, max(1, 128 // 4) + 1, jnp.int32)
        _lenS2 = 77 - jax.random.randint(jax.random.fold_in(_rk, 8), (64,), 0, max(1, 77 // 4) + 1, jnp.int32)
        _ctx_1024P = jax.random.normal(jax.random.fold_in(_rk, 11), (64, 16, 128), jnp.float32)
        _ctx_1024c = jax.random.dirichlet(jax.random.fold_in(_rk, 511), 0.3 * jnp.ones((16,), jnp.float32), (64, 77))
        _ctx_1024t = jnp.einsum('bsk,bkd->bsd', _ctx_1024c, _ctx_1024P)
        _ctx_1024t = _ctx_1024t * jax.lax.rsqrt(jnp.mean(jnp.square(_ctx_1024t)) + 1e-12) * 0.953939
        ctx_1024 = -1.39393e-06 + 0.999914 * (_ctx_1024t + 0.3 * jax.random.normal(jax.random.fold_in(_rk, 611), (64, 77, 128), jnp.float32))
        return (x, ctx_1024)
    x, ctx_1024 = _rec_inputs()

    def _L0_xattn_setup():
        import jax, jax.numpy as jnp
        import numpy as np
        EMBED_DIM = 128
        NUM_HEADS = 16
        HEAD_DIM = EMBED_DIM // NUM_HEADS
        B, S = (2, 256)

        def _split_heads(x):
            b, s, _ = x.shape
            return x.reshape(b, s, NUM_HEADS, HEAD_DIM).transpose(0, 2, 1, 3)
        key = jax.random.key(seed)
        ks = jax.random.split(key, 11)
        scale = 1.0 / np.sqrt(EMBED_DIM)
        inp = {'q': jax.random.normal(ks[0], (B, S, EMBED_DIM), jnp.float32), 'k': jax.random.normal(ks[1], (B, S, EMBED_DIM), jnp.float32), 'v': jax.random.normal(ks[2], (B, S, EMBED_DIM), jnp.float32), 'Wq': jax.random.normal(ks[3], (EMBED_DIM, EMBED_DIM), jnp.float32) * scale, 'bq': jnp.zeros((EMBED_DIM,), jnp.float32), 'Wk': jax.random.normal(ks[4], (EMBED_DIM, EMBED_DIM), jnp.float32) * scale, 'bk': jnp.zeros((EMBED_DIM,), jnp.float32), 'Wv': jax.random.normal(ks[5], (EMBED_DIM, EMBED_DIM), jnp.float32) * scale, 'bv': jnp.zeros((EMBED_DIM,), jnp.float32), 'Wo': jax.random.normal(ks[6], (EMBED_DIM, EMBED_DIM), jnp.float32) * scale, 'bo': jnp.zeros((EMBED_DIM,), jnp.float32)}
        return inp
    _L0_xattn_all = _L0_xattn_setup()
    _L0_xattn_in = {k: v for k, v in _L0_xattn_all.items() if k in ('Wq', 'bq', 'Wk', 'bk', 'Wv', 'bv', 'Wo', 'bo')}
    del _L0_xattn_all

    def _L0_ffn_setup():
        import jax, jax.numpy as jnp
        import numpy as np
        D_MODEL = 128
        N_HEADS = 16
        HEAD_DIM = D_MODEL // N_HEADS
        KV_LATENT = 64
        N_EXPERTS = 4
        D_HIDDEN = 4 * D_MODEL
        B, T = (2, 128)

        def rmsnorm(x, w, eps=1e-06):
            return w * (x * jax.lax.rsqrt(jnp.mean(x * x, axis=-1, keepdims=True) + eps))

        def layernorm(x, g, b, eps=1e-05):
            mu = jnp.mean(x, axis=-1, keepdims=True)
            var = jnp.mean((x - mu) ** 2, axis=-1, keepdims=True)
            return (x - mu) * jax.lax.rsqrt(var + eps) * g + b

        def apply_rope(x):
            t, d = (x.shape[2], x.shape[3])
            half = d // 2
            pos = jnp.arange(t, dtype=x.dtype)[:, None]
            inv_freq = 1.0 / 10000.0 ** (jnp.arange(half, dtype=x.dtype) / half)
            ang = pos * inv_freq[None, :]
            sin, cos = (jnp.sin(ang), jnp.cos(ang))
            x1, x2 = (x[..., :half], x[..., half:])
            return jnp.concatenate([x1 * cos - x2 * sin, x1 * sin + x2 * cos], axis=-1)

        def mla_attention(x, Wq, Wdkv, Wuk, Wuv, Wo, ln_g, ln_b):
            b, t, _ = x.shape
            q = (x @ Wq.T).reshape(b, t, N_HEADS, HEAD_DIM).transpose(0, 2, 1, 3)
            latent = layernorm(x @ Wdkv.T, ln_g, ln_b)
            k = (latent @ Wuk.T).reshape(b, t, N_HEADS, HEAD_DIM).transpose(0, 2, 1, 3)
            v = (latent @ Wuv.T).reshape(b, t, N_HEADS, HEAD_DIM).transpose(0, 2, 1, 3)
            q = apply_rope(q)
            k = apply_rope(k)
            scores = jnp.einsum('bhqd,bhkd->bhqk', q, k) / np.sqrt(HEAD_DIM)
            causal = jnp.tril(jnp.ones((t, t), dtype=bool))
            scores = jnp.where(causal, scores, -jnp.inf)
            attn = jax.nn.softmax(scores, axis=-1)
            out = jnp.einsum('bhqk,bhkd->bhqd', attn, v).transpose(0, 2, 1, 3).reshape(b, t, D_MODEL)
            return out @ Wo.T

        def moe(x, gate_w, gate_b, W1, b1, W2, b2):
            logits = x @ gate_w.T + gate_b
            top = jnp.argmax(logits, axis=-1)
            onehot = jax.nn.one_hot(top, N_EXPERTS, dtype=x.dtype)
            h = jax.nn.relu(jnp.einsum('btd,ehd->bteh', x, W1) + b1)
            y = jnp.einsum('bteh,edh->bted', h, W2) + b2
            return jnp.einsum('bted,bte->btd', y, onehot)
        key = jax.random.key(seed)
        ks = jax.random.split(key, 16)
        s = lambda fan_in: 1.0 / np.sqrt(fan_in)
        return {'x': jax.random.normal(ks[0], (B, T, D_MODEL), jnp.float32), 'norm1_w': jnp.ones((D_MODEL,), jnp.float32), 'norm2_w': jnp.ones((D_MODEL,), jnp.float32), 'Wq': jax.random.normal(ks[1], (D_MODEL, D_MODEL), jnp.float32) * s(D_MODEL), 'Wdkv': jax.random.normal(ks[2], (KV_LATENT, D_MODEL), jnp.float32) * s(D_MODEL), 'Wuk': jax.random.normal(ks[3], (D_MODEL, KV_LATENT), jnp.float32) * s(KV_LATENT), 'Wuv': jax.random.normal(ks[4], (D_MODEL, KV_LATENT), jnp.float32) * s(KV_LATENT), 'Wo': jax.random.normal(ks[5], (D_MODEL, D_MODEL), jnp.float32) * s(D_MODEL), 'ln_g': jnp.ones((KV_LATENT,), jnp.float32), 'ln_b': jnp.zeros((KV_LATENT,), jnp.float32), 'gate_w': jax.random.normal(ks[6], (N_EXPERTS, D_MODEL), jnp.float32) * s(D_MODEL), 'gate_b': jnp.zeros((N_EXPERTS,), jnp.float32), 'W1': jax.random.normal(ks[7], (N_EXPERTS, D_HIDDEN, D_MODEL), jnp.float32) * s(D_MODEL), 'b1': jnp.zeros((N_EXPERTS, D_HIDDEN), jnp.float32), 'W2': jax.random.normal(ks[8], (N_EXPERTS, D_MODEL, D_HIDDEN), jnp.float32) * s(D_HIDDEN), 'b2': jnp.zeros((N_EXPERTS, D_MODEL), jnp.float32)}
    _L0_ffn_all = _L0_ffn_setup()
    _L0_ffn_in = {k: v for k, v in _L0_ffn_all.items() if k in ('norm1_w', 'norm2_w', 'Wq', 'Wdkv', 'Wuk', 'Wuv', 'Wo', 'ln_g', 'ln_b', 'gate_w', 'gate_b', 'W1', 'b1', 'W2', 'b2')}
    del _L0_ffn_all

    def _L1_xattn_setup():
        import jax, jax.numpy as jnp
        import numpy as np
        HEADS = 8
        DIM_HEAD = 64
        DIM = 128
        CTX_DIM = 128
        HIDDEN = HEADS * DIM_HEAD
        key = jax.random.key(seed)
        ks = jax.random.split(key, 7)
        b, n, m = (2, 256, 256)
        x = jax.random.normal(ks[0], (b, n, DIM), dtype=jnp.float32)
        context = jax.random.normal(ks[1], (b, m, CTX_DIM), dtype=jnp.float32)
        Wq = jax.random.normal(ks[2], (DIM, HIDDEN), dtype=jnp.float32) * (1.0 / np.sqrt(DIM))
        Wk = jax.random.normal(ks[3], (CTX_DIM, HIDDEN), dtype=jnp.float32) * (1.0 / np.sqrt(CTX_DIM))
        Wv = jax.random.normal(ks[4], (CTX_DIM, HIDDEN), dtype=jnp.float32) * (1.0 / np.sqrt(CTX_DIM))
        Wo = jax.random.normal(ks[5], (HIDDEN, DIM), dtype=jnp.float32) * (1.0 / np.sqrt(HIDDEN))
        bo = jax.random.normal(ks[6], (DIM,), dtype=jnp.float32) * 0.01
        return {'x': x, 'context': context, 'Wq': Wq, 'Wk': Wk, 'Wv': Wv, 'Wo': Wo, 'bo': bo}
    _L1_xattn_all = _L1_xattn_setup()
    _L1_xattn_in = {k: v for k, v in _L1_xattn_all.items() if k in ('Wq', 'Wk', 'Wv', 'Wo', 'bo')}
    del _L1_xattn_all

    def _L1_ffn_setup():
        import jax, jax.numpy as jnp
        import numpy as np
        HIDDEN = 128
        NUM_EXPERTS = 8
        TOP_K = 2
        FFN = 512
        BATCH, SEQ = (4, 256)
        key = jax.random.key(seed)
        k_x, k_r, k_w1, k_w2 = jax.random.split(key, 4)
        x = jax.random.normal(k_x, (BATCH, SEQ, HIDDEN), dtype=jnp.float32)
        router_w = jax.random.normal(k_r, (NUM_EXPERTS, HIDDEN), dtype=jnp.float32) * (1.0 / np.sqrt(HIDDEN))
        lim = float(np.sqrt(6.0 / (FFN + HIDDEN)))
        expert_w1 = jax.random.uniform(k_w1, (NUM_EXPERTS, FFN, HIDDEN), dtype=jnp.float32, minval=-lim, maxval=lim)
        expert_w2 = jax.random.uniform(k_w2, (NUM_EXPERTS, HIDDEN, FFN), dtype=jnp.float32, minval=-lim, maxval=lim)
        return {'x': x, 'router_w': router_w, 'expert_w1': expert_w1, 'expert_w2': expert_w2}
    _L1_ffn_all = _L1_ffn_setup()
    _L1_ffn_in = {k: v for k, v in _L1_ffn_all.items() if k in ('router_w', 'expert_w1', 'expert_w2')}
    del _L1_ffn_all
    return {'x': x, 'ctx_1024': ctx_1024, 'L0_xattn_Wq': _L0_xattn_in['Wq'], 'L0_xattn_bq': _L0_xattn_in['bq'], 'L0_xattn_Wk': _L0_xattn_in['Wk'], 'L0_xattn_bk': _L0_xattn_in['bk'], 'L0_xattn_Wv': _L0_xattn_in['Wv'], 'L0_xattn_bv': _L0_xattn_in['bv'], 'L0_xattn_Wo': _L0_xattn_in['Wo'], 'L0_xattn_bo': _L0_xattn_in['bo'], 'L0_ffn_norm1_w': _L0_ffn_in['norm1_w'], 'L0_ffn_norm2_w': _L0_ffn_in['norm2_w'], 'L0_ffn_Wq': _L0_ffn_in['Wq'], 'L0_ffn_Wdkv': _L0_ffn_in['Wdkv'], 'L0_ffn_Wuk': _L0_ffn_in['Wuk'], 'L0_ffn_Wuv': _L0_ffn_in['Wuv'], 'L0_ffn_Wo': _L0_ffn_in['Wo'], 'L0_ffn_ln_g': _L0_ffn_in['ln_g'], 'L0_ffn_ln_b': _L0_ffn_in['ln_b'], 'L0_ffn_gate_w': _L0_ffn_in['gate_w'], 'L0_ffn_gate_b': _L0_ffn_in['gate_b'], 'L0_ffn_W1': _L0_ffn_in['W1'], 'L0_ffn_b1': _L0_ffn_in['b1'], 'L0_ffn_W2': _L0_ffn_in['W2'], 'L0_ffn_b2': _L0_ffn_in['b2'], 'L1_xattn_Wq': _L1_xattn_in['Wq'], 'L1_xattn_Wk': _L1_xattn_in['Wk'], 'L1_xattn_Wv': _L1_xattn_in['Wv'], 'L1_xattn_Wo': _L1_xattn_in['Wo'], 'L1_xattn_bo': _L1_xattn_in['bo'], 'L1_ffn_router_w': _L1_ffn_in['router_w'], 'L1_ffn_expert_w1': _L1_ffn_in['expert_w1'], 'L1_ffn_expert_w2': _L1_ffn_in['expert_w2']}

def reference(x, ctx_1024, L0_xattn_Wq, L0_xattn_bq, L0_xattn_Wk, L0_xattn_bk, L0_xattn_Wv, L0_xattn_bv, L0_xattn_Wo, L0_xattn_bo, L0_ffn_norm1_w, L0_ffn_norm2_w, L0_ffn_Wq, L0_ffn_Wdkv, L0_ffn_Wuk, L0_ffn_Wuv, L0_ffn_Wo, L0_ffn_ln_g, L0_ffn_ln_b, L0_ffn_gate_w, L0_ffn_gate_b, L0_ffn_W1, L0_ffn_b1, L0_ffn_W2, L0_ffn_b2, L1_xattn_Wq, L1_xattn_Wk, L1_xattn_Wv, L1_xattn_Wo, L1_xattn_bo, L1_ffn_router_w, L1_ffn_expert_w1, L1_ffn_expert_w2):
    import jax
    import jax.numpy as jnp

    def _L0_xattn_ref(q, k, v, Wq, bq, Wk, bk, Wv, bv, Wo, bo):
        import jax, jax.numpy as jnp
        import numpy as np
        EMBED_DIM = 128
        NUM_HEADS = 16
        HEAD_DIM = EMBED_DIM // NUM_HEADS
        B, S = (2, 256)

        def _split_heads(x):
            b, s, _ = x.shape
            return x.reshape(b, s, NUM_HEADS, HEAD_DIM).transpose(0, 2, 1, 3)
        query = _split_heads(q @ Wq + bq)
        key_ = _split_heads(k @ Wk + bk)
        value = _split_heads(v @ Wv + bv)
        logits = jnp.einsum('bhqd,bhkd->bhqk', query, key_) / jnp.sqrt(jnp.asarray(HEAD_DIM, jnp.float32))
        weights = jax.nn.softmax(logits, axis=-1)
        attn = jnp.einsum('bhqk,bhkd->bhqd', weights, value)
        concat = attn.transpose(0, 2, 1, 3).reshape(q.shape[0], -1, EMBED_DIM)
        return concat @ Wo + bo

    def _L0_ffn_ref(x, norm1_w, norm2_w, Wq, Wdkv, Wuk, Wuv, Wo, ln_g, ln_b, gate_w, gate_b, W1, b1, W2, b2):
        import jax, jax.numpy as jnp
        import numpy as np
        D_MODEL = 128
        N_HEADS = 16
        HEAD_DIM = D_MODEL // N_HEADS
        KV_LATENT = 64
        N_EXPERTS = 4
        D_HIDDEN = 4 * D_MODEL
        B, T = (2, 128)

        def rmsnorm(x, w, eps=1e-06):
            return w * (x * jax.lax.rsqrt(jnp.mean(x * x, axis=-1, keepdims=True) + eps))

        def layernorm(x, g, b, eps=1e-05):
            mu = jnp.mean(x, axis=-1, keepdims=True)
            var = jnp.mean((x - mu) ** 2, axis=-1, keepdims=True)
            return (x - mu) * jax.lax.rsqrt(var + eps) * g + b

        def apply_rope(x):
            t, d = (x.shape[2], x.shape[3])
            half = d // 2
            pos = jnp.arange(t, dtype=x.dtype)[:, None]
            inv_freq = 1.0 / 10000.0 ** (jnp.arange(half, dtype=x.dtype) / half)
            ang = pos * inv_freq[None, :]
            sin, cos = (jnp.sin(ang), jnp.cos(ang))
            x1, x2 = (x[..., :half], x[..., half:])
            return jnp.concatenate([x1 * cos - x2 * sin, x1 * sin + x2 * cos], axis=-1)

        def mla_attention(x, Wq, Wdkv, Wuk, Wuv, Wo, ln_g, ln_b):
            b, t, _ = x.shape
            q = (x @ Wq.T).reshape(b, t, N_HEADS, HEAD_DIM).transpose(0, 2, 1, 3)
            latent = layernorm(x @ Wdkv.T, ln_g, ln_b)
            k = (latent @ Wuk.T).reshape(b, t, N_HEADS, HEAD_DIM).transpose(0, 2, 1, 3)
            v = (latent @ Wuv.T).reshape(b, t, N_HEADS, HEAD_DIM).transpose(0, 2, 1, 3)
            q = apply_rope(q)
            k = apply_rope(k)
            scores = jnp.einsum('bhqd,bhkd->bhqk', q, k) / np.sqrt(HEAD_DIM)
            causal = jnp.tril(jnp.ones((t, t), dtype=bool))
            scores = jnp.where(causal, scores, -jnp.inf)
            attn = jax.nn.softmax(scores, axis=-1)
            out = jnp.einsum('bhqk,bhkd->bhqd', attn, v).transpose(0, 2, 1, 3).reshape(b, t, D_MODEL)
            return out @ Wo.T

        def moe(x, gate_w, gate_b, W1, b1, W2, b2):
            logits = x @ gate_w.T + gate_b
            top = jnp.argmax(logits, axis=-1)
            onehot = jax.nn.one_hot(top, N_EXPERTS, dtype=x.dtype)
            h = jax.nn.relu(jnp.einsum('btd,ehd->bteh', x, W1) + b1)
            y = jnp.einsum('bteh,edh->bted', h, W2) + b2
            return jnp.einsum('bted,bte->btd', y, onehot)
        x = x + mla_attention(rmsnorm(x, norm1_w), Wq, Wdkv, Wuk, Wuv, Wo, ln_g, ln_b)
        x = x + moe(rmsnorm(x, norm2_w), gate_w, gate_b, W1, b1, W2, b2)
        return x

    def _L1_xattn_ref(x, context, Wq, Wk, Wv, Wo, bo):
        import jax, jax.numpy as jnp
        import numpy as np
        HEADS = 8
        DIM_HEAD = 64
        DIM = 128
        CTX_DIM = 128
        HIDDEN = HEADS * DIM_HEAD
        b, n, _ = x.shape
        m = context.shape[1]
        scale = DIM_HEAD ** (-0.5)
        q = (x @ Wq).reshape(b, n, HEADS, DIM_HEAD).transpose(0, 2, 1, 3)
        k = (context @ Wk).reshape(b, m, HEADS, DIM_HEAD).transpose(0, 2, 1, 3)
        v = (context @ Wv).reshape(b, m, HEADS, DIM_HEAD).transpose(0, 2, 1, 3)
        scores = jnp.einsum('bhnd,bhmd->bhnm', q, k) * scale
        attn = jax.nn.softmax(scores, axis=-1)
        out = jnp.einsum('bhnm,bhmd->bhnd', attn, v)
        out = out.transpose(0, 2, 1, 3).reshape(b, n, HIDDEN)
        return out @ Wo + bo

    def _L1_ffn_ref(x, router_w, expert_w1, expert_w2):
        import jax, jax.numpy as jnp
        import numpy as np
        HIDDEN = 128
        NUM_EXPERTS = 8
        TOP_K = 2
        FFN = 512
        BATCH, SEQ = (4, 256)
        B, S, D = x.shape
        xf = x.reshape(-1, D)
        scores = xf @ router_w.T
        top_v, top_i = jax.lax.top_k(scores, TOP_K)
        routing_w = jax.nn.softmax(top_v, axis=-1)
        out = jnp.zeros_like(xf)
        for e in range(NUM_EXPERTS):
            w_e = jnp.sum(jnp.where(top_i == e, routing_w, 0.0), axis=-1)
            h = jax.nn.gelu(xf @ expert_w1[e].T, approximate=False)
            out = out + h @ expert_w2[e].T * w_e[:, None]
        return out.reshape(B, S, D)
    x = x + _L0_xattn_ref(_layernorm(x, axis=-1), ctx_1024, ctx_1024, L0_xattn_Wq, L0_xattn_bq, L0_xattn_Wk, L0_xattn_bk, L0_xattn_Wv, L0_xattn_bv, L0_xattn_Wo, L0_xattn_bo)
    x = x + _L0_ffn_ref(_layernorm(x, axis=-1), L0_ffn_norm1_w, L0_ffn_norm2_w, L0_ffn_Wq, L0_ffn_Wdkv, L0_ffn_Wuk, L0_ffn_Wuv, L0_ffn_Wo, L0_ffn_ln_g, L0_ffn_ln_b, L0_ffn_gate_w, L0_ffn_gate_b, L0_ffn_W1, L0_ffn_b1, L0_ffn_W2, L0_ffn_b2)
    x = x + _L1_xattn_ref(_layernorm(x, axis=-1), ctx_1024, L1_xattn_Wq, L1_xattn_Wk, L1_xattn_Wv, L1_xattn_Wo, L1_xattn_bo)
    x = x + _L1_ffn_ref(_layernorm(x, axis=-1), L1_ffn_router_w, L1_ffn_expert_w1, L1_ffn_expert_w2)
    return x

_drawn_inputs = setup_inputs


def setup_inputs(seed=0):
    import zlib

    import numpy as np

    out = dict(_drawn_inputs(seed))
    spreads = {'L0_xattn_bq': (0.0, 0.1),
     'L0_xattn_bk': (0.0, 0.8),
     'L0_xattn_bv': (0.0, 0.1),
     'L0_xattn_bo': (0.0, 0.1),
     'L0_ffn_norm1_w': (1.0, 0.2),
     'L0_ffn_norm2_w': (1.0, 0.2),
     'L0_ffn_ln_g': (1.0, 0.2),
     'L0_ffn_ln_b': (0.0, 0.1),
     'L0_ffn_gate_b': (0.0, 0.1),
     'L0_ffn_b1': (0.0, 0.1),
     'L0_ffn_b2': (0.0, 0.1)}
    factors = {'L1_xattn_bo': 6.595}
    for name, (base, spread) in spreads.items():
        noise = np.random.default_rng([zlib.crc32(name.encode()), seed]).standard_normal(out[name].shape)
        drawn = base * np.exp(spread * noise) if base else spread * noise
        out[name] = jnp.asarray(drawn.astype(out[name].dtype))
    for name, factor in factors.items():
        out[name] = (out[name] * factor).astype(out[name].dtype)
    return out
```

```python
import numpy as np
from contextlib import ExitStack

import concourse.bass as bass
from concourse import mybir

F32 = mybir.dt.float32
F16 = mybir.dt.float16
BF16 = mybir.dt.bfloat16
U16 = mybir.dt.uint16
ALU = mybir.AluOpType
ACT = mybir.ActivationFunctionType
AX = mybir.AxisListType

P = 128
D = 128
NB = 64
KC = 77
GB = 4
NG = NB // GB
TG = GB * P
H = 16
HD = D // H
HQ = 4
WH_ = 8
WD = 64
WHID = WH_ * WD
LAT = 64
FF = 512
FC = FF // P
E0, E1 = 4, 8
SHIFT = 64.0
LN_EPS, RMS_EPS = 1e-5, 1e-6

SPLIT_COLS = [
    ("ctx", NB * KC),
    ("a_q", D), ("a_k", D), ("a_v", D), ("a_o", D), ("a_bo", D),
    ("m_q", D), ("m_qs", D), ("m_kv", LAT), ("m_k", D), ("m_ks", D), ("m_v", D), ("m_o", D),
    ("w_q", WHID), ("w_k", WHID), ("w_v", WHID), ("w_o", WHID), ("w_bo", D),
    ("gate", E0), ("gate_b", E0), ("router", E1), ("b2", E0 * D),
    ("w1a", E0 * FF), ("w2a", E0 * FF),
]
OFF, _n = {}, 0
for _name, _w in SPLIT_COLS:
    OFF[_name] = _n
    _n += _w
CH = 1024
NSPLIT = -(-_n // CH) * CH
NLATE = 2 * E1 * FF
SMALL = ["bq", "bk", "bv", "n1", "n2", "lg", "lb", "b1"]
SM_OFF = {name: k for k, name in enumerate(SMALL)}
NSMALL = len(SMALL) - 1 + E0 * FC


def lin(g, mult, add=0):
    i, c = g
    return mult * c + add if i is None else i * (2 * mult) + (mult * c + add)


def shift(g, by):
    return g[0], g[1] + by


def is_first(g):
    return g[0] is None and g[1] == 0


def wait(engine, semaphore, value):
    if isinstance(value, int) and value <= 0:
        return
    engine.wait_ge(semaphore, value)


def settle(engine, c):
    engine.sem_inc(c["passed"], 1)


def groups(engine, body):
    for c in (0, 1):
        body((None, c), c, True, True)
    with engine.Fori(1, NG // 2 - 1, 1) as i:
        for c in (0, 1):
            body((i, c), c, True, True)
    body((None, NG - 2), 0, True, False)
    body((None, NG - 1), 1, False, False)


class Parts:

    def __init__(self, hi, lo):
        self.hi, self.lo = hi, lo

    def of(self, name, start, width, rows=P):
        a = OFF[name] + start
        return self.hi[:rows, bass.ds(a, width)], self.lo[:rows, bass.ds(a, width)]


def product(pe, out, left, right, first=True, last=True, check=True):
    (lh, ll), (rh, rl) = left, right
    kw = {} if check else {"skip_group_check": True}
    pe.matmul(out, lh, rh, start=first, stop=False, **kw)
    pe.matmul(out, lh, rl, start=False, stop=False, **kw)
    return pe.matmul(out, ll, rh, start=False, stop=last, **kw)


def split_columns(nc, src, n_cols, hi, lo):
    n = n_cols // CH
    with ExitStack() as ctx:
        stage = ctx.enter_context(nc.sbuf_tensor(f"stage{n_cols}", [P, 2, CH], F32))
        loaded = [ctx.enter_context(nc.semaphore(f"loaded{n_cols}_{k}")) for k in range(2)]
        hi_done = ctx.enter_context(nc.semaphore(f"hi_done{n_cols}"))
        lo_done = ctx.enter_context(nc.semaphore(f"lo_done{n_cols}"))
        block = ctx.enter_context(nc.Block())

        @block.sync
        def _(sp):
            for c in range(n):
                wait(sp, lo_done, c - 1)
                sp.dma_start(stage[:, c % 2, :], src[:, c * CH:(c + 1) * CH]).then_inc(loaded[c % 2], 16)

        @block.scalar
        def _(act):
            for c in range(n):
                act.wait_ge(loaded[c % 2], 16 * (c // 2 + 1))
                act.activation(hi[:, c * CH:(c + 1) * CH], stage[:, c % 2, :], ACT.Copy).then_inc(hi_done, 1)

        @block.vector
        def _(dve):
            for c in range(n):
                dve.wait_ge(hi_done, c + 1)
                dve.tensor_tensor(lo[:, c * CH:(c + 1) * CH], stage[:, c % 2, :], hi[:, c * CH:(c + 1) * CH],
                                  ALU.subtract).then_inc(lo_done, 1)


def load_all(nc, pairs, tag):
    with nc.semaphore(f"loads_{tag}") as loads, nc.Block() as block:
        @block.sync
        def _(sp):
            for dst, src in pairs:
                sp.dma_start(dst, src).then_inc(loads, 16)
            sp.wait_ge(loads, 16 * len(pairs))


def narrow_attention(nc, c, X, Y, latent):
    W, SM = c["parts"], c["small"]
    NK = P if latent else KC
    tag = "m" if latent else "a"
    USES = 8 if latent else 4
    n_q_dma = 12
    with ExitStack() as ctx:
        def sb(name, shape, dt):
            return ctx.enter_context(nc.sbuf_tensor(f"{tag}_{name}", shape, dt))

        def pb(name, shape, dt=F32):
            return ctx.enter_context(nc.psum_tensor(f"{tag}_{name}", shape, dt))

        def sem(name):
            return ctx.enter_context(nc.semaphore(f"{tag}_{name}"))


        Qd = sb("Qd", [P, 2, HQ, HQ, TG], F16)
        Ks = sb("Ks", [P, 2, HQ, GB * NK], F16)
        qh, ql = sb("qh", [P, TG], F16), sb("ql", [P, TG], F16)
        kh, kl = sb("kh", [P, GB * NK], F16), sb("kl", [P, GB * NK], F16)
        V = sb("V", [P, 2, GB, H, HD + 1], F32)
        stats, aggr = sb("stats", [P, GB, 6], F32), sb("aggr", [P, GB, 2], F32)
        var, rstd = sb("var", [P, GB], F32), sb("rstd", [P, GB], F32)
        xn = sb("xn", [P, GB, D], F32)
        xh, xl = sb("xh", [P, TG], F16), sb("xl", [P, TG], F16)
        mx = sb("mx", [P, H], F32)
        ng = sb("ng", [P, H], F16)
        mT = sb("mT", [P, 2, P], F16)
        PT = sb("PT", [P, 2, H, P], F32)
        Os = sb("Os", [P, HQ, P], F32)
        rec = sb("rec", [P, H], F32)
        On = sb("On", [P, D], F32)
        oh, ol = sb("oh", [P, P], F16), sb("ol", [P, P], F16)
        if latent:
            sq, ms = sb("sq", [P, D], F32), sb("ms", [P, GB], F32)
            rv, rr = sb("rv", [P, GB], F32), sb("rr", [P, GB], F32)
            t1, t2 = sb("t1", [P, TG], F32), sb("t2", [P, TG], F32)
            lstats, laggr = sb("lstats", [P, GB, 6], F32), sb("laggr", [P, GB, 2], F32)
            lvar, lrstd = sb("lvar", [P, GB], F32), sb("lrstd", [P, GB], F32)
            latn = sb("latn", [P, GB, LAT], F32)
            lt = sb("lt", [LAT, TG], F32)
            lh, ll = sb("lh", [LAT, TG], F16), sb("ll", [LAT, TG], F16)

        pM = pb("pM", [P, H // 2, P])
        pS = pb("pS", [P, H // 2, P])
        pV = pb("pV", [P, HQ, P])
        pO = pb("pO", [P, 512])
        pP = pb("pP", [P, 512])
        pT = pb("pT", [P, 512])
        pTh = pT[:, 0:P // 2].bitcast(F16)

        zeroed, x_norm, ln_agg, ln_rstd = sem("zeroed"), sem("x_norm"), sem("ln_agg"), sem("ln_rstd")
        ln_st = sem("ln_st")
        sq_done, ms_done, rms_r = sem("sq_done"), sem("ms_done"), sem("rms_r")
        used, hi_made, evac = sem("used"), sem("hi_made"), sem("evac")
        rope_in, rope_sum, rope_lo, rope_mul = sem("rope_in"), sem("rope_sum"), sem("rope_lo"), sem("rope_mul")
        lat_st, lat_agg, lat_rstd, lat_lo = sem("lat_st"), sem("lat_agg"), sem("lat_rstd"), sem("lat_lo")
        q_sent, k_sent = sem("q_sent"), sem("k_sent")
        m_ready, m_max, neg, mt_ready, mt_kept = (sem("m_ready"), sem("m_max"), sem("neg"), sem("mt_ready"),
                                                  sem("mt_kept"))
        s_ready, exp_done, pv_ready, os_kept = sem("s_ready"), sem("exp_done"), sem("pv_ready"), sem("os_kept")
        t1_ready, rec_done, on_done, t2_ready = sem("t1_ready"), sem("rec_done"), sem("on_done"), sem("t2_ready")
        oh_done, ol_done, wo_ready, res_done = sem("oh_done"), sem("ol_done"), sem("wo_ready"), sem("res_done")
        own = sem("own")
        block = ctx.enter_context(nc.Block())

        if latent:
            order = ["q", "qs", "k", "ks", "v", "x", "lat", "latT"]
            first_use = 3
        else:
            order = ["q", "k", "v", "x"]
            first_use = 1

        def use(g, what):
            back = 1 if what in ("x", "lat", "latT") else 0
            return lin(g, USES, first_use + order.index(what) - back * USES)

        if latent:
            slots = {(0, 0): "q", (0, 1): "qs", (1, 0): "k", (1, 1): "ks", (2, 0): "v", (2, 1): "x",
                     (3, 0): "lat", (3, 1): "latT"}
        else:
            slots = {(0, 0): "q", (0, 1): "k", (1, 0): "v", (2, 0): "x"}

        def slot(b, half, g, nxt, nxt2):
            what = slots.get((b, half))
            if what in ("x", "lat", "latT"):
                return (what, shift(g, 2), 2) if nxt2 else (None, None, 0)
            return (what, shift(g, 1), 1) if what and nxt else (None, None, 0)

        start_x = ["x", "lat", "latT"] if latent else ["x"]
        start = ([(w, 0) for w in start_x] + [(w, 0) for w in order if w not in start_x]
                 + [(w, 1) for w in start_x])

        def walk(engine, begin, step, finish):
            begin()
            groups(engine, lambda g, p, nxt, nxt2: [step(g, p, b, nxt, nxt2) for b in range(GB)])
            finish()

        def hi_count(g, what):
            per = [w for w in order if w in (("x", "qs", "ks", "latT") if latent else ("x", "q", "k"))]
            lead = 2 if latent else 1
            back = 1 if what in ("x", "latT") else 0
            return lin(g, len(per), lead + per.index(what) + 1 - back * len(per))

        @block.tensor
        def _(pe):
            pe.wait_ge(zeroed, 8)

            def project(what, g, p):
                u = use(g, what)
                wait(pe, evac, u)
                if what == "x":
                    pe.wait_ge(rms_r if latent else x_norm, lin(g, GB, GB))
                    for b in range(GB):
                        mm = pe.transpose(pP[:, b * P:(b + 1) * P], xn[:, b, :], c["ident"][:])
                elif what in ("q", "qs"):
                    wait(pe, evac, use(g, "x") + 1)
                    mm = product(pe, pP[:, :TG], W.of(f"{tag}_{what}", 0, D), (xh[:], xl[:]))
                elif what in ("k", "ks") and not latent:
                    mm = product(pe, pP[:, :GB * KC], W.of("a_k", 0, D), W.of("ctx", lin(g, GB * KC), GB * KC))
                elif what in ("k", "ks"):
                    pe.wait_ge(lat_lo, lin(g, 1, 1))
                    mm = product(pe, pP[:, :TG], W.of(f"m_{what}", 0, D, LAT), (lh[:], ll[:]))
                elif what == "v":
                    for b in range(GB):
                        if latent:
                            s = slice(b * P, (b + 1) * P)
                            mm = product(pe, pP[:, s], (lh[:, s], ll[:, s]), W.of("m_v", 0, D, LAT))
                        else:
                            mm = product(pe, pP[:KC, b * P:(b + 1) * P], W.of("ctx", lin(g, GB * KC, b * KC), KC),
                                         W.of("a_v", 0, D))
                elif what == "lat":
                    wait(pe, evac, use(g, "x") + 1)
                    for b in range(GB):
                        s = slice(b * P, (b + 1) * P)
                        mm = product(pe, pP[:, b * LAT:(b + 1) * LAT], (xh[:, s], xl[:, s]), W.of("m_kv", 0, LAT))
                elif what == "latT":
                    settle(pe, c)
                    for b in range(GB):
                        mm = pe.transpose(pP[:LAT, b * P:(b + 1) * P], latn[:, b, :], c["ident"][:])
                mm.then_inc(used, 1)

            def maxima(g, p, b, half, gd):
                wait(pe, m_max, lin(gd, 2 * GB, 2 * b + half))
                if b == 0 and half == 0:
                    pe.wait_ge(q_sent, lin(gd, 16 * n_q_dma, 16 * n_q_dma))
                    pe.wait_ge(k_sent, lin(gd, 16 * n_q_dma, 16 * n_q_dma))
                for gg in range(2):
                    hg = 2 * half + gg
                    if latent:
                        pe.matmul(pM[:, 4 * gg:4 * gg + 4, :], c["id16"][:].bitcast(BF16), c["maskM"][:].bitcast(BF16), start=True, stop=False,
                                  skip_group_check=True)
                    for j in range(HQ):
                        mm = pe.matmul(pM[:, 4 * gg + j, :NK], Qd[:, p, hg, j, b * P:(b + 1) * P],
                                       Ks[:, p, hg, b * NK:(b + 1) * NK], start=not latent, stop=True,
                                       skip_group_check=True)
                mm.then_inc(m_ready, 1)

            def max_transpose(g, p, b):
                pe.wait_ge(neg, lin(g, GB, b + 1))
                pe.transpose(pTh[:H, :], ng[:], c["ident16"][:]).then_inc(mt_ready, 1)

            def scores(g, p, b, half):
                wait(pe, exp_done, lin(g, 2 * GB, 2 * b + half))
                if half == 0:
                    pe.wait_ge(mt_kept, lin(g, GB, b + 1))
                for gg in range(2):
                    hg = 2 * half + gg
                    pe.matmul(pS[:NK, 4 * gg:4 * gg + 4, :], Ks[:, p, hg, b * NK:(b + 1) * NK],
                              Qd[:, p, hg, :, b * P:(b + 1) * P], start=True, stop=False, skip_group_check=True)
                    if latent:
                        pe.matmul(pS[:, 4 * gg:4 * gg + 4, :], c["id16"][:].bitcast(BF16), c["maskS"][:].bitcast(BF16), start=False, stop=False,
                                  skip_group_check=True)
                    for j in range(HQ):
                        mm = pe.matmul(pS[:NK, 4 * gg + j, :], c["sel"][:, HQ * hg + j, :NK], mT[:, b % 2, :],
                                       start=False, stop=(j == HQ - 1), skip_group_check=True)
                mm.then_inc(s_ready, 1)

            def values(g, p, b):
                wait(pe, exp_done, lin(g, 2 * GB, 2 * b + 2))
                wait(pe, os_kept, lin(g, GB, b))
                if b == 0:
                    pe.wait_ge(evac, use(g, "v") + 1)
                for hg in range(HQ):
                    for j in range(HQ):
                        h = HQ * hg + j
                        mm = pe.matmul(pV[32 * j:32 * j + HD + 1, hg, :], V[:NK, p, b, h, :], PT[:NK, b % 2, h, :],
                                       start=True, stop=True)
                mm.then_inc(pv_ready, 1)

            def turn_heads(g, b):
                pe.wait_ge(os_kept, lin(g, GB, b + 1))
                wait(pe, res_done, lin(g, GB, b))
                for hg in range(HQ):
                    mm = pe.transpose(pO[:, hg * P:(hg + 1) * P], Os[:, hg, :], c["ident"][:])
                mm.then_inc(t1_ready, 1)

            def turn_output(g, b):
                pe.wait_ge(on_done, lin(g, GB, b + 1))
                pe.transpose(pO[:, :P], On[:], c["ident"][:]).then_inc(t2_ready, 1)

            def project_output(g, b):
                pe.wait_ge(oh_done, lin(g, GB, b + 1))
                pe.wait_ge(ol_done, lin(g, GB, b + 1))
                if latent:
                    mm = product(pe, pO[:, :D], (oh[:], ol[:]), W.of("m_o", 0, D))
                else:
                    product(pe, pO[:, :D], (oh[:], ol[:]), W.of("a_o", 0, D), last=False)
                    bh, bl = W.of("a_bo", 0, D)
                    pe.matmul(pO[:, :D], c["row0"][:], bh, start=False, stop=False)
                    mm = pe.matmul(pO[:, :D], c["row0"][:], bl, start=False, stop=True)
                mm.then_inc(wo_ready, 1)

            def begin():
                for what, k in start:
                    project(what, (None, k), k)
                maxima(None, 0, 0, 0, (None, 0))
                maxima(None, 0, 0, 1, (None, 0))

            def step(g, p, b, nxt, nxt2):
                gn, pn, bn = (g, p, b + 1) if b < GB - 1 else (shift(g, 1), 1 - p, 0)
                gp, pp, bp = (g, p, b - 1) if b else (shift(g, -1), 1 - p, GB - 1)
                more = nxt or b < GB - 1
                before = b > 0 or not is_first(g)
                max_transpose(g, p, b)
                what, gw, far = slot(b, 0, g, nxt, nxt2)
                if what:
                    project(what, gw, None)
                if more:
                    maxima(None, pn, bn, 0, gn)
                if before:
                    values(gp, pp, bp)
                scores(g, p, b, 0)
                if before:
                    turn_heads(gp, bp)
                if more:
                    maxima(None, pn, bn, 1, gn)
                what, gw, far = slot(b, 1, g, nxt, nxt2)
                if what:
                    project(what, gw, None)
                if before:
                    turn_output(gp, bp)
                scores(g, p, b, 1)
                if before:
                    project_output(gp, bp)

            def finish():
                g = (None, NG - 1)
                values(g, 1, GB - 1)
                turn_heads(g, GB - 1)
                turn_output(g, GB - 1)
                project_output(g, GB - 1)

            walk(pe, begin, step, finish)

        @block.scalar
        def _(act):
            def part(what, g):
                u = use(g, what)
                if what == "x":
                    act.wait_ge(used, u + 1)
                    if latent:
                        act.activation(xh[:], pP[:, :TG], ACT.Copy, scale=SM("n1")).then_inc(hi_made, 1)
                    else:
                        act.activation(xh[:], pP[:, :TG], ACT.Copy).then_inc(hi_made, 1)
                elif what in ("q", "k") and not latent:
                    dst, n = (qh, TG) if what == "q" else (kh, GB * KC)
                    act.wait_ge(used, u + 1)
                    wait(act, q_sent if what == "q" else k_sent, lin(g, 16 * n_q_dma, 0))
                    act.activation(dst[:, :n], pP[:, :n], ACT.Identity, bias=SM("b" + what)).then_inc(hi_made, 1)
                elif what in ("qs", "ks"):
                    dst = qh if what == "qs" else kh
                    wait(act, q_sent if what == "qs" else k_sent, lin(g, 16 * n_q_dma, 0))
                    act.wait_ge(rope_sum, lin(g, 2, 1 if what == "qs" else 2))
                    act.activation(dst[:], t1[:], ACT.Copy).then_inc(hi_made, 1)
                elif what == "latT":
                    act.wait_ge(evac, u + 1)
                    act.activation(lh[:], lt[:], ACT.Copy).then_inc(hi_made, 1)

            def squares(g):
                for b in range(GB):
                    act.wait_ge(x_norm, lin(g, GB, b + 1))
                    wait(act, ms_done, lin(g, 1, 0))
                    wait(act, sq_done, lin(g, GB, b))
                    act.activation(sq[:], Y[:, bass.ds(lin(g, GB, b), 1), :], ACT.Square,
                                   accum_out=ms[:, b:b + 1]).then_inc(sq_done, 1)

            def exps(g, p, b, half):
                act.wait_ge(s_ready, lin(g, 2 * GB, 2 * b + half + 1))
                if half == 0:
                    wait(act, pv_ready, lin(g, GB, b - 1))
                act.activation(PT[:NK, b % 2, 8 * half:8 * half + 8, :], pS[:NK, :, :], ACT.Exp,
                               scale=float(1.0 / np.sqrt(HD))).then_inc(exp_done, 1)

            def keep_heads(g, b):
                act.wait_ge(pv_ready, lin(g, GB, b + 1))
                wait(act, t1_ready, lin(g, GB, b))
                act.activation(Os[:], pV[:], ACT.Copy).then_inc(os_kept, 1)

            def output_hi(g, b):
                act.wait_ge(t2_ready, lin(g, GB, b + 1))
                wait(act, wo_ready, lin(g, GB, b))
                if latent:
                    act.activation(oh[:], pO[:, :P], ACT.Copy).then_inc(oh_done, 1)
                else:
                    act.activation(oh[:], pO[:, :P], ACT.Identity, bias=SM("bv")).then_inc(oh_done, 1)

            def begin():
                act.wait_ge(zeroed, 8)
                if latent:
                    squares((None, 0))
                for what, k in start:
                    if latent and what == "x" and k == 1:
                        squares((None, 1))
                    part(what, (None, k))

            def step(g, p, b, nxt, nxt2):
                gp, pp, bp = (g, p, b - 1) if b else (shift(g, -1), 1 - p, GB - 1)
                before = b > 0 or not is_first(g)
                what, gw, far = slot(b, 0, g, nxt, nxt2)
                if what:
                    part(what, gw)
                if before:
                    keep_heads(gp, bp)
                exps(g, p, b, 0)
                if latent and b == 1 and nxt2:
                    squares(shift(g, 2))
                what, gw, far = slot(b, 1, g, nxt, nxt2)
                if what:
                    part(what, gw)
                if before:
                    output_hi(gp, bp)
                exps(g, p, b, 1)

            def finish():
                g = (None, NG - 1)
                keep_heads(g, GB - 1)
                output_hi(g, GB - 1)

            walk(act, begin, step, finish)

        @block.vector
        def _(dve):
            def norm_stats(g):
                for b in range(GB):
                    dve.bn_stats(stats[:, b, :], X[:, bass.ds(lin(g, GB, b), 1), :]).then_inc(ln_st, 1)
                for b in range(GB):
                    dve.wait_ge(ln_st, lin(g, GB, b + 1))
                    if b == 0:
                        wait(dve, ln_rstd, lin(g, 1, 0))
                        wait(dve, x_norm, lin(g, GB, 0))
                    settle(dve, c)
                    dve.bn_aggr(aggr[:, b, :], stats[:, b, :]).then_inc(ln_agg, 1)

            def norm_rows(g):
                dve.wait_ge(ln_rstd, lin(g, 1, 1))
                if not latent:
                    wait(dve, used, use(g, "x") - USES + 1)
                for b in range(GB):
                    n = bass.ds(lin(g, GB, b), 1)
                    dst = Y[:, n, :] if latent else xn[:, b:b + 1, :]
                    dve.tensor_scalar(dst, X[:, n, :], aggr[:, b, 0:1], rstd[:, b:b + 1], ALU.subtract,
                                      ALU.mult).then_inc(x_norm, 1)

            def rms_rows(g):
                dve.wait_ge(ms_done, lin(g, 1, 1))
                if not is_first(g):
                    wait(dve, used, use(g, "x") - USES + 1)
                for b in range(GB):
                    dve.tensor_scalar(xn[:, b:b + 1, :], Y[:, bass.ds(lin(g, GB, b), 1), :], rr[:, b:b + 1], None,
                                      ALU.mult).then_inc(rms_r, 1)

            def part(what, g, p):
                u = use(g, what)
                if what == "x":
                    dve.wait_ge(hi_made, hi_count(g, what))
                    if latent:
                        dve.scalar_tensor_tensor(xl[:], pP[:, :TG], SM("n1"), xh[:], ALU.mult,
                                                 ALU.subtract).then_inc(evac, 1)
                    else:
                        dve.tensor_tensor(xl[:], pP[:, :TG], xh[:], ALU.subtract).then_inc(evac, 1)
                elif what in ("q", "k") and not latent:
                    hi, lo, n = (qh, ql, TG) if what == "q" else (kh, kl, GB * KC)
                    dve.wait_ge(hi_made, hi_count(g, what))
                    dve.scalar_tensor_tensor(lo[:, :n], pP[:, :n], SM("b" + what), hi[:, :n], ALU.add,
                                             ALU.subtract).then_inc(evac, 1)
                elif what in ("q", "qs", "k", "ks"):
                    dve.wait_ge(used, u + 1)
                    if what in ("q", "k"):
                        wait(dve, rope_lo, lin(g, 2, 0 if what == "q" else 1))
                    dst, table = (t1, "cos") if what in ("q", "k") else (t2, "sin")
                    dve.tensor_tensor(dst[:].rearrange("p (b t) -> p b t", b=GB),
                                      pP[:, :TG].rearrange("p (b t) -> p b t", b=GB),
                                      c[table][:].rearrange("p (o t) -> p o t", o=1).to_broadcast([P, GB, P]),
                                      ALU.mult).then_inc(evac, 1)
                elif what == "v":
                    dve.wait_ge(used, u + 1)
                    wait(dve, pv_ready, lin(g, GB, -GB))
                    for b in range(GB):
                        cp = dve.tensor_copy(V[:NK, p, b, :, 0:HD],
                                             pP[:NK, b * P:(b + 1) * P].rearrange("k (h d) -> k h d", h=H))
                    cp.then_inc(evac, 1)
                elif what == "lat":
                    dve.wait_ge(used, u + 1)
                    for b in range(GB):
                        dve.bn_stats(lstats[:, b, :], pP[:, b * LAT:(b + 1) * LAT]).then_inc(lat_st, 1)
                    for b in range(GB):
                        dve.wait_ge(lat_st, lin(g, GB, b + 1))
                        settle(dve, c)
                        dve.bn_aggr(laggr[:, b, :], lstats[:, b, :]).then_inc(lat_agg, 1)
                    dve.wait_ge(lat_rstd, lin(g, 1, 1))
                    for b in range(GB):
                        ts = dve.tensor_scalar(latn[:, b, :], pP[:, b * LAT:(b + 1) * LAT], laggr[:, b, 0:1],
                                               lrstd[:, b:b + 1], ALU.subtract, ALU.mult)
                    ts.then_inc(evac, 1)
                elif what == "latT":
                    dve.wait_ge(used, u + 1)
                    wait(dve, lat_lo, lin(g, 1, 0))
                    dve.tensor_scalar(lt[:], pP[:LAT, :TG], SM("lg", LAT), SM("lb", LAT), ALU.mult,
                                      ALU.add).then_inc(evac, 1)

            def take_max(g, b, half):
                dve.wait_ge(m_ready, lin(g, 2 * GB, 2 * b + half + 1))
                if half == 0:
                    wait(dve, neg, lin(g, GB, b))
                dve.tensor_reduce(out=mx[:, 8 * half:8 * half + 8], in_=pM[:, :, :NK], op=ALU.max,
                                  axis=AX.X).then_inc(m_max, 1)

            def negate(g, b):
                dve.wait_ge(m_max, lin(g, 2 * GB, 2 * b + 2))
                wait(dve, mt_ready, lin(g, GB, b))
                dve.tensor_scalar(ng[:], mx[:], -1.0 / SHIFT, None, ALU.mult).then_inc(neg, 1)

            def keep_max(g, b):
                dve.wait_ge(mt_ready, lin(g, GB, b + 1))
                wait(dve, s_ready, lin(g, 2 * GB, 2 * (b - 1)))
                dve.tensor_copy(mT[:H, b % 2, :], pTh[:H, :]).then_inc(mt_kept, 1)

            def divide(g, b):
                dve.wait_ge(t1_ready, lin(g, GB, b + 1))
                wait(dve, on_done, lin(g, GB, b))
                dve.reciprocal(rec[:].rearrange("p (h o) -> p h o", o=1),
                               pO[:].rearrange("p (h c) -> p h c", h=H)[:, :, HD:HD + 1]).then_inc(rec_done, 1)
                dve.wait_ge(rec_done, lin(g, GB, b + 1))
                wait(dve, t2_ready, lin(g, GB, b))
                dve.tensor_tensor(On[:].rearrange("p (h d) -> p h d", h=H),
                                  pO[:].rearrange("p (h c) -> p h c", h=H)[:, :, 0:HD],
                                  rec[:].rearrange("p (h o) -> p h o", o=1).to_broadcast([P, H, HD]),
                                  ALU.mult).then_inc(on_done, 1)

            def output_lo(g, b):
                dve.wait_ge(oh_done, lin(g, GB, b + 1))
                if latent:
                    dve.tensor_tensor(ol[:], pO[:, :P], oh[:], ALU.subtract).then_inc(ol_done, 1)
                else:
                    dve.scalar_tensor_tensor(ol[:], pO[:, :P], SM("bv"), oh[:], ALU.add,
                                             ALU.subtract).then_inc(ol_done, 1)

            def residual(g, b):
                n = bass.ds(lin(g, GB, b), 1)
                dve.wait_ge(wo_ready, lin(g, GB, b + 1))
                R = Y if latent else X
                dve.tensor_tensor(R[:, n, :], pO[:, :D].rearrange("p (o d) -> p o d", o=1), R[:, n, :],
                                  ALU.add).then_inc(res_done, 1)

            def begin():
                dve.memset(Qd[:, 0].bitcast(F32), 0.0).then_inc(zeroed, 1)
                dve.memset(Qd[:, 1].bitcast(F32), 0.0).then_inc(zeroed, 1)
                dve.memset(Ks[:].bitcast(F32), 0.0).then_inc(zeroed, 1)
                dve.memset(V[:], 1.0).then_inc(zeroed, 1)
                dve.memset(mT[:].bitcast(F32), 0.0).then_inc(zeroed, 1)
                dve.memset(pV[:], 0.0).then_inc(zeroed, 1)
                dve.memset(mx[:], 0.0).then_inc(zeroed, 1)
                dve.memset(var[:], 0.0).then_inc(zeroed, 1)
                dve.wait_ge(zeroed, 8)
                for what, k in start:
                    if what == "x":
                        norm_stats((None, k))
                        norm_rows((None, k))
                        if latent:
                            rms_rows((None, k))
                    part(what, (None, k), k)
                take_max((None, 0), 0, 0)
                take_max((None, 0), 0, 1)
                negate((None, 0), 0)

            def step(g, p, b, nxt, nxt2):
                gn, pn, bn = (g, p, b + 1) if b < GB - 1 else (shift(g, 1), 1 - p, 0)
                gp, pp, bp = (g, p, b - 1) if b else (shift(g, -1), 1 - p, GB - 1)
                more = nxt or b < GB - 1
                before = b > 0 or not is_first(g)
                keep_max(g, b)
                if latent and b == 2 and nxt2:
                    rms_rows(shift(g, 2))
                what, gw, far = slot(b, 0, g, nxt, nxt2)
                if what:
                    part(what, gw, (p + far) % 2)
                if more:
                    take_max(gn, bn, 0)
                if b == 0 and nxt2:
                    norm_stats(shift(g, 2))
                if b == 1 and nxt2:
                    norm_rows(shift(g, 2))
                if before:
                    divide(gp, bp)
                if more:
                    take_max(gn, bn, 1)
                    negate(gn, bn)
                what, gw, far = slot(b, 1, g, nxt, nxt2)
                if what:
                    part(what, gw, (p + far) % 2)
                if before:
                    output_lo(gp, bp)
                    residual(gp, bp)

            def finish():
                g = (None, NG - 1)
                divide(g, GB - 1)
                output_lo(g, GB - 1)
                residual(g, GB - 1)

            walk(dve, begin, step, finish)

        @block.gpsimd
        def _(pool):

            def root(g, src_ready, value, src, out, mult, eps, tmp, done):
                src_ready()
                settle(pool, c)
                pool.tensor_scalar(tmp, src, mult, eps, ALU.mult, ALU.add).then_inc(own, 1)
                pool.wait_ge(own, value)
                pool.tensor_tensor(out, tmp, c["mhalf"][:, 0:GB], ALU.pow).then_inc(done, 1)

            per = 3 if latent else 1

            def rows(g):
                wait(pool, x_norm, lin(g, GB, 0))
                root(g, lambda: pool.wait_ge(ln_agg, lin(g, GB, GB)), row_root(g), aggr[:, :, 1], rstd[:],
                     1.0, LN_EPS, var[:], ln_rstd)

            def row_root(g):
                return lin(g, per, 1) if not latent else own_count(g, "rows")

            def own_count(g, what):
                return lin(g, 3, {"rows": 1, "squares": 2, "lat": 3}[what])

            def squares(g):
                root(g, lambda: pool.wait_ge(sq_done, lin(g, GB, GB)), own_count(g, "squares"), ms[:], rr[:],
                     1.0 / D, RMS_EPS, rv[:], ms_done)

            def latents(g):
                root(g, lambda: pool.wait_ge(lat_agg, lin(g, GB, GB)), own_count(g, "lat"), laggr[:, :, 1], lrstd[:],
                     1.0, LN_EPS, lvar[:], lat_rstd)

            def rope(what, g):
                if what in ("qs", "ks"):
                    k = 0 if what == "qs" else 1
                    hi, lo = (qh, ql) if what == "qs" else (kh, kl)
                    pool.wait_ge(evac, use(g, what) + 1)
                    pool.tensor_tensor(t1[:], t1[:], t2[:], ALU.add).then_inc(rope_sum, 1)
                    pool.wait_ge(rope_sum, lin(g, 2, 1 + k))
                    pool.wait_ge(hi_made, hi_count(g, what))
                    wait(pool, q_sent if what == "qs" else k_sent, lin(g, 16 * n_q_dma, 0))
                    pool.tensor_tensor(lo[:], t1[:], hi[:], ALU.subtract).then_inc(rope_lo, 1)
                elif what == "latT":
                    pool.wait_ge(evac, use(g, what) + 1)
                    pool.wait_ge(hi_made, hi_count(g, what))
                    pool.tensor_tensor(ll[:], lt[:], lh[:], ALU.subtract).then_inc(lat_lo, 1)
                elif what == "lat":
                    latents(g)

            def begin():
                if not latent:
                    rows((None, 0))
                    rows((None, 1))
                    return
                for what, k in start:
                    if what == "x":
                        rows((None, k))
                        squares((None, k))
                    rope(what, (None, k))

            def step(g, p, b, nxt, nxt2):
                if b == 0 and nxt2:
                    rows(shift(g, 2))
                if not latent:
                    return
                if b == 1 and nxt2:
                    squares(shift(g, 2))
                for half_ in (0, 1):
                    what, gw, far = slot(b, half_, g, nxt, nxt2)
                    if what:
                        rope(what, gw)

            walk(pool, begin, step, lambda: None)

        @block.sync
        def _(sp):
            sp.wait_ge(zeroed, 8)

            def stack(g, p, what):
                if what == "q":
                    sp.wait_ge(rope_lo, lin(g, 2, 1)) if latent else sp.wait_ge(evac, use(g, "q") + 1)
                else:
                    sp.wait_ge(rope_lo, lin(g, 2, 2)) if latent else sp.wait_ge(evac, use(g, "k") + 1)
                settle(sp, c)
                wait(sp, s_ready, lin(g, 2 * GB, -2 * GB))
                settle(sp, c)
                for j in range(HQ):
                    for r in range(3):
                        if what == "q":
                            src = (qh, qh, ql)[r]
                            dst = Qd[32 * j + HD * r:32 * j + HD * (r + 1), p, :, j, :]
                        else:
                            src = (kh, kl, kh)[r]
                            dst = Ks[32 * j + HD * r:32 * j + HD * (r + 1), p, :, :]
                        sp.dma_start(dst, src[32 * j:32 * j + 32, :]).then_inc(q_sent if what == "q" else k_sent, 16)

            def begin():
                stack((None, 0), 0, "q")
                stack((None, 0), 0, "k")

            def step(g, p, b, nxt, nxt2):
                if b == 0 and nxt:
                    stack(shift(g, 1), 1 - p, "q")
                    stack(shift(g, 1), 1 - p, "k")

            walk(sp, begin, step, lambda: None)

    if latent:
        add_rows(nc, X, Y)


def add_rows(nc, X, Y):
    with nc.semaphore("rows_added") as added, nc.Block() as block:
        @block.vector
        def _(dve):
            for n in range(0, NB, 8):
                last = dve.tensor_tensor(X[:, n:n + 8, :], X[:, n:n + 8, :], Y[:, n:n + 8, :], ALU.add)
            last.then_inc(added, 1)
            dve.wait_ge(added, 1)


def wide_attention(nc, c, X):
    W = c["parts"]
    HB = WH_ // 2
    with ExitStack() as ctx:
        def sb(name, shape, dt):
            return ctx.enter_context(nc.sbuf_tensor(f"w_{name}", shape, dt))

        def pb(name, shape, dt=F32):
            return ctx.enter_context(nc.psum_tensor(f"w_{name}", shape, dt))

        def sem(name):
            return ctx.enter_context(nc.semaphore(f"w_{name}"))


        stats, aggr = sb("stats", [P, GB, 6], F32), sb("aggr", [P, GB, 2], F32)
        var, rstd = sb("var", [P, GB], F32), sb("rstd", [P, GB], F32)
        xn = sb("xn", [P, GB, D], F32)
        xh, xl = sb("xh", [P, TG], F16), sb("xl", [P, TG], F16)
        Qh, Ql = sb("Qh", [P, 2, HB, TG], F16), sb("Ql", [P, 2, HB, TG], F16)
        Kh, Kl = sb("Kh", [P, 2, HB, GB * KC], F16), sb("Kl", [P, 2, HB, GB * KC], F16)
        V = sb("V", [P, 2, WHID], F32)
        ones = sb("ones", [P, WD], F32)
        mx = sb("mx", [P, WH_], F32)
        ng = sb("ng", [P, WH_], F16)
        mT = sb("mT", [P, 2, P], F16)
        PT = sb("PT", [P, 2, WH_, P], F32)
        rec, O = sb("rec", [P, HB * P], F32), sb("O", [P, HB * P], F32)
        oh, ol = sb("oh", [P, HB, P], F16), sb("ol", [P, HB, P], F16)

        pM = pb("pM", [P, 2, HB, P])
        pS = pb("pS", [P, 2, HB, P])
        pV, pD = pb("pV", [P, HB * P]), pb("pD", [P, HB * P])
        pP = pb("pP", [P, 512])
        pT = pb("pT", [P, 512])

        zeroed, x_norm, ln_st, ln_agg, ln_rstd = (sem("zeroed"), sem("x_norm"), sem("ln_st"), sem("ln_agg"),
                                                  sem("ln_rstd"))
        own, used, hi_made, evac = sem("own"), sem("used"), sem("hi_made"), sem("evac")
        v_kept = sem("v_kept")
        m_ready, m_max, neg, mt_ready, mt_kept = (sem("m_ready"), sem("m_max"), sem("neg"), sem("mt_ready"),
                                                  sem("mt_kept"))
        s_ready, exp_done, pv_ready, rec_done, o_done = (sem("s_ready"), sem("exp_done"), sem("pv_ready"),
                                                         sem("rec_done"), sem("o_done"))
        oh_done, ol_done, wo_ready, res_done = sem("oh_done"), sem("ol_done"), sem("wo_ready"), sem("res_done")
        block = ctx.enter_context(nc.Block())

        LEAD, USES = 2 + 2 * HB, 3 * GB + 1

        def use(g, what, b=0):
            if is_start(g, what):
                return {"x": 0 if g[1] == 0 else LEAD - 1, "q": 1 + 2 * b, "k": 2 + 2 * b}[what]
            if what == "x":
                return lin(g, USES, LEAD - 2 * USES + 3 * GB)
            if what == "v":
                if g[0] is None and g[1] == NG - 1:
                    return LEAD + USES * (NG - 1) - 1 + b
                return lin(g, USES, LEAD + 3 * b + 2)
            return lin(g, USES, LEAD - USES + 3 * b + (what == "k"))

        def is_start(g, what):
            return g[0] is None and (what == "x" and g[1] < 2 or what in "qk" and g[1] == 0)

        def values_before(g, what, b):
            if is_start(g, what):
                return 0
            if what == "x":
                return lin(g, GB, -GB)
            return lin(g, GB, b) if what == "v" else lin(g, GB, b - GB)

        def by_vector(g, what, b=0):
            if is_start(g, what):
                return use(g, what, b) + 1
            if what == "x":
                return lin(g, 2 * GB + 1, LEAD - 2 * (2 * GB + 1) + 2 * GB + 1)
            if what == "v":
                if g[0] is None and g[1] == NG - 1:
                    return LEAD + (2 * GB + 1) * (NG - 1) - 1
                return lin(g, 2 * GB + 1, LEAD + 2 * b + 2)
            return lin(g, 2 * GB + 1, LEAD - (2 * GB + 1) + 2 * b + (what == "k") + 1)

        def walk(engine, begin, step, finish):
            begin()
            groups(engine, lambda g, p, nxt, nxt2: [step(g, p, b, nxt, nxt2) for b in range(GB)])
            finish()

        start = [("x", 0, 0)] + [(w, 0, b) for b in range(HB) for w in "qk"] + [("x", 1, 0)]

        @block.tensor
        def _(pe):
            pe.wait_ge(zeroed, 2)

            def project(what, g, b):
                wait(pe, evac, by_vector(g, what, b) - (what != "v"))
                wait(pe, v_kept, values_before(g, what, b))
                if what == "x":
                    pe.wait_ge(x_norm, lin(g, GB, GB))
                    for t in range(GB):
                        mm = pe.transpose(pP[:, t * P:(t + 1) * P], xn[:, t, :], c["ident"][:])
                elif what == "q":
                    wait(pe, evac, by_vector(g, "x"))
                    mm = product(pe, pP[:, :TG], W.of("w_q", b * P, P), (xh[:], xl[:]))
                elif what == "k":
                    mm = product(pe, pP[:, :GB * KC], W.of("w_k", b * P, P), W.of("ctx", lin(g, GB * KC), GB * KC))
                else:
                    mm = product(pe, pP[:KC, :], W.of("ctx", lin(g, GB * KC, b * KC), KC), W.of("w_v", 0, WHID))
                mm.then_inc(used, 1)

            def maxima(g, p, b):
                wait(pe, m_max, lin(g, GB, b))
                if b == 0:
                    pe.wait_ge(evac, by_vector(g, "k", HB - 1))
                for h in range(WH_):
                    r = slice(WD * (h % 2), WD * (h % 2) + WD)
                    mm = pe.matmul(pM[:, h % 2, h // 2, :KC], Qh[r, p, h // 2, b * P:(b + 1) * P],
                                   Kh[r, p, h // 2, b * KC:(b + 1) * KC], start=True, stop=True)
                mm.then_inc(m_ready, 1)

            def max_transpose(g, b):
                pe.wait_ge(neg, lin(g, GB, b + 1))
                wait(pe, res_done, lin(g, GB, b - 1))
                pe.transpose(pT[:, :P // 2].bitcast(F16)[:WH_, :], ng[:], c["ident16"][:]).then_inc(mt_ready, 1)

            def scores(g, p, b):
                wait(pe, exp_done, lin(g, GB, b))
                for h in range(WH_):
                    r = slice(WD * (h % 2), WD * (h % 2) + WD)
                    q, k = slice(b * P, (b + 1) * P), slice(b * KC, (b + 1) * KC)
                    product(pe, pS[:KC, h % 2, h // 2, :], (Kh[r, p, h // 2, k], Kl[r, p, h // 2, k]),
                            (Qh[r, p, h // 2, q], Ql[r, p, h // 2, q]), first=h < 2, last=False, check=False)
                pe.wait_ge(mt_kept, lin(g, GB, b + 1))
                for h in range(WH_):
                    s = HB * (h % 2) + h // 2
                    mm = pe.matmul(pS[:KC, h % 2, h // 2, :], c["sel"][:, s, :KC], mT[:, b % 2, :],
                                   start=False, stop=h >= WH_ - 2, skip_group_check=True)
                mm.then_inc(s_ready, 1)

            def values(g, p, b):
                wait(pe, exp_done, lin(g, GB, b + 1))
                wait(pe, o_done, lin(g, GB, b))
                pe.wait_ge(v_kept, lin(g, GB, b + 1))
                for h in range(WH_):
                    o = slice(WD * (h % 2), WD * (h % 2) + WD)
                    cols = slice(P * (h // 2), P * (h // 2) + P)
                    pe.matmul(pV[o, cols], V[:KC, b % 2, WD * h:WD * h + WD], PT[:KC, b % 2, HB * (h % 2) + h // 2, :],
                              start=True, stop=True)
                    mm = pe.matmul(pD[o, cols], ones[:KC, :], PT[:KC, b % 2, HB * (h % 2) + h // 2, :],
                                   start=True, stop=True)
                mm.then_inc(pv_ready, 1)

            def project_output(g, b):
                pe.wait_ge(oh_done, lin(g, GB, b + 1))
                pe.wait_ge(ol_done, lin(g, GB, b + 1))
                pe.wait_ge(mt_kept, mt_count(g, b))
                for k in range(HB):
                    product(pe, pT[:, :D], (oh[:, k, :], ol[:, k, :]), W.of("w_o", k * D, D), first=k == 0, last=False)
                bh, bl = W.of("w_bo", 0, D)
                pe.matmul(pT[:, :D], c["row0"][:], bh, start=False, stop=False)
                pe.matmul(pT[:, :D], c["row0"][:], bl, start=False, stop=True).then_inc(wo_ready, 1)

            def mt_count(g, b):
                if g[0] is None and g[1] == NG - 1 and b == GB - 1:
                    return NB
                return lin(g, GB, b + 2)

            def begin():
                for what, k, b in start:
                    project(what, (None, k), b)
                maxima((None, 0), 0, 0)

            def step(g, p, b, nxt, nxt2):
                gn, pn, bn = (g, p, b + 1) if b < GB - 1 else (shift(g, 1), 1 - p, 0)
                gp, pp, bp = (g, p, b - 1) if b else (shift(g, -1), 1 - p, GB - 1)
                before = b > 0 or not is_first(g)
                max_transpose(g, b)
                if nxt:
                    project("q", shift(g, 1), b)
                if before:
                    values(gp, pp, bp)
                scores(g, p, b)
                if nxt:
                    project("k", shift(g, 1), b)
                if nxt or b < GB - 1:
                    maxima(gn, pn, bn)
                project("v", g, b)
                if before:
                    project_output(gp, bp)
                if b == GB - 1 and nxt2:
                    project("x", shift(g, 2), 0)

            def finish():
                g = (None, NG - 1)
                values(g, 1, GB - 1)
                project_output(g, GB - 1)

            walk(pe, begin, step, finish)

        @block.scalar
        def _(act):
            def part(what, g, p, b):
                act.wait_ge(used, use(g, what, b) + 1)
                if what == "x":
                    act.activation(xh[:], pP[:, :TG], ACT.Copy).then_inc(hi_made, 1)
                elif what == "q":
                    act.activation(Qh[:, p, b, :], pP[:, :TG], ACT.Copy).then_inc(hi_made, 1)
                elif what == "k":
                    act.activation(Kh[:, p, b, :], pP[:, :GB * KC], ACT.Copy).then_inc(hi_made, 1)
                else:
                    wait(act, pv_ready, lin(g, GB, b - 1))
                    act.activation(V[:KC, b % 2, :], pP[:KC, :], ACT.Copy).then_inc(v_kept, 1)

            def exps(g, b):
                act.wait_ge(s_ready, lin(g, GB, b + 1))
                wait(act, pv_ready, lin(g, GB, b - 1))
                act.activation(PT[:KC, b % 2, :, :], pS[:KC].rearrange("k o h q -> k (o h) q"), ACT.Exp,
                               scale=float(WD) ** -0.5).then_inc(exp_done, 1)

            def output_hi(g, b):
                act.wait_ge(o_done, lin(g, GB, b + 1))
                wait(act, wo_ready, lin(g, GB, b))
                act.activation(oh[:].rearrange("p k t -> p (k t)"), O[:], ACT.Copy).then_inc(oh_done, 1)

            def begin():
                for what, k, b in start:
                    part(what, (None, k), k, b)

            def step(g, p, b, nxt, nxt2):
                gp, pp, bp = (g, p, b - 1) if b else (shift(g, -1), 1 - p, GB - 1)
                before = b > 0 or not is_first(g)
                if nxt:
                    part("q", shift(g, 1), 1 - p, b)
                exps(g, b)
                if nxt:
                    part("k", shift(g, 1), 1 - p, b)
                if before:
                    output_hi(gp, bp)
                part("v", g, p, b)
                if b == GB - 1 and nxt2:
                    part("x", shift(g, 2), p, 0)

            walk(act, begin, step, lambda: output_hi((None, NG - 1), GB - 1))

        @block.vector
        def _(dve):
            def norm_stats(g):
                for b in range(GB):
                    dve.bn_stats(stats[:, b, :], X[:, bass.ds(lin(g, GB, b), 1), :]).then_inc(ln_st, 1)
                for b in range(GB):
                    dve.wait_ge(ln_st, lin(g, GB, b + 1))
                    settle(dve, c)
                    dve.bn_aggr(aggr[:, b, :], stats[:, b, :]).then_inc(ln_agg, 1)

            def norm_rows(g):
                dve.wait_ge(ln_rstd, lin(g, 1, 1))
                if not is_first(g):
                    dve.wait_ge(used, use(shift(g, -1), "x") + 1)
                for b in range(GB):
                    dve.tensor_scalar(xn[:, b:b + 1, :], X[:, bass.ds(lin(g, GB, b), 1), :], aggr[:, b, 0:1],
                                      rstd[:, b:b + 1], ALU.subtract, ALU.mult).then_inc(x_norm, 1)

            def part(what, g, p, b):
                dve.wait_ge(hi_made, by_vector(g, what, b))
                if what == "x":
                    dve.tensor_tensor(xl[:], pP[:, :TG], xh[:], ALU.subtract).then_inc(evac, 1)
                elif what == "q":
                    dve.tensor_tensor(Ql[:, p, b, :], pP[:, :TG], Qh[:, p, b, :], ALU.subtract).then_inc(evac, 1)
                else:
                    dve.tensor_tensor(Kl[:, p, b, :], pP[:, :GB * KC], Kh[:, p, b, :], ALU.subtract).then_inc(evac, 1)

            def take_max(g, b):
                dve.wait_ge(m_ready, lin(g, GB, b + 1))
                wait(dve, neg, lin(g, GB, b))
                dve.tensor_reduce(out=mx[:], in_=pM[:].rearrange("p o h k -> p (o h) k")[:, :, :KC], op=ALU.max,
                                  axis=AX.X).then_inc(m_max, 1)
                dve.wait_ge(m_max, lin(g, GB, b + 1))
                wait(dve, mt_ready, lin(g, GB, b))
                dve.tensor_scalar(ng[:], mx[:], -1.0 / SHIFT, None, ALU.mult).then_inc(neg, 1)

            def keep_max(g, b):
                dve.wait_ge(mt_ready, lin(g, GB, b + 1))
                wait(dve, s_ready, lin(g, GB, b - 1))
                dve.tensor_copy(mT[:WH_, b % 2, :], pT[:, :P // 2].bitcast(F16)[:WH_, :]).then_inc(mt_kept, 1)

            def divide(g, b):
                dve.wait_ge(pv_ready, lin(g, GB, b + 1))
                dve.reciprocal(rec[:], pD[:]).then_inc(rec_done, 1)
                dve.wait_ge(rec_done, lin(g, GB, b + 1))
                wait(dve, oh_done, lin(g, GB, b))
                dve.tensor_tensor(O[:], pV[:], rec[:], ALU.mult).then_inc(o_done, 1)

            def output_lo(g, b):
                dve.wait_ge(oh_done, lin(g, GB, b + 1))
                dve.tensor_tensor(ol[:].rearrange("p k t -> p (k t)"), O[:], oh[:].rearrange("p k t -> p (k t)"),
                                  ALU.subtract).then_inc(ol_done, 1)

            def residual(g, b):
                n = bass.ds(lin(g, GB, b), 1)
                dve.wait_ge(wo_ready, lin(g, GB, b + 1))
                dve.tensor_tensor(X[:, n, :], pT[:, :D].rearrange("p (o d) -> p o d", o=1), X[:, n, :],
                                  ALU.add).then_inc(res_done, 1)

            def begin():
                dve.memset(mT[:].bitcast(F32), 0.0).then_inc(zeroed, 1)
                dve.memset(ones[:], 1.0).then_inc(zeroed, 1)
                for what, k, b in start:
                    if what == "x":
                        norm_stats((None, k))
                        norm_rows((None, k))
                    part(what, (None, k), k, b)
                take_max((None, 0), 0)

            def step(g, p, b, nxt, nxt2):
                gn, pn, bn = (g, p, b + 1) if b < GB - 1 else (shift(g, 1), 1 - p, 0)
                gp, pp, bp = (g, p, b - 1) if b else (shift(g, -1), 1 - p, GB - 1)
                before = b > 0 or not is_first(g)
                keep_max(g, b)
                if nxt:
                    part("q", shift(g, 1), 1 - p, b)
                if before:
                    divide(gp, bp)
                if nxt:
                    part("k", shift(g, 1), 1 - p, b)
                if before:
                    output_lo(gp, bp)
                if nxt or b < GB - 1:
                    take_max(gn, bn)
                if b == 1 and nxt2:
                    norm_stats(shift(g, 2))
                if b == 2 and nxt2:
                    norm_rows(shift(g, 2))
                if before:
                    residual(gp, bp)
                if b == GB - 1 and nxt2:
                    part("x", shift(g, 2), p, 0)

            def finish():
                g = (None, NG - 1)
                divide(g, GB - 1)
                output_lo(g, GB - 1)
                residual(g, GB - 1)

            walk(dve, begin, step, finish)

        @block.gpsimd
        def _(pool):
            def rows(g):
                pool.wait_ge(ln_agg, lin(g, GB, GB))
                wait(pool, x_norm, lin(g, GB, 0))
                settle(pool, c)
                pool.tensor_scalar(var[:], aggr[:, :, 1], 1.0, LN_EPS, ALU.mult, ALU.add).then_inc(own, 1)
                pool.wait_ge(own, lin(g, 1, 1))
                pool.tensor_tensor(rstd[:], var[:], c["mhalf"][:, 0:GB], ALU.pow).then_inc(ln_rstd, 1)

            rows((None, 0))
            rows((None, 1))
            groups(pool, lambda g, p, nxt, nxt2: rows(shift(g, 2)) if nxt2 else None)


def route(nc, c, S, XH, XL, WR, second):
    W, SM = c["parts"], c["small"]
    E = E1 if second else E0
    tag = "e1" if second else "e0"
    gate = "router" if second else "gate"
    with ExitStack() as ctx:
        def sb(name, shape, dt):
            return ctx.enter_context(nc.sbuf_tensor(f"{tag}r_{name}", shape, dt))

        def sem(name):
            return ctx.enter_context(nc.semaphore(f"{tag}r_{name}"))


        stats, aggr = sb("stats", [P, 2, GB, 6], F32), sb("aggr", [P, 2, GB, 2], F32)
        ms, var, rstd = sb("ms", [P, 2, GB], F32), sb("var", [P, 2, GB], F32), sb("rstd", [P, 2, GB], F32)
        sq = sb("sq", [P, D], F32)
        xn = sb("xn", [P, 2, GB, D], F32)
        LG = sb("LG", [P, NB, E], F32)
        a_, b_, c_ = (sb(k, [P, NB, E], F32) for k in "abc")
        v1, v2, d1, d2 = (sb(k, [P, NB], F32) for k in ("v1", "v2", "d1", "d2"))
        pX = ctx.enter_context(nc.psum_tensor(f"{tag}r_pX", [P, 2, TG], F32))
        pL = ctx.enter_context(nc.psum_tensor(f"{tag}r_pL", [P, 2, 512], F32))
        st, agg, root, rstd_done, rows = sem("st"), sem("agg"), sem("root"), sem("rstd_done"), sem("rows")
        turned, hi_made, lo_made, scored, kept = sem("turned"), sem("hi_made"), sem("lo_made"), sem("scored"), sem("kept")
        picked, asked, exp_done = sem("picked"), sem("asked"), sem("exp_done")
        block = ctx.enter_context(nc.Block())

        def every(engine, step):
            groups(engine, lambda g, p, nxt, nxt2: step(g, p))

        def ahead(engine, early, late):
            early((None, 0), 0)
            groups(engine, lambda g, p, nxt, nxt2: (early(shift(g, 1), 1 - p) if nxt else None, late(g, p)))

        @block.tensor
        def _(pe):
            def turn(g, p):
                pe.wait_ge(rows, lin(g, 1, 1))
                wait(pe, lo_made, lin(g, 1, -1))
                for t in range(GB):
                    mm = pe.transpose(pX[:, p, t * P:(t + 1) * P], xn[:, p, t, :], c["ident"][:])
                mm.then_inc(turned, 1)

            def score(g, p):
                pe.wait_ge(lo_made, lin(g, 1, 1))
                wait(pe, kept, lin(g, 1, -1))
                for t in range(GB):
                    rows_ = bass.ds(lin(g, TG, t * P), P)
                    out = pL[:, p, t * E:(t + 1) * E]
                    mm = product(pe, out, (XH[:, rows_], XL[:, rows_]), W.of(gate, 0, E), last=second)
                    if not second:
                        gh, gl = W.of("gate_b", 0, E)
                        pe.matmul(out, c["row0"][:], gh, start=False, stop=False)
                        mm = pe.matmul(out, c["row0"][:], gl, start=False, stop=True)
                mm.then_inc(scored, 1)

            ahead(pe, turn, score)

        @block.scalar
        def _(act):
            def squares(g, p):
                wait(act, rstd_done, lin(g, 1, -1))
                for t in range(GB):
                    wait(act, agg, lin(g, GB, t))
                    act.activation(sq[:], S[:, bass.ds(lin(g, GB, t), 1), :], ACT.Square,
                                   accum_out=ms[:, p, t:t + 1]).then_inc(agg, 1)

            def hi(g, p):
                act.wait_ge(turned, lin(g, 1, 1))
                out = XH[:, bass.ds(lin(g, TG), TG)]
                if second:
                    act.activation(out, pX[:, p, :], ACT.Copy).then_inc(hi_made, 1)
                else:
                    act.activation(out, pX[:, p, :], ACT.Copy, scale=SM("n2")).then_inc(hi_made, 1)

            if second:
                every(act, hi)
                act.wait_ge(asked, 1)
                act.activation(d2[:], d1[:], ACT.Exp).then_inc(exp_done, 1)
            else:
                ahead(act, squares, hi)

        @block.gpsimd
        def _(pool):
            def roots(g, p):
                pool.wait_ge(agg, lin(g, GB, GB))
                wait(pool, rows, lin(g, 1, -1))
                settle(pool, c)
                src = aggr[:, p, :, 1] if second else ms[:, p, :]
                pool.tensor_scalar(var[:, p, :], src, 1.0 if second else 1.0 / D, LN_EPS if second else RMS_EPS,
                                   ALU.mult, ALU.add).then_inc(root, 1)
                pool.wait_ge(root, lin(g, 1, 1))
                pool.tensor_tensor(rstd[:, p, :], var[:, p, :], c["mhalf"][:, 0:GB], ALU.pow).then_inc(rstd_done, 1)

            every(pool, roots)

        @block.vector
        def _(dve):
            def statistics(g, p):
                for t in range(GB):
                    dve.bn_stats(stats[:, p, t, :], S[:, bass.ds(lin(g, GB, t), 1), :]).then_inc(st, 1)
                for t in range(GB):
                    dve.wait_ge(st, lin(g, GB, t + 1))
                    settle(dve, c)
                    dve.bn_aggr(aggr[:, p, t, :], stats[:, p, t, :]).then_inc(agg, 1)

            def norm(g, p):
                dve.wait_ge(rstd_done, lin(g, 1, 1))
                wait(dve, turned, lin(g, 1, -1))
                for t in range(GB):
                    src, dst = S[:, bass.ds(lin(g, GB, t), 1), :], xn[:, p, t:t + 1, :]
                    if second:
                        ts = dve.tensor_scalar(dst, src, aggr[:, p, t, 0:1], rstd[:, p, t:t + 1], ALU.subtract, ALU.mult)
                    else:
                        ts = dve.tensor_scalar(dst, src, rstd[:, p, t:t + 1], None, ALU.mult)
                ts.then_inc(rows, 1)

            def lo(g, p):
                dve.wait_ge(hi_made, lin(g, 1, 1))
                at = bass.ds(lin(g, TG), TG)
                if second:
                    dve.tensor_tensor(XL[:, at], pX[:, p, :], XH[:, at], ALU.subtract).then_inc(lo_made, 1)
                else:
                    dve.scalar_tensor_tensor(XL[:, at], pX[:, p, :], SM("n2"), XH[:, at], ALU.mult,
                                             ALU.subtract).then_inc(lo_made, 1)

            def keep(g, p):
                dve.wait_ge(scored, lin(g, 1, 1))
                dve.tensor_copy(LG[:, bass.ds(lin(g, GB), GB), :],
                                pL[:, p, :GB * E].rearrange("p (t e) -> p t e", e=E)).then_inc(kept, 1)

            if second:
                statistics((None, 0), 0)
                statistics((None, 1), 1)
            norm((None, 0), 0)

            def step(g, p, nxt, nxt2):
                if second and nxt2:
                    statistics(shift(g, 2), p)
                if nxt:
                    norm(shift(g, 1), 1 - p)
                lo(g, p)
                keep(g, p)

            groups(dve, step)

            chain = [0]

            def then(instruction, upto=picked):
                chain[0] += 1
                instruction.then_inc(picked, 1)
                dve.wait_ge(picked, chain[0])

            def over(v):
                return v[:].rearrange("p (n o) -> p n o", o=1).to_broadcast([P, NB, E])

            def first_max(values, value, onehot, work):
                then(dve.tensor_reduce(out=value[:], in_=values[:], op=ALU.max, axis=AX.X))
                then(dve.tensor_tensor(work[:], values[:], over(value), ALU.is_equal))
                then(dve.tensor_tensor(work[:], work[:], c["first"][:, :, :E].to_broadcast([P, NB, E]), ALU.mult))
                then(dve.tensor_reduce(out=d1[:], in_=work[:], op=ALU.max, axis=AX.X))
                then(dve.tensor_tensor(onehot[:], work[:], over(d1), ALU.is_equal))

            dve.wait_ge(kept, NG)
            if not second:
                first_max(LG, v1, WR, a_)
            else:
                first_max(LG, v1, b_, a_)
                then(dve.scalar_tensor_tensor(LG[:], b_[:], -3.0e38, LG[:], ALU.mult, ALU.add))
                first_max(LG, v2, c_, a_)
                then(dve.tensor_tensor(d1[:], v2[:], v1[:], ALU.subtract))
                dve.sem_inc(asked, 1)
                dve.wait_ge(exp_done, 1)
                then(dve.tensor_scalar(v1[:], d2[:], 1.0, None, ALU.add))
                then(dve.reciprocal(v1[:], v1[:]))
                then(dve.tensor_tensor(v2[:], v1[:], d2[:], ALU.mult))
                then(dve.tensor_tensor(b_[:], b_[:], over(v1), ALU.mult))
                then(dve.tensor_tensor(c_[:], c_[:], over(v2), ALU.mult))
                then(dve.tensor_tensor(WR[:], b_[:], c_[:], ALU.add))


def experts(nc, c, X, XH, XL, WR, second, parts):
    W, SM = c["parts"], c["small"]
    E = E1 if second else E0
    tag = "e1" if second else "e0"
    U, LAG, NU, NA = E * FC, 2, 4, 2
    with ExitStack() as ctx:
        def sem(name):
            return ctx.enter_context(nc.semaphore(f"{tag}x_{name}"))

        gh = ctx.enter_context(nc.sbuf_tensor(f"{tag}_gh", [P, NU, TG], F16))
        gl = ctx.enter_context(nc.sbuf_tensor(f"{tag}_gl", [P, NU, TG], F16))
        g32 = ctx.enter_context(nc.sbuf_tensor(f"{tag}_g32", [P, NA, TG], F32))
        pU = ctx.enter_context(nc.psum_tensor(f"{tag}_pU", [P, NU, TG], F32))
        pY = ctx.enter_context(nc.psum_tensor(f"{tag}_pY", [P, 2, GB, D], F32))
        up, hi, full, lo, down, summed = (sem(k) for k in ("up", "hi", "full", "lo", "down", "summed"))
        block = ctx.enter_context(nc.Block())

        @block.tensor
        def _(pe):
            with pe.Fori(0, NG, 1) as g:
                def raise_(u):
                    e, f = divmod(u, FC)
                    wait(pe, full, g * U + (u - NU + 1) if u >= NU else g * U)
                    toks = bass.ds(g * TG, TG)
                    product(pe, pU[:, u % NU, :], parts(0, e * FF + f * P, P), (XH[:, toks], XL[:, toks])).then_inc(up, 1)

                def lower(u):
                    e, f = divmod(u, FC)
                    pe.wait_ge(lo, g * U + (u + 1))
                    if f == 0:
                        wait(pe, summed, g * E + max(e - 1, 0))
                    for t in range(GB):
                        out = pY[:, e % 2, t, :]
                        ts = slice(t * P, (t + 1) * P)
                        mm = product(pe, out, (gh[:, u % NU, ts], gl[:, u % NU, ts]), parts(1, e * FF + f * D, D),
                                     first=f == 0 and t == 0, last=f == FC - 1 and (second or False), check=False)
                        if f == FC - 1 and not second:
                            bh, bl = W.of("b2", e * D, D)
                            pe.matmul(out, c["row0"][:], bh, start=False, stop=False, skip_group_check=True)
                            mm = pe.matmul(out, c["row0"][:], bl, start=False, stop=True, skip_group_check=True)
                    mm.then_inc(down, 1)

                for u in range(U + LAG):
                    if u < U:
                        raise_(u)
                    if u >= LAG:
                        lower(u - LAG)

        @block.scalar
        def _(act):
            with act.Fori(0, NG, 1) as g:
                for u in range(U):
                    act.wait_ge(up, g * U + (u + 1))
                    if u >= NU:
                        act.wait_ge(down, g * U + (u - NU + 1))
                    else:
                        act.wait_ge(down, g * U) if u == 0 else None
                    f = ACT.Gelu if second else ACT.Relu
                    bias = 0.0 if second else SM("b1", P, u)
                    act.activation(gh[:, u % NU, :], pU[:, u % NU, :], f, bias=bias).then_inc(hi, 1)
                    if u >= NA:
                        act.wait_ge(lo, g * U + (u - NA + 1))
                    act.activation(g32[:, u % NA, :], pU[:, u % NU, :], f, bias=bias).then_inc(full, 1)

        @block.vector
        def _(dve):
            with dve.Fori(0, NG, 1) as g:
                def add(e):
                    dve.wait_ge(down, g * U + (e + 1) * FC)
                    for t in range(GB):
                        n = bass.ds(g * GB + t, 1)
                        last = dve.scalar_tensor_tensor(X[:, n, :], pY[:, e % 2, t:t + 1, :], WR[:, n, e], X[:, n, :],
                                                        ALU.mult, ALU.add)
                    last.then_inc(summed, 1)

                for u in range(U):
                    dve.wait_ge(full, g * U + (u + 1))
                    dve.tensor_tensor(gl[:, u % NU, :], g32[:, u % NA, :], gh[:, u % NU, :], ALU.subtract).then_inc(lo, 1)
                    if u % FC == 1 and u > FC:
                        add(u // FC - 1)
                add(E - 1)


def build(nc, ins, out, stop=99):
    ctx = ExitStack()
    with ctx:
        def sb(name, shape, dt):
            return ctx.enter_context(nc.sbuf_tensor(name, shape, dt))

        X = sb("X", [P, NB, D], F32)
        YW = sb("YW", [P, NB * D], F32)
        Y = YW[:].rearrange("p (n d) -> p n d", n=NB)
        SH, SL = sb("SH", [P, NSPLIT], F16), sb("SL", [P, NSPLIT], F16)
        small = sb("small", [P, NSMALL], F32)
        c = {
            "passed": ctx.enter_context(nc.semaphore("passed")),
            "parts": Parts(SH, SL),
            "small": lambda name, rows=P, k=0: small[:rows, SM_OFF[name] + k:SM_OFF[name] + k + 1],
            "ident": sb("ident", [P, P], F32), "ident16": sb("ident16", [P, P], F16), "id16": sb("identb", [P, P], U16),
            "maskM": sb("maskM", [P, HQ, P], U16), "maskS": sb("maskS", [P, HQ, P], U16),
            "sel": sb("sel", [P, H, P], F16), "row0": sb("row0", [P, P], F16),
            "cos": sb("cos", [P, P], F32), "sin": sb("sin", [P, P], F32), "mhalf": sb("mhalf", [P, 8], F32), "first": sb("first", [P, 1, E1], F32),
        }
        load_all(nc, [(X[:], ins["x"].rearrange("n t d -> t n d")), (small[:], ins["small"])]
                 + [(c[k][:], ins[k]) for k in ("ident", "ident16", "id16", "maskM", "maskS", "sel", "row0", "cos",
                                               "sin", "mhalf", "first")], "first")
        split_columns(nc, ins["split"], NSPLIT, SH, SL)
        narrow_attention(nc, c, X, Y, False)
        if stop > 1:
            narrow_attention(nc, c, X, Y, True)
        def moe(second, S, parts):
            with (nc.sbuf_tensor(f"XH{second}", [P, NB * P], F16) as XH, nc.sbuf_tensor(f"XL{second}", [P, NB * P], F16) as XL,
                  nc.sbuf_tensor(f"WR{second}", [P, NB, E1 if second else E0], F32) as WR):
                route(nc, c, S, XH, XL, WR, second)
                experts(nc, c, X, XH, XL, WR, second, parts)
        if stop > 2:
            moe(False, Y, lambda k, a, n: c["parts"].of(("w1a", "w2a")[k], a, n))
        if stop > 3:
            wide_attention(nc, c, X)
        if stop > 4:
            late = YW[:].bitcast(F16)
            split_columns(nc, ins["late"], NLATE, late[:, :NLATE], late[:, NLATE:])
            moe(True, X, lambda k, a, n: (late[:, k * E1 * FF + a:k * E1 * FF + a + n],
                                          late[:, NLATE + k * E1 * FF + a:NLATE + k * E1 * FF + a + n]))
        with nc.semaphore("stored") as stored, nc.Block() as block:
            @block.sync
            def _(sp):
                sp.dma_start(out.rearrange("n t d -> t n d"), X[:]).then_inc(stored, 16)
                sp.wait_ge(stored, 16)


def shape_constants():
    f = np.float32
    b16 = lambda m: (np.ascontiguousarray(m, f).view(np.uint32) >> 16).astype(np.uint16)
    i = np.arange(P)
    sel = np.zeros((P, H, P), np.float16)
    sel[np.arange(H), np.arange(H), :] = SHIFT
    row0 = np.zeros((P, P), np.float16)
    row0[0] = 1
    maskM = np.where(i[None, :] > i[:, None], f(-1e30), f(0))
    half = HD // 2
    freq = f(1.0) / f(10000.0) ** (np.arange(half, dtype=f) / f(half))
    ang = i.astype(f)[None, :] * freq[:, None]
    d = (i % 32) // 4
    cos, sin = np.cos(ang).astype(f)[d % half], np.sin(ang).astype(f)[d % half]
    sin = np.where((d < half)[:, None], -sin, sin)
    tile4 = lambda m: b16(np.broadcast_to(m[:, None, :], (P, HQ, P)))
    return {"ident": np.eye(P, dtype=f), "ident16": np.eye(P, dtype=np.float16), "id16": b16(np.eye(P)),
            "maskM": tile4(maskM), "maskS": tile4(maskM.T), "sel": sel, "row0": row0,
            "cos": cos.astype(f), "sin": sin.astype(f), "mhalf": np.full((P, 8), -0.5, f),
            "first": np.ascontiguousarray(np.broadcast_to(f(E1) - np.arange(E1, dtype=f), (P, 1, E1)))}


def lay_out(a):
    f = np.float32
    r = np.arange(D)
    row_head, row_dim = HQ * (r % 4) + r // 32, (r % 32) // 4
    perm = row_head * HD + row_dim
    swap = row_head * HD + (row_dim + HD // 2) % HD
    full = lambda m: np.pad(m, ((0, P - m.shape[0]), (0, 0)))
    row = lambda v: full(v.reshape(1, -1))
    up = lambda w: w.transpose(2, 0, 1).reshape(D, -1)
    down = lambda w: w.reshape(w.shape[0], D, FC, P).transpose(3, 0, 2, 1).reshape(P, -1)
    cols = {
        "ctx": a["ctx_1024"].transpose(2, 0, 1).reshape(D, -1),
        "a_q": a["L0_xattn_Wq"][:, perm], "a_k": a["L0_xattn_Wk"][:, perm], "a_v": a["L0_xattn_Wv"],
        "a_o": a["L0_xattn_Wo"], "a_bo": row(a["L0_xattn_bo"]),
        "m_q": a["L0_ffn_Wq"].T[:, perm], "m_qs": a["L0_ffn_Wq"].T[:, swap], "m_kv": a["L0_ffn_Wdkv"].T,
        "m_k": full(a["L0_ffn_Wuk"].T[:, perm]), "m_ks": full(a["L0_ffn_Wuk"].T[:, swap]),
        "m_v": full(a["L0_ffn_Wuv"].T), "m_o": a["L0_ffn_Wo"].T,
        "w_q": a["L1_xattn_Wq"], "w_k": a["L1_xattn_Wk"], "w_v": a["L1_xattn_Wv"],
        "w_o": a["L1_xattn_Wo"].reshape(FC, P, D).transpose(1, 0, 2).reshape(P, -1), "w_bo": row(a["L1_xattn_bo"]),
        "gate": a["L0_ffn_gate_w"].T, "gate_b": row(a["L0_ffn_gate_b"]), "router": a["L1_ffn_router_w"].T,
        "b2": row(a["L0_ffn_b2"]), "w1a": up(a["L0_ffn_W1"]), "w2a": down(a["L0_ffn_W2"]),
    }
    split = np.zeros((P, NSPLIT), f)
    for name, width in SPLIT_COLS:
        split[:, OFF[name]:OFF[name] + width] = cols[name]
    late = np.concatenate([up(a["L1_ffn_expert_w1"]), down(a["L1_ffn_expert_w2"])], axis=1)
    small = np.zeros((P, NSMALL), f)
    for name, v in (("bq", a["L0_xattn_bq"][perm]), ("bk", a["L0_xattn_bk"][perm]), ("bv", a["L0_xattn_bv"]),
                    ("n1", a["L0_ffn_norm1_w"]), ("n2", a["L0_ffn_norm2_w"]), ("lg", a["L0_ffn_ln_g"]),
                    ("lb", a["L0_ffn_ln_b"])):
        small[:len(v), SM_OFF[name]] = v
    small[:, SM_OFF["b1"]:] = a["L0_ffn_b1"].reshape(E0 * FC, P).T
    return {"x": a["x"], "split": split, "late": np.ascontiguousarray(late), "small": small}


def kernel(**inputs):
    import concourse.bacc as bacc
    from concourse.bass_utils import run_bass_kernel_spmd

    a = {k: np.asarray(v) for k, v in inputs.items()}
    arrays = {f"in_{k}": np.ascontiguousarray(v) for k, v in (lay_out(a) | shape_constants()).items()}
    nc = bacc.Bacc("TRN2", target_bir_lowering=False, num_devices=1)
    ins = {k[3:]: nc.dram_tensor(k, v.shape, mybir.dt.from_np(v.dtype), kind="ExternalInput").ap()
           for k, v in arrays.items()}
    out = nc.dram_tensor("out", a["x"].shape, F32, kind="ExternalOutput").ap()
    build(nc, ins, out)
    return run_bass_kernel_spmd(nc, [arrays], core_ids=[0]).results[0]["out"]
```

```python
import numpy as np
from contextlib import ExitStack

import concourse.bass as bass
from concourse import mybir

F32 = mybir.dt.float32
F16 = mybir.dt.float16
BF16 = mybir.dt.bfloat16
U16 = mybir.dt.uint16
ALU = mybir.AluOpType
ACT = mybir.ActivationFunctionType
AX = mybir.AxisListType

P = 128
D = 128
NB = 64
KC = 77
GB = 4
NG = NB // GB
TG = GB * P
H = 16
HD = D // H
HQ = 4
WH_ = 8
WD = 64
WHID = WH_ * WD
LAT = 64
FF = 512
FC = FF // P
E0, E1 = 4, 8
SHIFT = 64.0
LN_EPS, RMS_EPS = 1e-5, 1e-6

SPLIT_COLS = [
    ("ctx", NB * KC),
    ("a_q", D), ("a_k", D), ("a_v", D), ("a_o", D), ("a_bo", D),
    ("m_q", D), ("m_qs", D), ("m_kv", LAT), ("m_k", D), ("m_ks", D), ("m_v", D), ("m_o", D),
    ("w_q", WHID), ("w_k", WHID), ("w_v", WHID), ("w_o", WHID), ("w_bo", D),
    ("gate", E0), ("gate_b", E0), ("router", E1), ("b2", E0 * D),
    ("w1a", E0 * FF), ("w2a", E0 * FF),
]
OFF, _n = {}, 0
for _name, _w in SPLIT_COLS:
    OFF[_name] = _n
    _n += _w
CH = 1024
NSPLIT = -(-_n // CH) * CH
NLATE = 2 * E1 * FF
SMALL = ["bq", "bk", "bv", "n1", "n2", "lg", "lb", "b1"]
SM_OFF = {name: k for k, name in enumerate(SMALL)}
NSMALL = len(SMALL) - 1 + E0 * FC


def lin(g, mult, add=0):
    i, c = g
    return mult * c + add if i is None else i * (2 * mult) + (mult * c + add)


def shift(g, by):
    return g[0], g[1] + by


def is_first(g):
    return g[0] is None and g[1] == 0


def wait(engine, semaphore, value):
    if isinstance(value, int) and value <= 0:
        return
    engine.wait_ge(semaphore, value)


def settle(engine, c):
    engine.sem_inc(c["passed"], 1)


def groups(engine, body):
    for c in (0, 1):
        body((None, c), c, True, True)
    with engine.Fori(1, NG // 2 - 1, 1) as i:
        for c in (0, 1):
            body((i, c), c, True, True)
    body((None, NG - 2), 0, True, False)
    body((None, NG - 1), 1, False, False)


class Parts:

    def __init__(self, hi, lo):
        self.hi, self.lo = hi, lo

    def of(self, name, start, width, rows=P):
        a = OFF[name] + start
        return self.hi[:rows, bass.ds(a, width)], self.lo[:rows, bass.ds(a, width)]


def product(pe, out, left, right, first=True, last=True, check=True):
    (lh, ll), (rh, rl) = left, right
    kw = {} if check else {"skip_group_check": True}
    pe.matmul(out, lh, rh, start=first, stop=False, **kw)
    pe.matmul(out, lh, rl, start=False, stop=False, **kw)
    return pe.matmul(out, ll, rh, start=False, stop=last, **kw)


def split_columns(nc, src, n_cols, hi, lo):
    n = n_cols // CH
    with ExitStack() as ctx:
        stage = ctx.enter_context(nc.sbuf_tensor(f"stage{n_cols}", [P, 2, CH], F32))
        loaded = [ctx.enter_context(nc.semaphore(f"loaded{n_cols}_{k}")) for k in range(2)]
        hi_done = ctx.enter_context(nc.semaphore(f"hi_done{n_cols}"))
        lo_done = ctx.enter_context(nc.semaphore(f"lo_done{n_cols}"))
        block = ctx.enter_context(nc.Block())

        @block.sync
        def _(sp):
            for c in range(n):
                wait(sp, lo_done, c - 1)
                sp.dma_start(stage[:, c % 2, :], src[:, c * CH:(c + 1) * CH]).then_inc(loaded[c % 2], 16)

        @block.scalar
        def _(act):
            for c in range(n):
                act.wait_ge(loaded[c % 2], 16 * (c // 2 + 1))
                act.activation(hi[:, c * CH:(c + 1) * CH], stage[:, c % 2, :], ACT.Copy).then_inc(hi_done, 1)

        @block.vector
        def _(dve):
            for c in range(n):
                dve.wait_ge(hi_done, c + 1)
                dve.tensor_tensor(lo[:, c * CH:(c + 1) * CH], stage[:, c % 2, :], hi[:, c * CH:(c + 1) * CH],
                                  ALU.subtract).then_inc(lo_done, 1)


def load_all(nc, pairs, tag):
    with nc.semaphore(f"loads_{tag}") as loads, nc.Block() as block:
        @block.sync
        def _(sp):
            for dst, src in pairs:
                sp.dma_start(dst, src).then_inc(loads, 16)
            sp.wait_ge(loads, 16 * len(pairs))


def narrow_attention(nc, c, X, Y, latent):
    W, SM = c["parts"], c["small"]
    NK = P if latent else KC
    tag = "m" if latent else "a"
    USES = 8 if latent else 4
    POOL_STACKS, SYNC_STACKS = (range(1), range(1, HQ)) if latent else (range(HQ // 2), range(HQ // 2, HQ))
    N_SYNC, N_POOL = 3 * (HQ + len(SYNC_STACKS)), 3 * len(POOL_STACKS)
    with ExitStack() as ctx:
        def sb(name, shape, dt):
            return ctx.enter_context(nc.sbuf_tensor(f"{tag}_{name}", shape, dt))

        def pb(name, shape, dt=F32):
            return ctx.enter_context(nc.psum_tensor(f"{tag}_{name}", shape, dt))

        def sem(name):
            return ctx.enter_context(nc.semaphore(f"{tag}_{name}"))


        Qd = sb("Qd", [P, 2, HQ, HQ, TG], F16)
        Ks = sb("Ks", [P, 2, HQ, GB * NK], F16)
        qh, ql = sb("qh", [P, TG], F16), sb("ql", [P, TG], F16)
        kh, kl = sb("kh", [P, GB * NK], F16), sb("kl", [P, GB * NK], F16)
        V = sb("V", [P, 2, GB, H, HD + 1], F32)
        stats, aggr = sb("stats", [P, GB, 6], F32), sb("aggr", [P, GB, 2], F32)
        var, rstd = sb("var", [P, GB], F32), sb("rstd", [P, GB], F32)
        xn = sb("xn", [P, GB, D], F32)
        xh, xl = sb("xh", [P, TG], F16), sb("xl", [P, TG], F16)
        mx = sb("mx", [P, H], F32)
        ng = sb("ng", [P, H], F16)
        mT = sb("mT", [P, 2, P], F16)
        PT = sb("PT", [P, 2, H, P], F32)
        Os = sb("Os", [P, HQ, P], F32)
        rec = sb("rec", [P, H], F32)
        On = sb("On", [P, D], F32)
        oh, ol = sb("oh", [P, P], F16), sb("ol", [P, P], F16)
        if latent:
            sq, ms = sb("sq", [P, D], F32), sb("ms", [P, GB], F32)
            rv, rr = sb("rv", [P, GB], F32), sb("rr", [P, GB], F32)
            t1, t2 = sb("t1", [P, 2, TG], F32), sb("t2", [P, 2, TG], F32)
            lstats, laggr = sb("lstats", [P, GB, 6], F32), sb("laggr", [P, GB, 2], F32)
            lvar, lrstd = sb("lvar", [P, GB], F32), sb("lrstd", [P, GB], F32)
            latn = xn[:, :, 0:LAT]
            lt = xn[0:LAT, :, :].rearrange("p b d -> p (b d)")
            lh, ll = sb("lh", [LAT, TG], F16), sb("ll", [LAT, TG], F16)

        pM = pb("pM", [P, H // 2, P])
        pS = pb("pS", [P, H // 2, P])
        pV = pb("pV", [P, HQ, P])
        pO = pb("pO", [P, 512])
        pP = pb("pP", [P, 512])
        pT = pb("pT", [P, 512])
        pTh = pT[:, 0:P // 2].bitcast(F16)

        zeroed, x_norm, ln_agg, ln_rstd = sem("zeroed"), sem("x_norm"), sem("ln_agg"), sem("ln_rstd")
        ln_st = sem("ln_st")
        sq_done, ms_done, rms_r = sem("sq_done"), sem("ms_done"), sem("rms_r")
        used, hi_made, evac = sem("used"), sem("hi_made"), sem("evac")
        rope_in, rope_sum, rope_lo, rope_mul = sem("rope_in"), sem("rope_sum"), sem("rope_lo"), sem("rope_mul")
        lat_st, lat_agg, lat_rstd, lat_lo = sem("lat_st"), sem("lat_agg"), sem("lat_rstd"), sem("lat_lo")
        sync_sent = sem("sync_sent")
        pool_sent = sem("pool_sent")
        m_ready, m_max, neg, mt_ready, mt_kept = (sem("m_ready"), sem("m_max"), sem("neg"), sem("mt_ready"),
                                                  sem("mt_kept"))
        s_ready, exp_done, pv_ready, os_kept = sem("s_ready"), sem("exp_done"), sem("pv_ready"), sem("os_kept")
        t1_ready, rec_done, on_done, t2_ready = sem("t1_ready"), sem("rec_done"), sem("on_done"), sem("t2_ready")
        oh_done, ol_done, wo_ready, res_done = sem("oh_done"), sem("ol_done"), sem("wo_ready"), sem("res_done")
        own = sem("own")
        block = ctx.enter_context(nc.Block())

        if latent:
            order = ["q", "qs", "k", "ks", "v", "x", "lat", "latT"]
            first_use = 3
        else:
            order = ["q", "k", "v", "x"]
            first_use = 1

        def use(g, what):
            back = 1 if what in ("x", "lat", "latT") else 0
            return lin(g, USES, first_use + order.index(what) - back * USES)

        if latent:
            slots = {(0, 0): "q", (0, 1): "qs", (1, 0): "k", (1, 1): "ks", (2, 0): "v", (2, 1): "x",
                     (3, 0): "lat", (3, 1): "latT"}
        else:
            slots = {(0, 0): "q", (0, 1): "k", (1, 0): "v", (2, 0): "x"}

        def slot(b, half, g, nxt, nxt2):
            what = slots.get((b, half))
            if what in ("x", "lat", "latT"):
                return (what, shift(g, 2), 2) if nxt2 else (None, None, 0)
            return (what, shift(g, 1), 1) if what and nxt else (None, None, 0)

        start_x = ["x", "lat", "latT"] if latent else ["x"]
        start = ([(w, 0) for w in start_x] + [(w, 0) for w in order if w not in start_x]
                 + [(w, 1) for w in start_x])

        def earlier(g, b, by):
            if b >= by:
                return g, b - by
            return None if is_first(g) else (shift(g, -1), b - by + GB)

        def walk(engine, begin, step, finish):
            begin()
            groups(engine, lambda g, p, nxt, nxt2: [step(g, p, b, nxt, nxt2) for b in range(GB)])
            finish()

        def hi_count(g, what):
            per = [w for w in order if w in (("x", "qs", "ks", "latT") if latent else ("x", "q", "k"))]
            lead = 2 if latent else 1
            back = 1 if what in ("x", "latT") else 0
            return lin(g, len(per), lead + per.index(what) + 1 - back * len(per))

        def stacked(engine, g):
            wait(engine, sync_sent, lin(g, 16 * N_SYNC, 0))
            wait(engine, pool_sent, lin(g, 16 * N_POOL, 0))

        def stack(engine, g, p, what, sent, blocks=range(HQ)):
            if what == "q":
                engine.wait_ge(rope_lo, lin(g, 2, 1)) if latent else engine.wait_ge(evac, use(g, "q") + 1)
            else:
                engine.wait_ge(rope_lo, lin(g, 2, 2)) if latent else engine.wait_ge(evac, use(g, "k") + 1)
            settle(engine, c)
            wait(engine, s_ready, lin(g, 2 * GB, -2 * GB))
            settle(engine, c)
            for j in blocks:
                for r in range(3):
                    if what == "q":
                        src = (qh, qh, ql)[r]
                        dst = Qd[32 * j + HD * r:32 * j + HD * (r + 1), p, :, j, :]
                    else:
                        src = (kh, kl, kh)[r]
                        dst = Ks[32 * j + HD * r:32 * j + HD * (r + 1), p, :, :]
                    engine.dma_start(dst, src[32 * j:32 * j + 32, :]).then_inc(sent, 16)

        @block.tensor
        def _(pe):
            pe.wait_ge(zeroed, 8)

            def project(what, g, p):
                u = use(g, what)
                wait(pe, evac, u)
                if what == "x":
                    pe.wait_ge(rms_r if latent else x_norm, lin(g, GB, GB))
                    for b in range(GB):
                        mm = pe.transpose(pP[:, b * P:(b + 1) * P], xn[:, b, :], c["ident"][:])
                elif what in ("q", "qs"):
                    wait(pe, evac, use(g, "x") + 1)
                    mm = product(pe, pP[:, :TG], W.of(f"{tag}_{what}", 0, D), (xh[:], xl[:]))
                elif what in ("k", "ks") and not latent:
                    mm = product(pe, pP[:, :GB * KC], W.of("a_k", 0, D), W.of("ctx", lin(g, GB * KC), GB * KC))
                elif what in ("k", "ks"):
                    pe.wait_ge(lat_lo, lin(g, 1, 1))
                    mm = product(pe, pP[:, :TG], W.of(f"m_{what}", 0, D, LAT), (lh[:], ll[:]))
                elif what == "v":
                    for b in range(GB):
                        if latent:
                            s = slice(b * P, (b + 1) * P)
                            mm = product(pe, pP[:, s], (lh[:, s], ll[:, s]), W.of("m_v", 0, D, LAT))
                        else:
                            mm = product(pe, pP[:KC, b * P:(b + 1) * P], W.of("ctx", lin(g, GB * KC, b * KC), KC),
                                         W.of("a_v", 0, D))
                elif what == "lat":
                    wait(pe, evac, use(g, "x") + 1)
                    for b in range(GB):
                        s = slice(b * P, (b + 1) * P)
                        mm = product(pe, pP[:, b * LAT:(b + 1) * LAT], (xh[:, s], xl[:, s]), W.of("m_kv", 0, LAT))
                elif what == "latT":
                    settle(pe, c)
                    for b in range(GB):
                        mm = pe.transpose(pP[:LAT, b * P:(b + 1) * P], latn[:, b, :], c["ident"][:])
                mm.then_inc(used, 1)

            def maxima(g, p, b, half, gd):
                wait(pe, m_max, lin(gd, 2 * GB, 2 * b + half))
                if b == 0 and half == 0:
                    stacked(pe, shift(gd, 1))
                for gg in range(2):
                    hg = 2 * half + gg
                    if latent:
                        pe.matmul(pM[:, 4 * gg:4 * gg + 4, :], c["id16"][:].bitcast(BF16), c["maskM"][:].bitcast(BF16), start=True, stop=False,
                                  skip_group_check=True)
                    for j in range(HQ):
                        mm = pe.matmul(pM[:, 4 * gg + j, :NK], Qd[:, p, hg, j, b * P:(b + 1) * P],
                                       Ks[:, p, hg, b * NK:(b + 1) * NK], start=not latent, stop=True,
                                       skip_group_check=True)
                mm.then_inc(m_ready, 1)

            def max_transpose(g, p, b):
                pe.wait_ge(neg, lin(g, GB, b + 1))
                pe.transpose(pTh[:H, :], ng[:], c["ident16"][:]).then_inc(mt_ready, 1)

            def scores(g, p, b, half):
                wait(pe, exp_done, lin(g, 2 * GB, 2 * b + half))
                if half == 0:
                    pe.wait_ge(mt_kept, lin(g, GB, b + 1))
                for gg in range(2):
                    hg = 2 * half + gg
                    pe.matmul(pS[:NK, 4 * gg:4 * gg + 4, :], Ks[:, p, hg, b * NK:(b + 1) * NK],
                              Qd[:, p, hg, :, b * P:(b + 1) * P], start=True, stop=False, skip_group_check=True)
                    if latent:
                        pe.matmul(pS[:, 4 * gg:4 * gg + 4, :], c["id16"][:].bitcast(BF16), c["maskS"][:].bitcast(BF16), start=False, stop=False,
                                  skip_group_check=True)
                    for j in range(HQ):
                        mm = pe.matmul(pS[:NK, 4 * gg + j, :], c["sel"][:, HQ * hg + j, :NK], mT[:, b % 2, :],
                                       start=False, stop=(j == HQ - 1), skip_group_check=True)
                mm.then_inc(s_ready, 1)

            def values(g, p, b):
                wait(pe, exp_done, lin(g, 2 * GB, 2 * b + 2))
                wait(pe, os_kept, lin(g, GB, b))
                if b == 0:
                    pe.wait_ge(evac, use(g, "v") + 1)
                for hg in range(HQ):
                    for j in range(HQ):
                        h = HQ * hg + j
                        mm = pe.matmul(pV[32 * j:32 * j + HD + 1, hg, :], V[:NK, p, b, h, :], PT[:NK, b % 2, h, :],
                                       start=True, stop=True)
                mm.then_inc(pv_ready, 1)

            def turn_heads(g, b):
                pe.wait_ge(os_kept, lin(g, GB, b + 1))
                wait(pe, res_done, lin(g, GB, b))
                for hg in range(HQ):
                    mm = pe.transpose(pO[:, hg * P:(hg + 1) * P], Os[:, hg, :], c["ident"][:])
                mm.then_inc(t1_ready, 1)

            def turn_output(g, b):
                pe.wait_ge(on_done, lin(g, GB, b + 1))
                pe.transpose(pO[:, :P], On[:], c["ident"][:]).then_inc(t2_ready, 1)

            def project_output(g, b):
                pe.wait_ge(oh_done, lin(g, GB, b + 1))
                pe.wait_ge(ol_done, lin(g, GB, b + 1))
                if latent:
                    mm = product(pe, pO[:, :D], (oh[:], ol[:]), W.of("m_o", 0, D))
                else:
                    product(pe, pO[:, :D], (oh[:], ol[:]), W.of("a_o", 0, D), last=False)
                    bh, bl = W.of("a_bo", 0, D)
                    pe.matmul(pO[:, :D], c["row0"][:], bh, start=False, stop=False)
                    mm = pe.matmul(pO[:, :D], c["row0"][:], bl, start=False, stop=True)
                mm.then_inc(wo_ready, 1)

            def begin():
                for what, k in start:
                    project(what, (None, k), k)
                maxima(None, 0, 0, 0, (None, 0))
                maxima(None, 0, 0, 1, (None, 0))

            def step(g, p, b, nxt, nxt2):
                gn, pn, bn = (g, p, b + 1) if b < GB - 1 else (shift(g, 1), 1 - p, 0)
                gp, pp, bp = (g, p, b - 1) if b else (shift(g, -1), 1 - p, GB - 1)
                more = nxt or b < GB - 1
                before = b > 0 or not is_first(g)
                two = earlier(g, b, 2)
                max_transpose(g, p, b)
                what, gw, far = slot(b, 0, g, nxt, nxt2)
                if what:
                    project(what, gw, None)
                if more:
                    maxima(None, pn, bn, 0, gn)
                if before:
                    values(gp, pp, bp)
                if two:
                    project_output(*two)
                scores(g, p, b, 0)
                if before:
                    turn_heads(gp, bp)
                if more:
                    maxima(None, pn, bn, 1, gn)
                what, gw, far = slot(b, 1, g, nxt, nxt2)
                if what:
                    project(what, gw, None)
                scores(g, p, b, 1)
                if before:
                    turn_output(gp, bp)

            def finish():
                g = (None, NG - 1)
                values(g, 1, GB - 1)
                project_output(g, GB - 2)
                turn_heads(g, GB - 1)
                turn_output(g, GB - 1)
                project_output(g, GB - 1)

            walk(pe, begin, step, finish)

        @block.scalar
        def _(act):
            def part(what, g):
                u = use(g, what)
                if what == "x":
                    act.wait_ge(used, u + 1)
                    if latent:
                        act.activation(xh[:], pP[:, :TG], ACT.Copy, scale=SM("n1")).then_inc(hi_made, 1)
                    else:
                        act.activation(xh[:], pP[:, :TG], ACT.Copy).then_inc(hi_made, 1)
                elif what in ("q", "k") and not latent:
                    dst, n = (qh, TG) if what == "q" else (kh, GB * KC)
                    act.wait_ge(used, u + 1)
                    stacked(act, g)
                    act.activation(dst[:, :n], pP[:, :n], ACT.Identity, bias=SM("b" + what)).then_inc(hi_made, 1)
                elif what in ("qs", "ks"):
                    dst = qh if what == "qs" else kh
                    stacked(act, g)
                    act.wait_ge(rope_sum, lin(g, 2, 1 if what == "qs" else 2))
                    act.activation(dst[:], t1[:, int(what == "ks"), :], ACT.Copy).then_inc(hi_made, 1)
                elif what == "latT":
                    act.wait_ge(evac, u + 1)
                    act.activation(lh[:], lt, ACT.Copy).then_inc(hi_made, 1)

            def squares(g):
                for b in range(GB):
                    act.wait_ge(x_norm, lin(g, GB, b + 1))
                    wait(act, ms_done, lin(g, 1, 0))
                    wait(act, sq_done, lin(g, GB, b))
                    act.activation(sq[:], Y[:, bass.ds(lin(g, GB, b), 1), :], ACT.Square,
                                   accum_out=ms[:, b:b + 1]).then_inc(sq_done, 1)

            def exps(g, p, b, half):
                act.wait_ge(s_ready, lin(g, 2 * GB, 2 * b + half + 1))
                if half == 0:
                    wait(act, pv_ready, lin(g, GB, b - 1))
                act.activation(PT[:NK, b % 2, 8 * half:8 * half + 8, :], pS[:NK, :, :], ACT.Exp,
                               scale=float(1.0 / np.sqrt(HD))).then_inc(exp_done, 1)

            def keep_heads(g, b):
                act.wait_ge(pv_ready, lin(g, GB, b + 1))
                wait(act, t1_ready, lin(g, GB, b))
                act.activation(Os[:], pV[:], ACT.Copy).then_inc(os_kept, 1)

            def output_hi(g, b):
                act.wait_ge(t2_ready, lin(g, GB, b + 1))
                wait(act, wo_ready, lin(g, GB, b))
                if latent:
                    act.activation(oh[:], pO[:, :P], ACT.Copy).then_inc(oh_done, 1)
                else:
                    act.activation(oh[:], pO[:, :P], ACT.Identity, bias=SM("bv")).then_inc(oh_done, 1)

            def begin():
                act.wait_ge(zeroed, 8)
                if latent:
                    squares((None, 0))
                for what, k in start:
                    if latent and what == "x" and k == 1:
                        squares((None, 1))
                    part(what, (None, k))

            def step(g, p, b, nxt, nxt2):
                gp, pp, bp = (g, p, b - 1) if b else (shift(g, -1), 1 - p, GB - 1)
                before = b > 0 or not is_first(g)
                what, gw, far = slot(b, 0, g, nxt, nxt2)
                if what:
                    part(what, gw)
                if before:
                    keep_heads(gp, bp)
                exps(g, p, b, 0)
                what, gw, far = slot(b, 1, g, nxt, nxt2)
                late = what in ("qs", "ks")
                if what and not late:
                    part(what, gw)
                exps(g, p, b, 1)
                if before:
                    output_hi(gp, bp)
                if late:
                    part(what, gw)
                if latent and b == 1 and nxt2:
                    squares(shift(g, 2))

            def finish():
                g = (None, NG - 1)
                keep_heads(g, GB - 1)
                output_hi(g, GB - 1)

            walk(act, begin, step, finish)

        @block.vector
        def _(dve):
            def norm_stats(g):
                for b in range(GB):
                    dve.bn_stats(stats[:, b, :], X[:, bass.ds(lin(g, GB, b), 1), :]).then_inc(ln_st, 1)
                for b in range(GB):
                    dve.wait_ge(ln_st, lin(g, GB, b + 1))
                    if b == 0:
                        wait(dve, ln_rstd, lin(g, 1, 0))
                        wait(dve, x_norm, lin(g, GB, 0))
                    settle(dve, c)
                    dve.bn_aggr(aggr[:, b, :], stats[:, b, :]).then_inc(ln_agg, 1)

            def norm_rows(g):
                dve.wait_ge(ln_rstd, lin(g, 1, 1))
                if not latent:
                    wait(dve, used, use(g, "x") - USES + 1)
                for b in range(GB):
                    n = bass.ds(lin(g, GB, b), 1)
                    dst = Y[:, n, :] if latent else xn[:, b:b + 1, :]
                    dve.tensor_scalar(dst, X[:, n, :], aggr[:, b, 0:1], rstd[:, b:b + 1], ALU.subtract,
                                      ALU.mult).then_inc(x_norm, 1)

            def rms_rows(g):
                dve.wait_ge(ms_done, lin(g, 1, 1))
                if not is_first(g):
                    dve.wait_ge(lat_lo, lin(g, 1, 0))
                for b in range(GB):
                    dve.tensor_scalar(xn[:, b:b + 1, :], Y[:, bass.ds(lin(g, GB, b), 1), :], rr[:, b:b + 1], None,
                                      ALU.mult).then_inc(rms_r, 1)

            def part(what, g, p):
                u = use(g, what)
                if what == "x":
                    dve.wait_ge(hi_made, hi_count(g, what))
                    if latent:
                        dve.scalar_tensor_tensor(xl[:], pP[:, :TG], SM("n1"), xh[:], ALU.mult,
                                                 ALU.subtract).then_inc(evac, 1)
                    else:
                        dve.tensor_tensor(xl[:], pP[:, :TG], xh[:], ALU.subtract).then_inc(evac, 1)
                elif what in ("q", "k") and not latent:
                    hi, lo, n = (qh, ql, TG) if what == "q" else (kh, kl, GB * KC)
                    dve.wait_ge(hi_made, hi_count(g, what))
                    dve.scalar_tensor_tensor(lo[:, :n], pP[:, :n], SM("b" + what), hi[:, :n], ALU.add,
                                             ALU.subtract).then_inc(evac, 1)
                elif what in ("q", "qs", "k", "ks"):
                    dve.wait_ge(used, u + 1)
                    if what in ("q", "k"):
                        wait(dve, rope_lo, lin(g, 2, -1 if what == "q" else 0))
                    dst, table = (t1, "cos") if what in ("q", "k") else (t2, "sin")
                    dve.tensor_tensor(dst[:, int(what in ("k", "ks")), :].rearrange("p (b t) -> p b t", b=GB),
                                      pP[:, :TG].rearrange("p (b t) -> p b t", b=GB),
                                      c[table][:].rearrange("p (o t) -> p o t", o=1).to_broadcast([P, GB, P]),
                                      ALU.mult).then_inc(evac, 1)
                elif what == "v":
                    dve.wait_ge(used, u + 1)
                    wait(dve, pv_ready, lin(g, GB, -GB))
                    for b in range(GB):
                        cp = dve.tensor_copy(V[:NK, p, b, :, 0:HD],
                                             pP[:NK, b * P:(b + 1) * P].rearrange("k (h d) -> k h d", h=H))
                    cp.then_inc(evac, 1)
                elif what == "lat":
                    dve.wait_ge(used, u + 1)
                    for b in range(GB):
                        dve.bn_stats(lstats[:, b, :], pP[:, b * LAT:(b + 1) * LAT]).then_inc(lat_st, 1)
                    for b in range(GB):
                        dve.wait_ge(lat_st, lin(g, GB, b + 1))
                        settle(dve, c)
                        dve.bn_aggr(laggr[:, b, :], lstats[:, b, :]).then_inc(lat_agg, 1)
                    dve.wait_ge(lat_rstd, lin(g, 1, 1))
                    for b in range(GB):
                        ts = dve.tensor_scalar(latn[:, b, :], pP[:, b * LAT:(b + 1) * LAT], laggr[:, b, 0:1],
                                               lrstd[:, b:b + 1], ALU.subtract, ALU.mult)
                    ts.then_inc(evac, 1)
                elif what == "latT":
                    dve.wait_ge(used, u + 1)
                    wait(dve, lat_lo, lin(g, 1, 0))
                    dve.tensor_scalar(lt, pP[:LAT, :TG], SM("lg", LAT), SM("lb", LAT), ALU.mult,
                                      ALU.add).then_inc(evac, 1)

            def take_max(g, b, half):
                dve.wait_ge(m_ready, lin(g, 2 * GB, 2 * b + half + 1))
                if half == 0:
                    wait(dve, neg, lin(g, GB, b))
                dve.tensor_reduce(out=mx[:, 8 * half:8 * half + 8], in_=pM[:, :, :NK], op=ALU.max,
                                  axis=AX.X).then_inc(m_max, 1)

            def negate(g, b):
                dve.wait_ge(m_max, lin(g, 2 * GB, 2 * b + 2))
                wait(dve, mt_ready, lin(g, GB, b))
                dve.tensor_scalar(ng[:], mx[:], -1.0 / SHIFT, None, ALU.mult).then_inc(neg, 1)

            def keep_max(g, b):
                dve.wait_ge(mt_ready, lin(g, GB, b + 1))
                wait(dve, s_ready, lin(g, 2 * GB, 2 * (b - 1)))
                dve.tensor_copy(mT[:H, b % 2, :], pTh[:H, :]).then_inc(mt_kept, 1)

            def divide(g, b):
                dve.wait_ge(t1_ready, lin(g, GB, b + 1))
                wait(dve, on_done, lin(g, GB, b))
                dve.reciprocal(rec[:].rearrange("p (h o) -> p h o", o=1),
                               pO[:].rearrange("p (h c) -> p h c", h=H)[:, :, HD:HD + 1]).then_inc(rec_done, 1)
                dve.wait_ge(rec_done, lin(g, GB, b + 1))
                wait(dve, t2_ready, lin(g, GB, b))
                dve.tensor_tensor(On[:].rearrange("p (h d) -> p h d", h=H),
                                  pO[:].rearrange("p (h c) -> p h c", h=H)[:, :, 0:HD],
                                  rec[:].rearrange("p (h o) -> p h o", o=1).to_broadcast([P, H, HD]),
                                  ALU.mult).then_inc(on_done, 1)

            def output_lo(g, b):
                dve.wait_ge(oh_done, lin(g, GB, b + 1))
                if latent:
                    dve.tensor_tensor(ol[:], pO[:, :P], oh[:], ALU.subtract).then_inc(ol_done, 1)
                else:
                    dve.scalar_tensor_tensor(ol[:], pO[:, :P], SM("bv"), oh[:], ALU.add,
                                             ALU.subtract).then_inc(ol_done, 1)

            def residual(g, b):
                n = bass.ds(lin(g, GB, b), 1)
                dve.wait_ge(wo_ready, lin(g, GB, b + 1))
                R = Y if latent else X
                dve.tensor_tensor(R[:, n, :], pO[:, :D].rearrange("p (o d) -> p o d", o=1), R[:, n, :],
                                  ALU.add).then_inc(res_done, 1)

            def begin():
                dve.memset(Qd[:, 0].bitcast(F32), 0.0).then_inc(zeroed, 1)
                dve.memset(Qd[:, 1].bitcast(F32), 0.0).then_inc(zeroed, 1)
                dve.memset(Ks[:].bitcast(F32), 0.0).then_inc(zeroed, 1)
                dve.memset(V[:], 1.0).then_inc(zeroed, 1)
                dve.memset(mT[:].bitcast(F32), 0.0).then_inc(zeroed, 1)
                dve.memset(pV[:], 0.0).then_inc(zeroed, 1)
                dve.memset(mx[:], 0.0).then_inc(zeroed, 1)
                dve.memset(var[:], 0.0).then_inc(zeroed, 1)
                dve.wait_ge(zeroed, 8)
                for what, k in start:
                    if what == "x":
                        norm_stats((None, k))
                        norm_rows((None, k))
                        if latent:
                            rms_rows((None, k))
                    part(what, (None, k), k)
                take_max((None, 0), 0, 0)
                take_max((None, 0), 0, 1)
                negate((None, 0), 0)

            def step(g, p, b, nxt, nxt2):
                gn, pn, bn = (g, p, b + 1) if b < GB - 1 else (shift(g, 1), 1 - p, 0)
                gp, pp, bp = (g, p, b - 1) if b else (shift(g, -1), 1 - p, GB - 1)
                more = nxt or b < GB - 1
                before = b > 0 or not is_first(g)
                two = earlier(g, b, 2)
                keep_max(g, b)
                what, gw, far = slot(b, 0, g, nxt, nxt2)
                if what:
                    part(what, gw, (p + far) % 2)
                if more:
                    take_max(gn, bn, 0)
                if two:
                    residual(*two)
                if latent and b == 2 and nxt2:
                    rms_rows(shift(g, 2))
                if before:
                    divide(gp, bp)
                if more:
                    take_max(gn, bn, 1)
                    negate(gn, bn)
                what, gw, far = slot(b, 1, g, nxt, nxt2)
                if what:
                    part(what, gw, (p + far) % 2)
                if b == 0 and nxt2:
                    norm_stats(shift(g, 2))
                if b == 1 and nxt2:
                    norm_rows(shift(g, 2))
                if before:
                    output_lo(gp, bp)

            def finish():
                g = (None, NG - 1)
                residual(g, GB - 2)
                divide(g, GB - 1)
                output_lo(g, GB - 1)
                residual(g, GB - 1)

            walk(dve, begin, step, finish)

        @block.gpsimd
        def _(pool):

            def root(g, src_ready, value, src, out, mult, eps, tmp, done):
                src_ready()
                settle(pool, c)
                pool.tensor_scalar(tmp, src, mult, eps, ALU.mult, ALU.add).then_inc(own, 1)
                pool.wait_ge(own, value)
                pool.tensor_tensor(out, tmp, c["mhalf"][:, 0:GB], ALU.pow).then_inc(done, 1)

            per = 3 if latent else 1

            def rows(g):
                wait(pool, x_norm, lin(g, GB, 0))
                root(g, lambda: pool.wait_ge(ln_agg, lin(g, GB, GB)), row_root(g), aggr[:, :, 1], rstd[:],
                     1.0, LN_EPS, var[:], ln_rstd)

            def row_root(g):
                return lin(g, per, 1) if not latent else own_count(g, "rows")

            def own_count(g, what):
                return lin(g, 3, {"rows": 1, "squares": 2, "lat": 3}[what])

            def squares(g):
                root(g, lambda: pool.wait_ge(sq_done, lin(g, GB, GB)), own_count(g, "squares"), ms[:], rr[:],
                     1.0 / D, RMS_EPS, rv[:], ms_done)

            def latents(g):
                root(g, lambda: pool.wait_ge(lat_agg, lin(g, GB, GB)), own_count(g, "lat"), laggr[:, :, 1], lrstd[:],
                     1.0, LN_EPS, lvar[:], lat_rstd)

            def rope(what, g):
                if what in ("qs", "ks"):
                    k = 0 if what == "qs" else 1
                    hi, lo = (qh, ql) if what == "qs" else (kh, kl)
                    pool.wait_ge(evac, use(g, what) + 1)
                    pool.tensor_tensor(t1[:, k, :], t1[:, k, :], t2[:, k, :], ALU.add).then_inc(rope_sum, 1)
                    pool.wait_ge(rope_sum, lin(g, 2, 1 + k))
                    pool.wait_ge(hi_made, hi_count(g, what))
                    stacked(pool, g)
                    pool.tensor_tensor(lo[:], t1[:, k, :], hi[:], ALU.subtract).then_inc(rope_lo, 1)
                elif what == "latT":
                    pool.wait_ge(evac, use(g, what) + 1)
                    pool.wait_ge(hi_made, hi_count(g, what))
                    pool.tensor_tensor(ll[:], lt, lh[:], ALU.subtract).then_inc(lat_lo, 1)
                elif what == "lat":
                    latents(g)

            def begin():
                for what, k in start:
                    if what == "x":
                        rows((None, k))
                        squares((None, k))
                    rope(what, (None, k))
                    if (what, k) == ("ks", 0):
                        stack(pool, (None, 0), 0, "k", pool_sent, POOL_STACKS)

            def step(g, p, b, nxt, nxt2):
                for half_ in (0, 1):
                    what, gw, far = slot(b, half_, g, nxt, nxt2)
                    if what:
                        rope(what, gw)
                if b == 0 and nxt2:
                    rows(shift(g, 2))
                if b == 1 and nxt2:
                    squares(shift(g, 2))
                if b == 1 and nxt:
                    stack(pool, shift(g, 1), 1 - p, "k", pool_sent, POOL_STACKS)

            pool.wait_ge(zeroed, 8)
            if latent:
                walk(pool, begin, step, lambda: None)
            else:
                rows((None, 0))
                rows((None, 1))
                stack(pool, (None, 0), 0, "k", pool_sent, POOL_STACKS)
                groups(pool, lambda g, p, nxt, nxt2: (rows(shift(g, 2)) if nxt2 else None,
                                                      stack(pool, shift(g, 1), 1 - p, "k", pool_sent, POOL_STACKS) if nxt else None))

        @block.sync
        def _(sp):
            sp.wait_ge(zeroed, 8)

            def begin():
                stack(sp, (None, 0), 0, "q", sync_sent)
                stack(sp, (None, 0), 0, "k", sync_sent, SYNC_STACKS)

            def step(g, p, b, nxt, nxt2):
                if b == 0 and nxt:
                    stack(sp, shift(g, 1), 1 - p, "q", sync_sent)
                    stack(sp, shift(g, 1), 1 - p, "k", sync_sent, SYNC_STACKS)

            walk(sp, begin, step, lambda: None)

    if latent:
        add_rows(nc, X, Y)


def add_rows(nc, X, Y):
    with nc.semaphore("rows_added") as added, nc.Block() as block:
        @block.vector
        def _(dve):
            for n in range(0, NB, 8):
                last = dve.tensor_tensor(X[:, n:n + 8, :], X[:, n:n + 8, :], Y[:, n:n + 8, :], ALU.add)
            last.then_inc(added, 1)
            dve.wait_ge(added, 1)


def wide_attention(nc, c, X):
    W = c["parts"]
    HB = WH_ // 2
    with ExitStack() as ctx:
        def sb(name, shape, dt):
            return ctx.enter_context(nc.sbuf_tensor(f"w_{name}", shape, dt))

        def pb(name, shape, dt=F32):
            return ctx.enter_context(nc.psum_tensor(f"w_{name}", shape, dt))

        def sem(name):
            return ctx.enter_context(nc.semaphore(f"w_{name}"))


        stats, aggr = sb("stats", [P, GB, 6], F32), sb("aggr", [P, GB, 2], F32)
        var, rstd = sb("var", [P, GB], F32), sb("rstd", [P, GB], F32)
        xn = sb("xn", [P, GB, D], F32)
        xh, xl = sb("xh", [P, TG], F16), sb("xl", [P, TG], F16)
        Qh, Ql = sb("Qh", [P, 2, HB, TG], F16), sb("Ql", [P, 2, HB, TG], F16)
        Kh, Kl = sb("Kh", [P, 2, HB, 2, GB * KC], F16), sb("Kl", [P, 2, HB, 2, GB * KC], F16)
        V = sb("V", [P, 2, WH_, WD + 1], F32)
        mx = sb("mx", [P, WH_], F32)
        ng = sb("ng", [P, WH_], F16)
        mT = sb("mT", [P, 2, P], F16)
        PT = sb("PT", [P, 2, WH_, P], F32)
        rec, O = sb("rec", [P, 2, HB, 1], F32), sb("O", [P, WHID], F32)
        oh, ol = sb("oh", [P, 2, HB, P], F16), sb("ol", [P, 2, HB, P], F16)

        pM = pb("pM", [P, WH_, P])
        pS = pb("pS", [P, WH_, P])
        pV = pb("pV", [P, 2, 512])
        heads_out = pV[:, :, :HB * (WD + 1)].rearrange("p b (h d) -> p b h d", d=WD + 1)
        pP = pb("pP", [P, 512])
        pT = pb("pT", [P, 512])

        zeroed, x_norm, ln_st, ln_agg, ln_rstd = (sem("zeroed"), sem("x_norm"), sem("ln_st"), sem("ln_agg"),
                                                  sem("ln_rstd"))
        own, used, hi_made, evac = sem("own"), sem("used"), sem("hi_made"), sem("evac")
        v_kept = sem("v_kept")
        m_ready, m_max, neg, mt_ready, mt_kept = (sem("m_ready"), sem("m_max"), sem("neg"), sem("mt_ready"),
                                                  sem("mt_kept"))
        s_ready, exp_done, pv_ready, rec_done, o_done = (sem("s_ready"), sem("exp_done"), sem("pv_ready"),
                                                         sem("rec_done"), sem("o_done"))
        o_turned = sem("o_turned")
        oh_done, ol_done, wo_ready, res_done = sem("oh_done"), sem("ol_done"), sem("wo_ready"), sem("res_done")
        block = ctx.enter_context(nc.Block())

        LEAD, USES = 2 + 2 * HB, 3 * GB + 1
        KEPT = 2 * GB + 1

        def is_start(g, what):
            return g[0] is None and (what == "x" and g[1] < 2 or what in "qk" and g[1] == 0)

        def is_last(g):
            return g[0] is None and g[1] == NG - 1

        def x_before_k(g, b):
            return int(b == GB - 1 and not is_last(g))

        def use(g, what, b=0):
            if is_start(g, what):
                return {"x": 0 if g[1] == 0 else LEAD - 1, "q": 1 + 2 * b, "k": 2 + 2 * b}[what]
            if what == "x":
                return lin(g, USES, LEAD - 2 * USES + 3 * GB - 1)
            if what == "v":
                return LEAD + USES * (NG - 1) - 1 + b if is_last(g) else lin(g, USES, LEAD + 3 * b + 1)
            if what == "q":
                return lin(g, USES, LEAD - USES + 3 * b)
            return lin(g, USES, LEAD - USES + 3 * b + 2 + x_before_k(g, b))

        def values_before(g, what, b):
            if is_start(g, what):
                return 0
            if what == "x":
                return lin(g, GB, -GB)
            return lin(g, GB, {"q": b - GB, "v": b, "k": b - GB + 1}[what])

        def by_vector(g, what, b=0):
            if is_start(g, what):
                return use(g, what, b) + 1
            if what == "x":
                return lin(g, KEPT, LEAD - 2 * KEPT + 2 * GB)
            if what == "v":
                return LEAD + KEPT * (NG - 1) - 1 if is_last(g) else lin(g, KEPT, LEAD + 2 * b + 1)
            if what == "q":
                return lin(g, KEPT, LEAD - KEPT + 2 * b + 1)
            return lin(g, KEPT, LEAD - KEPT + 2 * b + 2 + x_before_k(g, b))

        def earlier(g, b, by):
            if b >= by:
                return g, b - by
            return None if is_first(g) else (shift(g, -1), b - by + GB)

        def walk(engine, begin, step, finish):
            begin()
            groups(engine, lambda g, p, nxt, nxt2: [step(g, p, b, nxt, nxt2) for b in range(GB)])
            finish()

        start = [("x", 0, 0)] + [(w, 0, b) for b in range(HB) for w in "qk"] + [("x", 1, 0)]

        @block.tensor
        def _(pe):
            pe.wait_ge(zeroed, 4)

            def project(what, g, b):
                wait(pe, evac, by_vector(g, what, b) - (what != "v"))
                wait(pe, v_kept, values_before(g, what, b))
                if what == "x":
                    pe.wait_ge(x_norm, lin(g, GB, GB))
                    for t in range(GB):
                        mm = pe.transpose(pP[:, t * P:(t + 1) * P], xn[:, t, :], c["ident"][:])
                elif what == "q":
                    wait(pe, evac, by_vector(g, "x"))
                    mm = product(pe, pP[:, :TG], W.of("w_q", b * P, P), (xh[:], xl[:]))
                elif what == "k":
                    mm = product(pe, pP[:, :GB * KC], W.of("w_k", b * P, P), W.of("ctx", lin(g, GB * KC), GB * KC))
                else:
                    mm = product(pe, pP[:KC, :], W.of("ctx", lin(g, GB * KC, b * KC), KC), W.of("w_v", 0, WHID))
                mm.then_inc(used, 1)

            def maxima(g, p, b):
                wait(pe, m_max, lin(g, GB, b))
                if b == 0:
                    pe.wait_ge(evac, by_vector(g, "k", HB - 1))
                for k in range(HB):
                    mm = pe.matmul(pM[:, 2 * k:2 * k + 2, :KC], Qh[:, p, k, b * P:(b + 1) * P],
                                   Kh[:, p, k, :, b * KC:(b + 1) * KC], start=True, stop=True)
                mm.then_inc(m_ready, 1)

            def max_transpose(g, b):
                pe.wait_ge(neg, lin(g, GB, b + 1))
                wait(pe, res_done, lin(g, GB, b - 2))
                pe.transpose(pT[:, :P // 2].bitcast(F16)[:WH_, :], ng[:], c["ident16"][:]).then_inc(mt_ready, 1)

            def scores(g, p, b):
                wait(pe, exp_done, lin(g, GB, b))
                q, k = slice(b * P, (b + 1) * P), slice(b * KC, (b + 1) * KC)
                for h in range(WH_):
                    product(pe, pS[:KC, h, :], (Kh[:, p, h // 2, h % 2, k], Kl[:, p, h // 2, h % 2, k]),
                            (Qh[:, p, h // 2, q], Ql[:, p, h // 2, q]), first=h % HB == 0, last=False, check=False)

            def shift_scores(g, b):
                pe.wait_ge(mt_kept, lin(g, GB, b + 1))
                for h in range(WH_):
                    mm = pe.matmul(pS[:KC, h, :], c["sel"][:, h, :KC], mT[:, b % 2, :],
                                   start=False, stop=h % HB == HB - 1, skip_group_check=True)
                mm.then_inc(s_ready, 1)

            def values(g, b):
                pe.wait_ge(exp_done, lin(g, GB, b + 1))
                wait(pe, ol_done, lin(g, GB, b))
                pe.wait_ge(v_kept, lin(g, GB, b + 1))
                for h in range(WH_):
                    mm = pe.matmul(heads_out[:, h // HB, h % HB, :], PT[:KC, b % 2, h, :], V[:KC, b % 2, h, :],
                                   start=True, stop=True)
                mm.then_inc(pv_ready, 1)

            def turn_output(g, b):
                pe.wait_ge(o_done, lin(g, GB, b + 1))
                for k in range(HB):
                    mm = pe.transpose(pV[:, 1, k * P:(k + 1) * P], O[:, k * P:(k + 1) * P], c["ident"][:])
                mm.then_inc(o_turned, 1)

            def project_output(g, b, maxima_before):
                pe.wait_ge(oh_done, lin(g, GB, b + 1))
                pe.wait_ge(ol_done, lin(g, GB, b + 1))
                pe.wait_ge(mt_kept, maxima_before)
                wait(pe, res_done, lin(g, GB, b))
                for k in range(HB):
                    product(pe, pT[:, :D], (oh[:, b % 2, k, :], ol[:, b % 2, k, :]), W.of("w_o", k * D, D), first=k == 0, last=False)
                bh, bl = W.of("w_bo", 0, D)
                pe.matmul(pT[:, :D], c["row0"][:], bh, start=False, stop=False)
                pe.matmul(pT[:, :D], c["row0"][:], bl, start=False, stop=True).then_inc(wo_ready, 1)

            def begin():
                for what, k, b in start:
                    project(what, (None, k), b)

            def step(g, p, b, nxt, nxt2):
                one, two = earlier(g, b, 1), earlier(g, b, 2)
                if one:
                    values(*one)
                maxima(g, p, b)
                if nxt:
                    project("q", shift(g, 1), b)
                scores(g, p, b)
                if one:
                    turn_output(*one)
                max_transpose(g, b)
                project("v", g, b)
                shift_scores(g, b)
                if b == GB - 1 and nxt2:
                    project("x", shift(g, 2), 0)
                if two:
                    project_output(*two, lin(g, GB, b + 1))
                if nxt:
                    project("k", shift(g, 1), b)

            def finish():
                g = (None, NG - 1)
                project_output(g, GB - 2, NB)
                values(g, GB - 1)
                turn_output(g, GB - 1)
                project_output(g, GB - 1, NB)

            walk(pe, begin, step, finish)

        @block.scalar
        def _(act):
            def part(what, g, p, b):
                act.wait_ge(used, use(g, what, b) + 1)
                if what == "x":
                    act.activation(xh[:], pP[:, :TG], ACT.Copy).then_inc(hi_made, 1)
                elif what == "q":
                    act.activation(Qh[:, p, b, :], pP[:, :TG], ACT.Copy).then_inc(hi_made, 1)
                elif what == "k":
                    act.activation(Kh[:WD, p, b, 0, :], pP[:WD, :GB * KC], ACT.Copy)
                    act.activation(Kh[WD:, p, b, 1, :], pP[WD:, :GB * KC], ACT.Copy).then_inc(hi_made, 1)
                else:
                    wait(act, pv_ready, lin(g, GB, b - 1))
                    act.activation(V[:KC, b % 2, :, :WD], pP[:KC, :].rearrange("k (h d) -> k h d", h=WH_),
                                   ACT.Copy).then_inc(v_kept, 1)

            def exps(g, b):
                act.wait_ge(s_ready, lin(g, GB, b + 1))
                wait(act, pv_ready, lin(g, GB, b - 1))
                act.activation(PT[:KC, b % 2, :, :], pS[:KC], ACT.Exp,
                               scale=float(WD) ** -0.5).then_inc(exp_done, 1)

            def output_hi(g, b):
                act.wait_ge(o_turned, lin(g, GB, b + 1))
                wait(act, wo_ready, lin(g, GB, b - 1))
                act.activation(oh[:, b % 2].rearrange("p k t -> p (k t)"), pV[:, 1, :], ACT.Copy).then_inc(oh_done, 1)

            def begin():
                act.wait_ge(zeroed, 4)
                for what, k, b in start:
                    part(what, (None, k), k, b)

            def step(g, p, b, nxt, nxt2):
                one = earlier(g, b, 1)
                if nxt:
                    part("q", shift(g, 1), 1 - p, b)
                if one:
                    output_hi(*one)
                part("v", g, p, b)
                exps(g, b)
                if b == GB - 1 and nxt2:
                    part("x", shift(g, 2), p, 0)
                if nxt:
                    part("k", shift(g, 1), 1 - p, b)

            walk(act, begin, step, lambda: output_hi((None, NG - 1), GB - 1))

        @block.vector
        def _(dve):
            def norm_stats(g, start=0, count=GB):
                for b in range(start, start + count):
                    dve.bn_stats(stats[:, b, :], X[:, bass.ds(lin(g, GB, b), 1), :]).then_inc(ln_st, 1)
                for b in range(start, start + count):
                    dve.wait_ge(ln_st, lin(g, GB, b + 1))
                    settle(dve, c)
                    dve.bn_aggr(aggr[:, b, :], stats[:, b, :]).then_inc(ln_agg, 1)

            def norm_rows(g, start=0, count=GB):
                dve.wait_ge(ln_rstd, lin(g, 1, 1))
                if not is_first(g):
                    dve.wait_ge(used, use(shift(g, -1), "x") + 1)
                for b in range(start, start + count):
                    dve.tensor_scalar(xn[:, b:b + 1, :], X[:, bass.ds(lin(g, GB, b), 1), :], aggr[:, b, 0:1],
                                      rstd[:, b:b + 1], ALU.subtract, ALU.mult).then_inc(x_norm, 1)

            def part(what, g, p, b):
                dve.wait_ge(hi_made, by_vector(g, what, b))
                if what == "x":
                    dve.tensor_tensor(xl[:], pP[:, :TG], xh[:], ALU.subtract).then_inc(evac, 1)
                elif what == "q":
                    dve.tensor_tensor(Ql[:, p, b, :], pP[:, :TG], Qh[:, p, b, :], ALU.subtract).then_inc(evac, 1)
                else:
                    for o in range(2):
                        half = slice(WD * o, WD * (o + 1))
                        tt = dve.tensor_tensor(Kl[half, p, b, o, :], pP[half, :GB * KC], Kh[half, p, b, o, :],
                                               ALU.subtract)
                    tt.then_inc(evac, 1)

            def take_max(g, b):
                dve.wait_ge(m_ready, lin(g, GB, b + 1))
                wait(dve, neg, lin(g, GB, b))
                dve.tensor_reduce(out=mx[:], in_=pM[:, :, :KC], op=ALU.max,
                                  axis=AX.X).then_inc(m_max, 1)
                dve.wait_ge(m_max, lin(g, GB, b + 1))
                wait(dve, mt_ready, lin(g, GB, b))
                dve.tensor_scalar(ng[:], mx[:], -1.0 / SHIFT, None, ALU.mult).then_inc(neg, 1)

            def keep_max(g, b):
                dve.wait_ge(mt_ready, lin(g, GB, b + 1))
                wait(dve, s_ready, lin(g, GB, b - 1))
                dve.tensor_copy(mT[:WH_, b % 2, :], pT[:, :P // 2].bitcast(F16)[:WH_, :]).then_inc(mt_kept, 1)

            def divide(g, b):
                dve.wait_ge(pv_ready, lin(g, GB, b + 1))
                dve.reciprocal(rec[:], heads_out[:, :, :, WD:]).then_inc(rec_done, 1)
                dve.wait_ge(rec_done, lin(g, GB, b + 1))
                wait(dve, o_turned, lin(g, GB, b))
                dve.tensor_tensor(O[:].rearrange("p (b h d) -> p b h d", b=2, h=HB), heads_out[:, :, :, :WD],
                                  rec[:].to_broadcast([P, 2, HB, WD]), ALU.mult).then_inc(o_done, 1)

            def output_lo(g, b):
                dve.wait_ge(oh_done, lin(g, GB, b + 1))
                dve.tensor_tensor(ol[:, b % 2].rearrange("p k t -> p (k t)"), pV[:, 1, :], oh[:, b % 2].rearrange("p k t -> p (k t)"),
                                  ALU.subtract).then_inc(ol_done, 1)

            def residual(g, b):
                n = bass.ds(lin(g, GB, b), 1)
                dve.wait_ge(wo_ready, lin(g, GB, b + 1))
                dve.tensor_tensor(X[:, n, :], pT[:, :D].rearrange("p (o d) -> p o d", o=1), X[:, n, :],
                                  ALU.add).then_inc(res_done, 1)

            def begin():
                dve.memset(mT[:].bitcast(F32), 0.0).then_inc(zeroed, 1)
                dve.memset(V[:], 1.0).then_inc(zeroed, 1)
                dve.memset(Kh[:].bitcast(F32), 0.0).then_inc(zeroed, 1)
                dve.memset(Kl[:].bitcast(F32), 0.0).then_inc(zeroed, 1)
                dve.wait_ge(zeroed, 4)
                for what, k, b in start:
                    if what == "x":
                        norm_stats((None, k))
                        norm_rows((None, k))
                    part(what, (None, k), k, b)

            def step(g, p, b, nxt, nxt2):
                one, two = earlier(g, b, 1), earlier(g, b, 2)
                if one:
                    divide(*one)
                take_max(g, b)
                if nxt:
                    part("q", shift(g, 1), 1 - p, b)
                keep_max(g, b)
                if one:
                    output_lo(*one)
                if b == 0 and nxt2:
                    norm_stats(shift(g, 2))
                elif b < GB - 1 and nxt2:
                    norm_rows(shift(g, 2), 2 * (b - 1), 2)
                if b == GB - 1 and nxt2:
                    part("x", shift(g, 2), p, 0)
                if two:
                    residual(*two)
                if nxt:
                    part("k", shift(g, 1), 1 - p, b)

            def finish():
                g = (None, NG - 1)
                residual(g, GB - 2)
                divide(g, GB - 1)
                output_lo(g, GB - 1)
                residual(g, GB - 1)

            walk(dve, begin, step, finish)

        @block.gpsimd
        def _(pool):
            def rows(g):
                pool.wait_ge(ln_agg, lin(g, GB, GB))
                wait(pool, x_norm, lin(g, GB, 0))
                settle(pool, c)
                pool.tensor_scalar(var[:], aggr[:, :, 1], 1.0, LN_EPS, ALU.mult, ALU.add).then_inc(own, 1)
                pool.wait_ge(own, lin(g, 1, 1))
                pool.tensor_tensor(rstd[:], var[:], c["mhalf"][:, 0:GB], ALU.pow).then_inc(ln_rstd, 1)

            rows((None, 0))
            rows((None, 1))
            groups(pool, lambda g, p, nxt, nxt2: rows(shift(g, 2)) if nxt2 else None)


def route(nc, c, S, XH, XL, WR, second):
    W, SM = c["parts"], c["small"]
    E = E1 if second else E0
    tag = "e1" if second else "e0"
    gate = "router" if second else "gate"
    with ExitStack() as ctx:
        def sb(name, shape, dt):
            return ctx.enter_context(nc.sbuf_tensor(f"{tag}r_{name}", shape, dt))

        def sem(name):
            return ctx.enter_context(nc.semaphore(f"{tag}r_{name}"))


        stats, aggr = sb("stats", [P, 2, GB, 6], F32), sb("aggr", [P, 2, GB, 2], F32)
        ms, var, rstd = sb("ms", [P, 2, GB], F32), sb("var", [P, 2, GB], F32), sb("rstd", [P, 2, GB], F32)
        sq = sb("sq", [P, D], F32)
        xn = sb("xn", [P, 2, GB, D], F32)
        LG = sb("LG", [P, NB, E], F32)
        a_, b_, c_ = (sb(k, [P, NB, E], F32) for k in "abc")
        v1, v2, d1, d2 = (sb(k, [P, NB], F32) for k in ("v1", "v2", "d1", "d2"))
        pX = ctx.enter_context(nc.psum_tensor(f"{tag}r_pX", [P, 2, TG], F32))
        pL = ctx.enter_context(nc.psum_tensor(f"{tag}r_pL", [P, 2, 512], F32))
        st, agg, root, rstd_done, rows = sem("st"), sem("agg"), sem("root"), sem("rstd_done"), sem("rows")
        turned, hi_made, lo_made, scored, kept = sem("turned"), sem("hi_made"), sem("lo_made"), sem("scored"), sem("kept")
        picked, asked, exp_done = sem("picked"), sem("asked"), sem("exp_done")
        block = ctx.enter_context(nc.Block())

        def every(engine, step):
            groups(engine, lambda g, p, nxt, nxt2: step(g, p))

        def ahead(engine, early, late):
            early((None, 0), 0)
            groups(engine, lambda g, p, nxt, nxt2: (early(shift(g, 1), 1 - p) if nxt else None, late(g, p)))

        @block.tensor
        def _(pe):
            def turn(g, p):
                pe.wait_ge(rows, lin(g, 1, 1))
                wait(pe, lo_made, lin(g, 1, -1))
                for t in range(GB):
                    mm = pe.transpose(pX[:, p, t * P:(t + 1) * P], xn[:, p, t, :], c["ident"][:])
                mm.then_inc(turned, 1)

            def score(g, p):
                pe.wait_ge(lo_made, lin(g, 1, 1))
                wait(pe, kept, lin(g, 1, -1))
                for t in range(GB):
                    rows_ = bass.ds(lin(g, TG, t * P), P)
                    out = pL[:, p, t * E:(t + 1) * E]
                    mm = product(pe, out, (XH[:, rows_], XL[:, rows_]), W.of(gate, 0, E), last=second)
                    if not second:
                        gh, gl = W.of("gate_b", 0, E)
                        pe.matmul(out, c["row0"][:], gh, start=False, stop=False)
                        mm = pe.matmul(out, c["row0"][:], gl, start=False, stop=True)
                mm.then_inc(scored, 1)

            ahead(pe, turn, score)

        @block.scalar
        def _(act):
            def squares(g, p):
                wait(act, rstd_done, lin(g, 1, -1))
                for t in range(GB):
                    wait(act, agg, lin(g, GB, t))
                    act.activation(sq[:], S[:, bass.ds(lin(g, GB, t), 1), :], ACT.Square,
                                   accum_out=ms[:, p, t:t + 1]).then_inc(agg, 1)

            def hi(g, p):
                act.wait_ge(turned, lin(g, 1, 1))
                out = XH[:, bass.ds(lin(g, TG), TG)]
                if second:
                    act.activation(out, pX[:, p, :], ACT.Copy).then_inc(hi_made, 1)
                else:
                    act.activation(out, pX[:, p, :], ACT.Copy, scale=SM("n2")).then_inc(hi_made, 1)

            if second:
                every(act, hi)
                act.wait_ge(asked, 1)
                act.activation(d2[:], d1[:], ACT.Exp).then_inc(exp_done, 1)
            else:
                ahead(act, squares, hi)

        @block.gpsimd
        def _(pool):
            def roots(g, p):
                pool.wait_ge(agg, lin(g, GB, GB))
                wait(pool, rows, lin(g, 1, -1))
                settle(pool, c)
                src = aggr[:, p, :, 1] if second else ms[:, p, :]
                pool.tensor_scalar(var[:, p, :], src, 1.0 if second else 1.0 / D, LN_EPS if second else RMS_EPS,
                                   ALU.mult, ALU.add).then_inc(root, 1)
                pool.wait_ge(root, lin(g, 1, 1))
                pool.tensor_tensor(rstd[:, p, :], var[:, p, :], c["mhalf"][:, 0:GB], ALU.pow).then_inc(rstd_done, 1)

            every(pool, roots)

        @block.vector
        def _(dve):
            def statistics(g, p):
                for t in range(GB):
                    dve.bn_stats(stats[:, p, t, :], S[:, bass.ds(lin(g, GB, t), 1), :]).then_inc(st, 1)
                for t in range(GB):
                    dve.wait_ge(st, lin(g, GB, t + 1))
                    settle(dve, c)
                    dve.bn_aggr(aggr[:, p, t, :], stats[:, p, t, :]).then_inc(agg, 1)

            def norm(g, p):
                dve.wait_ge(rstd_done, lin(g, 1, 1))
                wait(dve, turned, lin(g, 1, -1))
                for t in range(GB):
                    src, dst = S[:, bass.ds(lin(g, GB, t), 1), :], xn[:, p, t:t + 1, :]
                    if second:
                        ts = dve.tensor_scalar(dst, src, aggr[:, p, t, 0:1], rstd[:, p, t:t + 1], ALU.subtract, ALU.mult)
                    else:
                        ts = dve.tensor_scalar(dst, src, rstd[:, p, t:t + 1], None, ALU.mult)
                ts.then_inc(rows, 1)

            def lo(g, p):
                dve.wait_ge(hi_made, lin(g, 1, 1))
                at = bass.ds(lin(g, TG), TG)
                if second:
                    dve.tensor_tensor(XL[:, at], pX[:, p, :], XH[:, at], ALU.subtract).then_inc(lo_made, 1)
                else:
                    dve.scalar_tensor_tensor(XL[:, at], pX[:, p, :], SM("n2"), XH[:, at], ALU.mult,
                                             ALU.subtract).then_inc(lo_made, 1)

            def keep(g, p):
                dve.wait_ge(scored, lin(g, 1, 1))
                dve.tensor_copy(LG[:, bass.ds(lin(g, GB), GB), :],
                                pL[:, p, :GB * E].rearrange("p (t e) -> p t e", e=E)).then_inc(kept, 1)

            if second:
                statistics((None, 0), 0)
                statistics((None, 1), 1)
            norm((None, 0), 0)

            def step(g, p, nxt, nxt2):
                if second and nxt2:
                    statistics(shift(g, 2), p)
                if nxt:
                    norm(shift(g, 1), 1 - p)
                lo(g, p)
                keep(g, p)

            groups(dve, step)

            chain = [0]

            def then(instruction, upto=picked):
                chain[0] += 1
                instruction.then_inc(picked, 1)
                dve.wait_ge(picked, chain[0])

            def over(v):
                return v[:].rearrange("p (n o) -> p n o", o=1).to_broadcast([P, NB, E])

            def first_max(values, value, onehot, work):
                then(dve.tensor_reduce(out=value[:], in_=values[:], op=ALU.max, axis=AX.X))
                then(dve.tensor_tensor(work[:], values[:], over(value), ALU.is_equal))
                then(dve.tensor_tensor(work[:], work[:], c["first"][:, :, :E].to_broadcast([P, NB, E]), ALU.mult))
                then(dve.tensor_reduce(out=d1[:], in_=work[:], op=ALU.max, axis=AX.X))
                then(dve.tensor_tensor(onehot[:], work[:], over(d1), ALU.is_equal))

            dve.wait_ge(kept, NG)
            if not second:
                first_max(LG, v1, WR, a_)
            else:
                first_max(LG, v1, b_, a_)
                then(dve.scalar_tensor_tensor(LG[:], b_[:], -3.0e38, LG[:], ALU.mult, ALU.add))
                first_max(LG, v2, c_, a_)
                then(dve.tensor_tensor(d1[:], v2[:], v1[:], ALU.subtract))
                dve.sem_inc(asked, 1)
                dve.wait_ge(exp_done, 1)
                then(dve.tensor_scalar(v1[:], d2[:], 1.0, None, ALU.add))
                then(dve.reciprocal(v1[:], v1[:]))
                then(dve.tensor_tensor(v2[:], v1[:], d2[:], ALU.mult))
                then(dve.tensor_tensor(b_[:], b_[:], over(v1), ALU.mult))
                then(dve.tensor_tensor(c_[:], c_[:], over(v2), ALU.mult))
                then(dve.tensor_tensor(WR[:], b_[:], c_[:], ALU.add))


def experts(nc, c, X, XH, XL, WR, second, parts):
    W, SM = c["parts"], c["small"]
    E = E1 if second else E0
    tag = "e1" if second else "e0"
    U, LAG, NU, NA = E * FC, 2, 4, 2
    with ExitStack() as ctx:
        def sem(name):
            return ctx.enter_context(nc.semaphore(f"{tag}x_{name}"))

        gh = ctx.enter_context(nc.sbuf_tensor(f"{tag}_gh", [P, NU, TG], F16))
        gl = ctx.enter_context(nc.sbuf_tensor(f"{tag}_gl", [P, NU, TG], F16))
        g32 = ctx.enter_context(nc.sbuf_tensor(f"{tag}_g32", [P, NA, TG], F32))
        pU = ctx.enter_context(nc.psum_tensor(f"{tag}_pU", [P, NU, TG], F32))
        pY = ctx.enter_context(nc.psum_tensor(f"{tag}_pY", [P, 2, GB, D], F32))
        up, hi, full, lo, down, summed = (sem(k) for k in ("up", "hi", "full", "lo", "down", "summed"))
        block = ctx.enter_context(nc.Block())

        @block.tensor
        def _(pe):
            with pe.Fori(0, NG, 1) as g:
                def raise_(u):
                    e, f = divmod(u, FC)
                    wait(pe, full, g * U + (u - NU + 1) if u >= NU else g * U)
                    toks = bass.ds(g * TG, TG)
                    product(pe, pU[:, u % NU, :], parts(0, e * FF + f * P, P), (XH[:, toks], XL[:, toks])).then_inc(up, 1)

                def lower(u):
                    e, f = divmod(u, FC)
                    pe.wait_ge(lo, g * U + (u + 1))
                    if f == 0:
                        wait(pe, summed, g * E + max(e - 1, 0))
                    for t in range(GB):
                        out = pY[:, e % 2, t, :]
                        ts = slice(t * P, (t + 1) * P)
                        mm = product(pe, out, (gh[:, u % NU, ts], gl[:, u % NU, ts]), parts(1, e * FF + f * D, D),
                                     first=f == 0 and t == 0, last=f == FC - 1 and (second or False), check=False)
                        if f == FC - 1 and not second:
                            bh, bl = W.of("b2", e * D, D)
                            pe.matmul(out, c["row0"][:], bh, start=False, stop=False, skip_group_check=True)
                            mm = pe.matmul(out, c["row0"][:], bl, start=False, stop=True, skip_group_check=True)
                    mm.then_inc(down, 1)

                for u in range(U + LAG):
                    if u < U:
                        raise_(u)
                    if u >= LAG:
                        lower(u - LAG)

        @block.scalar
        def _(act):
            with act.Fori(0, NG, 1) as g:
                for u in range(U):
                    act.wait_ge(up, g * U + (u + 1))
                    if u >= NU:
                        act.wait_ge(down, g * U + (u - NU + 1))
                    else:
                        act.wait_ge(down, g * U) if u == 0 else None
                    f = ACT.Gelu if second else ACT.Relu
                    bias = 0.0 if second else SM("b1", P, u)
                    act.activation(gh[:, u % NU, :], pU[:, u % NU, :], f, bias=bias).then_inc(hi, 1)
                    if u >= NA:
                        act.wait_ge(lo, g * U + (u - NA + 1))
                    act.activation(g32[:, u % NA, :], pU[:, u % NU, :], f, bias=bias).then_inc(full, 1)

        @block.vector
        def _(dve):
            with dve.Fori(0, NG, 1) as g:
                def add(e):
                    dve.wait_ge(down, g * U + (e + 1) * FC)
                    for t in range(GB):
                        n = bass.ds(g * GB + t, 1)
                        last = dve.scalar_tensor_tensor(X[:, n, :], pY[:, e % 2, t:t + 1, :], WR[:, n, e], X[:, n, :],
                                                        ALU.mult, ALU.add)
                    last.then_inc(summed, 1)

                for u in range(U):
                    dve.wait_ge(full, g * U + (u + 1))
                    dve.tensor_tensor(gl[:, u % NU, :], g32[:, u % NA, :], gh[:, u % NU, :], ALU.subtract).then_inc(lo, 1)
                    if u % FC == 1 and u > FC:
                        add(u // FC - 1)
                add(E - 1)


def build(nc, ins, out, stop=99):
    ctx = ExitStack()
    with ctx:
        def sb(name, shape, dt):
            return ctx.enter_context(nc.sbuf_tensor(name, shape, dt))

        X = sb("X", [P, NB, D], F32)
        YW = sb("YW", [P, NB * D], F32)
        Y = YW[:].rearrange("p (n d) -> p n d", n=NB)
        SH, SL = sb("SH", [P, NSPLIT], F16), sb("SL", [P, NSPLIT], F16)
        small = sb("small", [P, NSMALL], F32)
        c = {
            "passed": ctx.enter_context(nc.semaphore("passed")),
            "parts": Parts(SH, SL),
            "small": lambda name, rows=P, k=0: small[:rows, SM_OFF[name] + k:SM_OFF[name] + k + 1],
            "ident": sb("ident", [P, P], F32), "ident16": sb("ident16", [P, P], F16), "id16": sb("identb", [P, P], U16),
            "maskM": sb("maskM", [P, HQ, P], U16), "maskS": sb("maskS", [P, HQ, P], U16),
            "sel": sb("sel", [P, H, P], F16), "row0": sb("row0", [P, P], F16),
            "cos": sb("cos", [P, P], F32), "sin": sb("sin", [P, P], F32), "mhalf": sb("mhalf", [P, 8], F32), "first": sb("first", [P, 1, E1], F32),
        }
        load_all(nc, [(X[:], ins["x"].rearrange("n t d -> t n d")), (small[:], ins["small"])]
                 + [(c[k][:], ins[k]) for k in ("ident", "ident16", "id16", "maskM", "maskS", "sel", "row0", "cos",
                                               "sin", "mhalf", "first")], "first")
        split_columns(nc, ins["split"], NSPLIT, SH, SL)
        narrow_attention(nc, c, X, Y, False)
        if stop > 1:
            narrow_attention(nc, c, X, Y, True)
        def moe(second, S, parts):
            with (nc.sbuf_tensor(f"XH{second}", [P, NB * P], F16) as XH, nc.sbuf_tensor(f"XL{second}", [P, NB * P], F16) as XL,
                  nc.sbuf_tensor(f"WR{second}", [P, NB, E1 if second else E0], F32) as WR):
                route(nc, c, S, XH, XL, WR, second)
                experts(nc, c, X, XH, XL, WR, second, parts)
        if stop > 2:
            moe(False, Y, lambda k, a, n: c["parts"].of(("w1a", "w2a")[k], a, n))
        if stop > 3:
            wide_attention(nc, c, X)
        if stop > 4:
            late = YW[:].bitcast(F16)
            split_columns(nc, ins["late"], NLATE, late[:, :NLATE], late[:, NLATE:])
            moe(True, X, lambda k, a, n: (late[:, k * E1 * FF + a:k * E1 * FF + a + n],
                                          late[:, NLATE + k * E1 * FF + a:NLATE + k * E1 * FF + a + n]))
        with nc.semaphore("stored") as stored, nc.Block() as block:
            @block.sync
            def _(sp):
                sp.dma_start(out.rearrange("n t d -> t n d"), X[:]).then_inc(stored, 16)
                sp.wait_ge(stored, 16)


def shape_constants():
    f = np.float32
    b16 = lambda m: (np.ascontiguousarray(m, f).view(np.uint32) >> 16).astype(np.uint16)
    i = np.arange(P)
    sel = np.zeros((P, H, P), np.float16)
    sel[np.arange(H), np.arange(H), :] = SHIFT
    row0 = np.zeros((P, P), np.float16)
    row0[0] = 1
    maskM = np.where(i[None, :] > i[:, None], f(-1e30), f(0))
    half = HD // 2
    freq = f(1.0) / f(10000.0) ** (np.arange(half, dtype=f) / f(half))
    ang = i.astype(f)[None, :] * freq[:, None]
    d = (i % 32) // 4
    cos, sin = np.cos(ang).astype(f)[d % half], np.sin(ang).astype(f)[d % half]
    sin = np.where((d < half)[:, None], -sin, sin)
    tile4 = lambda m: b16(np.broadcast_to(m[:, None, :], (P, HQ, P)))
    return {"ident": np.eye(P, dtype=f), "ident16": np.eye(P, dtype=np.float16), "id16": b16(np.eye(P)),
            "maskM": tile4(maskM), "maskS": tile4(maskM.T), "sel": sel, "row0": row0,
            "cos": cos.astype(f), "sin": sin.astype(f), "mhalf": np.full((P, 8), -0.5, f),
            "first": np.ascontiguousarray(np.broadcast_to(f(E1) - np.arange(E1, dtype=f), (P, 1, E1)))}


def lay_out(a):
    f = np.float32
    r = np.arange(D)
    row_head, row_dim = HQ * (r % 4) + r // 32, (r % 32) // 4
    perm = row_head * HD + row_dim
    swap = row_head * HD + (row_dim + HD // 2) % HD
    full = lambda m: np.pad(m, ((0, P - m.shape[0]), (0, 0)))
    row = lambda v: full(v.reshape(1, -1))
    up = lambda w: w.transpose(2, 0, 1).reshape(D, -1)
    down = lambda w: w.reshape(w.shape[0], D, FC, P).transpose(3, 0, 2, 1).reshape(P, -1)
    cols = {
        "ctx": a["ctx_1024"].transpose(2, 0, 1).reshape(D, -1),
        "a_q": a["L0_xattn_Wq"][:, perm], "a_k": a["L0_xattn_Wk"][:, perm], "a_v": a["L0_xattn_Wv"],
        "a_o": a["L0_xattn_Wo"], "a_bo": row(a["L0_xattn_bo"]),
        "m_q": a["L0_ffn_Wq"].T[:, perm], "m_qs": a["L0_ffn_Wq"].T[:, swap], "m_kv": a["L0_ffn_Wdkv"].T,
        "m_k": full(a["L0_ffn_Wuk"].T[:, perm]), "m_ks": full(a["L0_ffn_Wuk"].T[:, swap]),
        "m_v": full(a["L0_ffn_Wuv"].T), "m_o": a["L0_ffn_Wo"].T,
        "w_q": a["L1_xattn_Wq"], "w_k": a["L1_xattn_Wk"], "w_v": a["L1_xattn_Wv"],
        "w_o": a["L1_xattn_Wo"].reshape(FC, P, D).transpose(1, 0, 2).reshape(P, -1), "w_bo": row(a["L1_xattn_bo"]),
        "gate": a["L0_ffn_gate_w"].T, "gate_b": row(a["L0_ffn_gate_b"]), "router": a["L1_ffn_router_w"].T,
        "b2": row(a["L0_ffn_b2"]), "w1a": up(a["L0_ffn_W1"]), "w2a": down(a["L0_ffn_W2"]),
    }
    split = np.zeros((P, NSPLIT), f)
    for name, width in SPLIT_COLS:
        split[:, OFF[name]:OFF[name] + width] = cols[name]
    late = np.concatenate([up(a["L1_ffn_expert_w1"]), down(a["L1_ffn_expert_w2"])], axis=1)
    small = np.zeros((P, NSMALL), f)
    for name, v in (("bq", a["L0_xattn_bq"][perm]), ("bk", a["L0_xattn_bk"][perm]), ("bv", a["L0_xattn_bv"]),
                    ("n1", a["L0_ffn_norm1_w"]), ("n2", a["L0_ffn_norm2_w"]), ("lg", a["L0_ffn_ln_g"]),
                    ("lb", a["L0_ffn_ln_b"])):
        small[:len(v), SM_OFF[name]] = v
    small[:, SM_OFF["b1"]:] = a["L0_ffn_b1"].reshape(E0 * FC, P).T
    return {"x": a["x"], "split": split, "late": np.ascontiguousarray(late), "small": small}


def kernel(**inputs):
    import concourse.bacc as bacc
    from concourse.bass_utils import run_bass_kernel_spmd

    a = {k: np.asarray(v) for k, v in inputs.items()}
    arrays = {f"in_{k}": np.ascontiguousarray(v) for k, v in (lay_out(a) | shape_constants()).items()}
    nc = bacc.Bacc("TRN2", target_bir_lowering=False, num_devices=1)
    ins = {k[3:]: nc.dram_tensor(k, v.shape, mybir.dt.from_np(v.dtype), kind="ExternalInput").ap()
           for k, v in arrays.items()}
    out = nc.dram_tensor("out", a["x"].shape, F32, kind="ExternalOutput").ap()
    build(nc, ins, out)
    return run_bass_kernel_spmd(nc, [arrays], core_ids=[0]).results[0]["out"]
```

```python
import numpy as np
from contextlib import ExitStack

import concourse.bass as bass
from concourse import mybir

F32 = mybir.dt.float32
F16 = mybir.dt.float16
BF16 = mybir.dt.bfloat16
U16 = mybir.dt.uint16
ALU = mybir.AluOpType
ACT = mybir.ActivationFunctionType
AX = mybir.AxisListType

P = 128
D = 128
NB = 64
KC = 77
GB = 4
NG = NB // GB
TG = GB * P
H = 16
HD = D // H
HQ = 4
WH_ = 8
WD = 64
WHID = WH_ * WD
LAT = 64
FF = 512
FC = FF // P
E0, E1 = 4, 8
SHIFT = 64.0
LN_EPS, RMS_EPS = 1e-5, 1e-6

SPLIT_COLS = [
    ("ctx", NB * KC),
    ("a_q", D), ("a_k", D), ("a_v", D), ("a_o", D), ("a_bo", D),
    ("m_q", D), ("m_qs", D), ("m_kv", LAT), ("m_k", D), ("m_ks", D), ("m_v", D), ("m_o", D),
    ("w_q", WHID), ("w_k", WHID), ("w_v", WHID), ("w_o", WHID), ("w_bo", D),
    ("gate", E0), ("gate_b", E0), ("router", E1), ("b2", E0 * D),
    ("w1a", E0 * FF), ("w2a", E0 * FF),
]
OFF, _n = {}, 0
for _name, _w in SPLIT_COLS:
    OFF[_name] = _n
    _n += _w
CH = 1024
NSPLIT = -(-_n // CH) * CH
NLATE = 2 * E1 * FF
SMALL = ["bq", "bk", "bv", "n1", "n2", "lg", "lb", "b1"]
CONSTANTS = ["ident", "ident16", "id16", "maskM", "maskS", "sel", "row0", "cos", "sin", "mhalf", "euler", "zero",
             "first"]
SM_OFF = {name: k for k, name in enumerate(SMALL)}
NSMALL = len(SMALL) - 1 + E0 * FC


def lin(g, mult, add=0):
    i, c = g
    return mult * c + add if i is None else i * (2 * mult) + (mult * c + add)


def shift(g, by):
    return g[0], g[1] + by


def is_first(g):
    return g[0] is None and g[1] == 0


def wait(engine, semaphore, value):
    if isinstance(value, int) and value <= 0:
        return
    engine.wait_ge(semaphore, value)


def settle(engine, c):
    engine.sem_inc(c["passed"], 1)


def groups(engine, body):
    for c in (0, 1):
        body((None, c), c, True, True)
    with engine.Fori(1, NG // 2 - 1, 1) as i:
        for c in (0, 1):
            body((i, c), c, True, True)
    body((None, NG - 2), 0, True, False)
    body((None, NG - 1), 1, False, False)


class Parts:

    def __init__(self, hi, lo):
        self.hi, self.lo = hi, lo

    def of(self, name, start, width, rows=P):
        a = OFF[name] + start
        return self.hi[:rows, bass.ds(a, width)], self.lo[:rows, bass.ds(a, width)]


def product(pe, out, left, right, first=True, last=True, check=True):
    (lh, ll), (rh, rl) = left, right
    kw = {} if check else {"skip_group_check": True}
    pe.matmul(out, lh, rh, start=first, stop=False, **kw)
    pe.matmul(out, lh, rl, start=False, stop=False, **kw)
    return pe.matmul(out, ll, rh, start=False, stop=last, **kw)


def load_and_split(nc, c, src, pairs):
    n, STAGES = NSPLIT // CH, 4
    hi, lo = c["parts"].hi, c["parts"].lo
    with ExitStack() as ctx:
        stage = ctx.enter_context(nc.sbuf_tensor("stage", [P, STAGES, CH], F32))
        loaded = [ctx.enter_context(nc.semaphore(f"loaded{k}")) for k in range(STAGES)]
        hi_done, lo_done = ctx.enter_context(nc.semaphore("hi_done")), ctx.enter_context(nc.semaphore("lo_done"))
        whole, zeroed = ctx.enter_context(nc.semaphore("whole")), ctx.enter_context(nc.semaphore("operands_zeroed"))
        block = ctx.enter_context(nc.Block())

        @block.sync
        def _(sp):
            for k in range(n):
                wait(sp, lo_done, k - STAGES + 1)
                sp.dma_start(stage[:, k % STAGES, :], src[:, k * CH:(k + 1) * CH]).then_inc(loaded[k % STAGES], 16)
            for dst, source in pairs:
                sp.dma_start(dst, source).then_inc(whole, 16)
            sp.wait_ge(whole, 16 * len(pairs))

        @block.scalar
        def _(act):
            for k in range(n):
                act.wait_ge(loaded[k % STAGES], 16 * (k // STAGES + 1))
                act.activation(hi[:, k * CH:(k + 1) * CH], stage[:, k % STAGES, :], ACT.Copy).then_inc(hi_done, 1)

        @block.vector
        def _(dve):
            dve.memset(c["Ks"][:].bitcast(F32), 0.0).then_inc(zeroed, 1)
            dve.memset(c["mT"][:].bitcast(F32), 0.0).then_inc(zeroed, 1)
            for k in range(n):
                dve.wait_ge(hi_done, k + 1)
                dve.tensor_tensor(lo[:, k * CH:(k + 1) * CH], stage[:, k % STAGES, :], hi[:, k * CH:(k + 1) * CH],
                                  ALU.subtract).then_inc(lo_done, 1)
            dve.memset(c["V"][:], 1.0).then_inc(zeroed, 1)
            dve.wait_ge(zeroed, 5)

        @block.gpsimd
        def _(pool):
            pool.memset(c["Qd"][:, 0].bitcast(F32), 0.0).then_inc(zeroed, 1)
            pool.memset(c["Qd"][:, 1].bitcast(F32), 0.0).then_inc(zeroed, 1)


def narrow_attention(nc, c, X, Y, latent):
    W, SM = c["parts"], c["small"]
    NK = P if latent else KC
    tag = "m" if latent else "a"
    USES = 8 if latent else 4
    POOL_QUERIES, POOL_KEYS = (range(1), range(1)) if latent else (range(0), range(HQ // 2))
    N_POOL = 3 * (len(POOL_QUERIES) + len(POOL_KEYS))
    N_SYNC = 3 * 2 * HQ - N_POOL
    with ExitStack() as ctx:
        def sb(name, shape, dt):
            return ctx.enter_context(nc.sbuf_tensor(f"{tag}_{name}", shape, dt))

        def pb(name, shape, dt=F32):
            return ctx.enter_context(nc.psum_tensor(f"{tag}_{name}", shape, dt))

        def sem(name):
            return ctx.enter_context(nc.semaphore(f"{tag}_{name}"))

        Qd, Ks, V, mT = c["Qd"], c["Ks"], c["V"], c["mT"]
        qh, ql = sb("qh", [P, TG], F16), sb("ql", [P, TG], F16)
        kh, kl = sb("kh", [P, GB * NK], F16), sb("kl", [P, GB * NK], F16)
        stats, aggr = sb("stats", [P, GB, 6], F32), sb("aggr", [P, GB, 2], F32)
        var, rstd = sb("var", [P, GB], F32), sb("rstd", [P, GB], F32)
        xn = sb("xn", [P, GB, D], F32)
        xh, xl = sb("xh", [P, TG], F16), sb("xl", [P, TG], F16)
        mx = sb("mx", [P, H], F32)
        ng = sb("ng", [P, H], F16)
        PT = sb("PT", [P, 2, H, P], F32)
        Os = sb("Os", [P, HQ, P], F32)
        rec = sb("rec", [P, H], F32)
        On = sb("On", [P, D], F32)
        oh, ol = sb("oh", [P, P], F16), sb("ol", [P, P], F16)
        if latent:
            sq, ms = sb("sq", [P, D], F32), sb("ms", [P, GB], F32)
            rv, rr = sb("rv", [P, GB], F32), sb("rr", [P, GB], F32)
            t1, t2 = sb("t1", [P, 2, TG], F32), sb("t2", [P, 2, TG], F32)
            lstats, laggr = sb("lstats", [P, GB, 6], F32), sb("laggr", [P, GB, 2], F32)
            lvar, lrstd = sb("lvar", [P, GB], F32), sb("lrstd", [P, GB], F32)
            latn = xn[:, :, 0:LAT]
            lt = xn[0:LAT, :, :].rearrange("p b d -> p (b d)")
            lh, ll = sb("lh", [LAT, TG], F16), sb("ll", [LAT, TG], F16)

        pM = pb("pM", [P, H // 2, P])
        pS = pb("pS", [P, H // 2, P])
        pV = pb("pV", [P, HQ, P])
        pO = pb("pO", [P, 512])
        pP = pb("pP", [P, 512])
        pT = pb("pT", [P, 512])
        pTh = pT[:, 0:P // 2].bitcast(F16)

        zeroed, x_norm, ln_agg, ln_rstd = sem("zeroed"), sem("x_norm"), sem("ln_agg"), sem("ln_rstd")
        ln_st = sem("ln_st")
        sq_done, ms_done, rms_r = sem("sq_done"), sem("ms_done"), sem("rms_r")
        used, hi_made, evac = sem("used"), sem("hi_made"), sem("evac")
        rope_sum, rope_lo = sem("rope_sum"), sem("rope_lo")
        lat_st, lat_agg, lat_rstd, lat_lo = sem("lat_st"), sem("lat_agg"), sem("lat_rstd"), sem("lat_lo")
        sync_sent = sem("sync_sent")
        pool_sent = sem("pool_sent")
        m_ready, m_max, neg, mt_ready, mt_kept = (sem("m_ready"), sem("m_max"), sem("neg"), sem("mt_ready"),
                                                  sem("mt_kept"))
        s_ready, exp_done, pv_ready, os_kept = sem("s_ready"), sem("exp_done"), sem("pv_ready"), sem("os_kept")
        t1_ready, rec_done, on_done, t2_ready = sem("t1_ready"), sem("rec_done"), sem("on_done"), sem("t2_ready")
        oh_done, ol_done, wo_ready, res_done = sem("oh_done"), sem("ol_done"), sem("wo_ready"), sem("res_done")
        own = sem("own")
        block = ctx.enter_context(nc.Block())

        if latent:
            order = ["q", "qs", "k", "ks", "v", "x", "lat", "latT"]
            first_use = 3
        else:
            order = ["q", "k", "v", "x"]
            first_use = 1

        def use(g, what):
            back = 1 if what in ("x", "lat", "latT") else 0
            return lin(g, USES, first_use + order.index(what) - back * USES)

        if latent:
            slots = {(0, 0): "q", (0, 1): "qs", (1, 0): "k", (1, 1): "ks", (2, 0): "v", (2, 1): "x",
                     (3, 0): "lat", (3, 1): "latT"}
        else:
            slots = {(0, 0): "q", (0, 1): "k", (1, 0): "v", (2, 0): "x"}

        def slot(b, half, g, nxt, nxt2):
            what = slots.get((b, half))
            if what in ("x", "lat", "latT"):
                return (what, shift(g, 2), 2) if nxt2 else (None, None, 0)
            return (what, shift(g, 1), 1) if what and nxt else (None, None, 0)

        start_x = ["x", "lat", "latT"] if latent else ["x"]
        start = ([(w, 0) for w in start_x] + [(w, 0) for w in order if w not in start_x]
                 + [(w, 1) for w in start_x])

        def earlier(g, b, by):
            if b >= by:
                return g, b - by
            return None if is_first(g) else (shift(g, -1), b - by + GB)

        def walk(engine, begin, step, finish):
            begin()
            groups(engine, lambda g, p, nxt, nxt2: [step(g, p, b, nxt, nxt2) for b in range(GB)])
            finish()

        def hi_count(g, what):
            per = [w for w in order if w in (("x", "qs", "ks", "latT") if latent else ("x", "q", "k"))]
            lead = 2 if latent else 1
            back = 1 if what in ("x", "latT") else 0
            return lin(g, len(per), lead + per.index(what) + 1 - back * len(per))

        def stacked(engine, g):
            wait(engine, sync_sent, lin(g, 16 * N_SYNC, 0))
            wait(engine, pool_sent, lin(g, 16 * N_POOL, 0))

        def stack(engine, g, p, what, sent):
            if what == "q":
                engine.wait_ge(rope_lo, lin(g, 2, 1)) if latent else engine.wait_ge(evac, use(g, "q") + 1)
            else:
                engine.wait_ge(rope_lo, lin(g, 2, 2)) if latent else engine.wait_ge(evac, use(g, "k") + 1)
            settle(engine, c)
            wait(engine, s_ready, lin(g, 2 * GB, -2 * GB))
            settle(engine, c)
            by_pool = POOL_QUERIES if what == "q" else POOL_KEYS
            for j in (by_pool if sent is pool_sent else range(len(by_pool), HQ)):
                for r in range(3):
                    if what == "q":
                        src = (qh, qh, ql)[r]
                        dst = Qd[32 * j + HD * r:32 * j + HD * (r + 1), p, :, j, :]
                    else:
                        src = (kh, kl, kh)[r]
                        dst = Ks[32 * j + HD * r:32 * j + HD * (r + 1), p, :, :GB * NK]
                    engine.dma_start(dst, src[32 * j:32 * j + 32, :]).then_inc(sent, 16)

        @block.tensor
        def _(pe):
            pe.wait_ge(zeroed, 3)

            def project(what, g, p):
                u = use(g, what)
                wait(pe, evac, u)
                if what == "x":
                    pe.wait_ge(rms_r if latent else x_norm, lin(g, GB, GB))
                    for b in range(GB):
                        mm = pe.transpose(pP[:, b * P:(b + 1) * P], xn[:, b, :], c["ident"][:])
                elif what in ("q", "qs"):
                    wait(pe, evac, use(g, "x") + 1)
                    mm = product(pe, pP[:, :TG], W.of(f"{tag}_{what}", 0, D), (xh[:], xl[:]))
                elif what in ("k", "ks") and not latent:
                    mm = product(pe, pP[:, :GB * KC], W.of("a_k", 0, D), W.of("ctx", lin(g, GB * KC), GB * KC))
                elif what in ("k", "ks"):
                    pe.wait_ge(lat_lo, lin(g, 1, 1))
                    mm = product(pe, pP[:, :TG], W.of(f"m_{what}", 0, D, LAT), (lh[:], ll[:]))
                elif what == "v":
                    for b in range(GB):
                        if latent:
                            s = slice(b * P, (b + 1) * P)
                            mm = product(pe, pP[:, s], (lh[:, s], ll[:, s]), W.of("m_v", 0, D, LAT))
                        else:
                            mm = product(pe, pP[:KC, b * P:(b + 1) * P], W.of("ctx", lin(g, GB * KC, b * KC), KC),
                                         W.of("a_v", 0, D))
                elif what == "lat":
                    wait(pe, evac, use(g, "x") + 1)
                    for b in range(GB):
                        s = slice(b * P, (b + 1) * P)
                        mm = product(pe, pP[:, b * LAT:(b + 1) * LAT], (xh[:, s], xl[:, s]), W.of("m_kv", 0, LAT))
                elif what == "latT":
                    settle(pe, c)
                    for b in range(GB):
                        mm = pe.transpose(pP[:LAT, b * P:(b + 1) * P], latn[:, b, :], c["ident"][:])
                mm.then_inc(used, 1)

            def maxima(p, b, half, g):
                wait(pe, m_max, lin(g, 2 * GB, 2 * b + half))
                if b == 0 and half == 0:
                    stacked(pe, shift(g, 1))
                for gg in range(2):
                    hg = 2 * half + gg
                    if latent:
                        pe.matmul(pM[:, 4 * gg:4 * gg + 4, :], c["id16"][:].bitcast(BF16),
                                  c["maskM"][:].bitcast(BF16), start=True, stop=False, skip_group_check=True)
                    for j in range(HQ):
                        mm = pe.matmul(pM[:, 4 * gg + j, :NK], Qd[:, p, hg, j, b * P:(b + 1) * P],
                                       Ks[:, p, hg, b * NK:(b + 1) * NK], start=not latent, stop=True,
                                       skip_group_check=True)
                mm.then_inc(m_ready, 1)

            def max_transpose(g, p, b):
                pe.wait_ge(neg, lin(g, GB, b + 1))
                pe.transpose(pTh[:H, :], ng[:], c["ident16"][:]).then_inc(mt_ready, 1)

            def scores(g, p, b, half):
                wait(pe, exp_done, lin(g, 2 * GB, 2 * b + half))
                if half == 0:
                    pe.wait_ge(mt_kept, lin(g, GB, b + 1))
                for gg in range(2):
                    hg = 2 * half + gg
                    pe.matmul(pS[:NK, 4 * gg:4 * gg + 4, :], Ks[:, p, hg, b * NK:(b + 1) * NK],
                              Qd[:, p, hg, :, b * P:(b + 1) * P], start=True, stop=False, skip_group_check=True)
                    if latent:
                        pe.matmul(pS[:, 4 * gg:4 * gg + 4, :], c["id16"][:].bitcast(BF16),
                                  c["maskS"][:].bitcast(BF16), start=False, stop=False, skip_group_check=True)
                    for j in range(HQ):
                        mm = pe.matmul(pS[:NK, 4 * gg + j, :], c["sel"][:, HQ * hg + j, :NK], mT[:, b % 2, :],
                                       start=False, stop=(j == HQ - 1), skip_group_check=True)
                mm.then_inc(s_ready, 1)

            def values(g, p, b):
                wait(pe, exp_done, lin(g, 2 * GB, 2 * b + 2))
                wait(pe, os_kept, lin(g, GB, b))
                if b == 0:
                    pe.wait_ge(evac, use(g, "v") + 1)
                for hg in range(HQ):
                    for j in range(HQ):
                        h = HQ * hg + j
                        mm = pe.matmul(pV[32 * j:32 * j + HD + 1, hg, :], V[:NK, p, b, h, :], PT[:NK, b % 2, h, :],
                                       start=True, stop=True)
                mm.then_inc(pv_ready, 1)

            def turn_heads(g, b):
                pe.wait_ge(os_kept, lin(g, GB, b + 1))
                wait(pe, res_done, lin(g, GB, b))
                for hg in range(HQ):
                    mm = pe.transpose(pO[:, hg * P:(hg + 1) * P], Os[:, hg, :], c["ident"][:])
                mm.then_inc(t1_ready, 1)

            def turn_output(g, b):
                pe.wait_ge(on_done, lin(g, GB, b + 1))
                pe.transpose(pO[:, :P], On[:], c["ident"][:]).then_inc(t2_ready, 1)

            def project_output(g, b):
                pe.wait_ge(oh_done, lin(g, GB, b + 1))
                pe.wait_ge(ol_done, lin(g, GB, b + 1))
                if latent:
                    mm = product(pe, pO[:, :D], (oh[:], ol[:]), W.of("m_o", 0, D))
                else:
                    product(pe, pO[:, :D], (oh[:], ol[:]), W.of("a_o", 0, D), last=False)
                    bh, bl = W.of("a_bo", 0, D)
                    pe.matmul(pO[:, :D], c["row0"][:], bh, start=False, stop=False)
                    mm = pe.matmul(pO[:, :D], c["row0"][:], bl, start=False, stop=True)
                mm.then_inc(wo_ready, 1)

            def begin():
                for what, k in start:
                    project(what, (None, k), k)
                maxima(0, 0, 0, (None, 0))
                maxima(0, 0, 1, (None, 0))

            def step(g, p, b, nxt, nxt2):
                gn, pn, bn = (g, p, b + 1) if b < GB - 1 else (shift(g, 1), 1 - p, 0)
                gp, pp, bp = (g, p, b - 1) if b else (shift(g, -1), 1 - p, GB - 1)
                more = nxt or b < GB - 1
                before = b > 0 or not is_first(g)
                two = earlier(g, b, 2)
                max_transpose(g, p, b)
                what, gw, far = slot(b, 0, g, nxt, nxt2)
                if what:
                    project(what, gw, None)
                if more:
                    maxima(pn, bn, 0, gn)
                if two:
                    turn_output(*two)
                scores(g, p, b, 0)
                if two:
                    project_output(*two)
                if before:
                    values(gp, pp, bp)
                if more:
                    maxima(pn, bn, 1, gn)
                what, gw, far = slot(b, 1, g, nxt, nxt2)
                if what:
                    project(what, gw, None)
                scores(g, p, b, 1)
                if before:
                    turn_heads(gp, bp)

            def finish():
                g = (None, NG - 1)
                turn_output(g, GB - 2)
                project_output(g, GB - 2)
                values(g, 1, GB - 1)
                turn_heads(g, GB - 1)
                turn_output(g, GB - 1)
                project_output(g, GB - 1)

            walk(pe, begin, step, finish)

        @block.scalar
        def _(act):
            def part(what, g):
                u = use(g, what)
                if what == "x":
                    act.wait_ge(used, u + 1)
                    if latent:
                        act.activation(xh[:], pP[:, :TG], ACT.Copy, scale=SM("n1")).then_inc(hi_made, 1)
                    else:
                        act.activation(xh[:], pP[:, :TG], ACT.Copy).then_inc(hi_made, 1)
                elif what in ("q", "k") and not latent:
                    dst, n = (qh, TG) if what == "q" else (kh, GB * KC)
                    act.wait_ge(used, u + 1)
                    stacked(act, g)
                    act.activation(dst[:, :n], pP[:, :n], ACT.Identity, bias=SM("b" + what)).then_inc(hi_made, 1)
                elif what in ("qs", "ks"):
                    dst = qh if what == "qs" else kh
                    stacked(act, g)
                    act.wait_ge(rope_sum, lin(g, 2, 1 if what == "qs" else 2))
                    act.activation(dst[:], t1[:, int(what == "ks"), :], ACT.Copy).then_inc(hi_made, 1)
                elif what == "latT":
                    act.wait_ge(evac, u + 1)
                    act.activation(lh[:], lt, ACT.Copy).then_inc(hi_made, 1)

            def squares(g):
                for b in range(GB):
                    act.wait_ge(x_norm, lin(g, GB, b + 1))
                    wait(act, ms_done, lin(g, 1, 0))
                    wait(act, sq_done, lin(g, GB, b))
                    act.activation(sq[:], Y[:, bass.ds(lin(g, GB, b), 1), :], ACT.Square,
                                   accum_out=ms[:, b:b + 1]).then_inc(sq_done, 1)

            def exps(g, p, b, half):
                act.wait_ge(s_ready, lin(g, 2 * GB, 2 * b + half + 1))
                if half == 0:
                    wait(act, pv_ready, lin(g, GB, b - 1))
                act.activation(PT[:NK, b % 2, 8 * half:8 * half + 8, :], pS[:NK, :, :], ACT.Exp,
                               scale=float(1.0 / np.sqrt(HD))).then_inc(exp_done, 1)

            def keep_heads(g, b):
                act.wait_ge(pv_ready, lin(g, GB, b + 1))
                wait(act, t1_ready, lin(g, GB, b))
                act.activation(Os[:], pV[:], ACT.Copy).then_inc(os_kept, 1)

            def output_hi(g, b):
                act.wait_ge(t2_ready, lin(g, GB, b + 1))
                wait(act, wo_ready, lin(g, GB, b))
                if latent:
                    act.activation(oh[:], pO[:, :P], ACT.Copy).then_inc(oh_done, 1)
                else:
                    act.activation(oh[:], pO[:, :P], ACT.Identity, bias=SM("bv")).then_inc(oh_done, 1)

            def begin():
                act.wait_ge(zeroed, 3)
                if latent:
                    squares((None, 0))
                for what, k in start:
                    if latent and what == "x" and k == 1:
                        squares((None, 1))
                    part(what, (None, k))

            def step(g, p, b, nxt, nxt2):
                one, two = earlier(g, b, 1), earlier(g, b, 2)
                what, gw, far = slot(b, 0, g, nxt, nxt2)
                if what:
                    part(what, gw)
                if two:
                    output_hi(*two)
                exps(g, p, b, 0)
                if one:
                    keep_heads(*one)
                if latent and b == 1 and nxt2:
                    squares(shift(g, 2))
                what, gw, far = slot(b, 1, g, nxt, nxt2)
                late = what in ("qs", "ks")
                if what and not late:
                    part(what, gw)
                exps(g, p, b, 1)
                if late:
                    part(what, gw)

            def finish():
                g = (None, NG - 1)
                output_hi(g, GB - 2)
                keep_heads(g, GB - 1)
                output_hi(g, GB - 1)

            walk(act, begin, step, finish)

        @block.vector
        def _(dve):
            def norm_stats(g):
                for b in range(GB):
                    dve.bn_stats(stats[:, b, :], X[:, bass.ds(lin(g, GB, b), 1), :]).then_inc(ln_st, 1)
                for b in range(GB):
                    dve.wait_ge(ln_st, lin(g, GB, b + 1))
                    if b == 0:
                        wait(dve, ln_rstd, lin(g, 1, 0))
                        wait(dve, x_norm, lin(g, GB, 0))
                    settle(dve, c)
                    dve.bn_aggr(aggr[:, b, :], stats[:, b, :]).then_inc(ln_agg, 1)

            def norm_rows(g):
                dve.wait_ge(ln_rstd, lin(g, 1, 1))
                if not latent:
                    wait(dve, used, use(g, "x") - USES + 1)
                for b in range(GB):
                    n = bass.ds(lin(g, GB, b), 1)
                    dst = Y[:, n, :] if latent else xn[:, b:b + 1, :]
                    dve.tensor_scalar(dst, X[:, n, :], aggr[:, b, 0:1], rstd[:, b:b + 1], ALU.subtract,
                                      ALU.mult).then_inc(x_norm, 1)

            def rms_rows(g):
                dve.wait_ge(ms_done, lin(g, 1, 1))
                if not is_first(g):
                    dve.wait_ge(lat_lo, lin(g, 1, 0))
                for b in range(GB):
                    dve.tensor_scalar(xn[:, b:b + 1, :], Y[:, bass.ds(lin(g, GB, b), 1), :], rr[:, b:b + 1], None,
                                      ALU.mult).then_inc(rms_r, 1)

            def part(what, g, p):
                u = use(g, what)
                if what == "x":
                    dve.wait_ge(hi_made, hi_count(g, what))
                    if latent:
                        dve.scalar_tensor_tensor(xl[:], pP[:, :TG], SM("n1"), xh[:], ALU.mult,
                                                 ALU.subtract).then_inc(evac, 1)
                    else:
                        dve.tensor_tensor(xl[:], pP[:, :TG], xh[:], ALU.subtract).then_inc(evac, 1)
                elif what in ("q", "k") and not latent:
                    hi, lo, n = (qh, ql, TG) if what == "q" else (kh, kl, GB * KC)
                    dve.wait_ge(hi_made, hi_count(g, what))
                    dve.scalar_tensor_tensor(lo[:, :n], pP[:, :n], SM("b" + what), hi[:, :n], ALU.add,
                                             ALU.subtract).then_inc(evac, 1)
                elif what in ("q", "qs", "k", "ks"):
                    dve.wait_ge(used, u + 1)
                    if what in ("q", "k"):
                        wait(dve, rope_lo, lin(g, 2, -1 if what == "q" else 0))
                    dst, table = (t1, "cos") if what in ("q", "k") else (t2, "sin")
                    dve.tensor_tensor(dst[:, int(what in ("k", "ks")), :].rearrange("p (b t) -> p b t", b=GB),
                                      pP[:, :TG].rearrange("p (b t) -> p b t", b=GB),
                                      c[table][:].rearrange("p (o t) -> p o t", o=1).to_broadcast([P, GB, P]),
                                      ALU.mult).then_inc(evac, 1)
                elif what == "v":
                    dve.wait_ge(used, u + 1)
                    wait(dve, pv_ready, lin(g, GB, -GB))
                    for b in range(GB):
                        cp = dve.tensor_copy(V[:NK, p, b, :, 0:HD],
                                             pP[:NK, b * P:(b + 1) * P].rearrange("k (h d) -> k h d", h=H))
                    cp.then_inc(evac, 1)
                elif what == "lat":
                    dve.wait_ge(used, u + 1)
                    for b in range(GB):
                        dve.bn_stats(lstats[:, b, :], pP[:, b * LAT:(b + 1) * LAT]).then_inc(lat_st, 1)
                    for b in range(GB):
                        dve.wait_ge(lat_st, lin(g, GB, b + 1))
                        settle(dve, c)
                        dve.bn_aggr(laggr[:, b, :], lstats[:, b, :]).then_inc(lat_agg, 1)
                    dve.wait_ge(lat_rstd, lin(g, 1, 1))
                    for b in range(GB):
                        ts = dve.tensor_scalar(latn[:, b, :], pP[:, b * LAT:(b + 1) * LAT], laggr[:, b, 0:1],
                                               lrstd[:, b:b + 1], ALU.subtract, ALU.mult)
                    ts.then_inc(evac, 1)
                elif what == "latT":
                    dve.wait_ge(used, u + 1)
                    wait(dve, lat_lo, lin(g, 1, 0))
                    dve.tensor_scalar(lt, pP[:LAT, :TG], SM("lg", LAT), SM("lb", LAT), ALU.mult,
                                      ALU.add).then_inc(evac, 1)

            def take_max(g, b, half):
                dve.wait_ge(m_ready, lin(g, 2 * GB, 2 * b + half + 1))
                if half == 0:
                    wait(dve, neg, lin(g, GB, b))
                dve.tensor_reduce(out=mx[:, 8 * half:8 * half + 8], in_=pM[:, :, :NK], op=ALU.max,
                                  axis=AX.X).then_inc(m_max, 1)

            def negate(g, b):
                dve.wait_ge(m_max, lin(g, 2 * GB, 2 * b + 2))
                wait(dve, mt_ready, lin(g, GB, b))
                dve.tensor_scalar(ng[:], mx[:], -1.0 / SHIFT, None, ALU.mult).then_inc(neg, 1)

            def keep_max(g, b):
                dve.wait_ge(mt_ready, lin(g, GB, b + 1))
                wait(dve, s_ready, lin(g, 2 * GB, 2 * (b - 1)))
                dve.tensor_copy(mT[:H, b % 2, :], pTh[:H, :]).then_inc(mt_kept, 1)

            def divide(g, b):
                dve.wait_ge(t1_ready, lin(g, GB, b + 1))
                wait(dve, on_done, lin(g, GB, b))
                dve.reciprocal(rec[:].rearrange("p (h o) -> p h o", o=1),
                               pO[:].rearrange("p (h c) -> p h c", h=H)[:, :, HD:HD + 1]).then_inc(rec_done, 1)
                dve.wait_ge(rec_done, lin(g, GB, b + 1))
                wait(dve, t2_ready, lin(g, GB, b))
                dve.tensor_tensor(On[:].rearrange("p (h d) -> p h d", h=H),
                                  pO[:].rearrange("p (h c) -> p h c", h=H)[:, :, 0:HD],
                                  rec[:].rearrange("p (h o) -> p h o", o=1).to_broadcast([P, H, HD]),
                                  ALU.mult).then_inc(on_done, 1)

            def output_lo(g, b):
                dve.wait_ge(oh_done, lin(g, GB, b + 1))
                if latent:
                    dve.tensor_tensor(ol[:], pO[:, :P], oh[:], ALU.subtract).then_inc(ol_done, 1)
                else:
                    dve.scalar_tensor_tensor(ol[:], pO[:, :P], SM("bv"), oh[:], ALU.add,
                                             ALU.subtract).then_inc(ol_done, 1)

            def residual(g, b):
                n = bass.ds(lin(g, GB, b), 1)
                dve.wait_ge(wo_ready, lin(g, GB, b + 1))
                R = Y if latent else X
                dve.tensor_tensor(R[:, n, :], pO[:, :D].rearrange("p (o d) -> p o d", o=1), R[:, n, :],
                                  ALU.add).then_inc(res_done, 1)

            def begin():
                dve.memset(pV[:], 0.0).then_inc(zeroed, 1)
                dve.memset(mx[:], 0.0).then_inc(zeroed, 1)
                dve.memset(var[:], 0.0).then_inc(zeroed, 1)
                dve.wait_ge(zeroed, 3)
                for what, k in start:
                    if what == "x":
                        norm_stats((None, k))
                        norm_rows((None, k))
                        if latent:
                            rms_rows((None, k))
                    part(what, (None, k), k)
                take_max((None, 0), 0, 0)
                take_max((None, 0), 0, 1)
                negate((None, 0), 0)

            def step(g, p, b, nxt, nxt2):
                gn, pn, bn = (g, p, b + 1) if b < GB - 1 else (shift(g, 1), 1 - p, 0)
                gp, pp, bp = (g, p, b - 1) if b else (shift(g, -1), 1 - p, GB - 1)
                more = nxt or b < GB - 1
                before = b > 0 or not is_first(g)
                two = earlier(g, b, 2)
                keep_max(g, b)
                what, gw, far = slot(b, 0, g, nxt, nxt2)
                if what:
                    part(what, gw, (p + far) % 2)
                if two:
                    output_lo(*two)
                if more:
                    take_max(gn, bn, 0)
                if two:
                    residual(*two)
                if b == 0 and nxt2:
                    norm_stats(shift(g, 2))
                if b == 1 and nxt2:
                    norm_rows(shift(g, 2))
                if latent and b == 2 and nxt2:
                    rms_rows(shift(g, 2))
                if more:
                    take_max(gn, bn, 1)
                    negate(gn, bn)
                what, gw, far = slot(b, 1, g, nxt, nxt2)
                if what:
                    part(what, gw, (p + far) % 2)
                if before:
                    divide(gp, bp)

            def finish():
                g = (None, NG - 1)
                output_lo(g, GB - 2)
                residual(g, GB - 2)
                divide(g, GB - 1)
                output_lo(g, GB - 1)
                residual(g, GB - 1)

            walk(dve, begin, step, finish)

        @block.gpsimd
        def _(pool):

            def root(g, src_ready, value, src, out, mult, eps, tmp, done):
                src_ready()
                settle(pool, c)
                pool.tensor_scalar(tmp, src, mult, eps, ALU.mult, ALU.add).then_inc(own, 1)
                pool.wait_ge(own, value)
                pool.tensor_tensor(out, tmp, c["mhalf"][:, 0:GB], ALU.pow).then_inc(done, 1)

            per = 3 if latent else 1

            def rows(g):
                wait(pool, x_norm, lin(g, GB, 0))
                root(g, lambda: pool.wait_ge(ln_agg, lin(g, GB, GB)), row_root(g), aggr[:, :, 1], rstd[:],
                     1.0, LN_EPS, var[:], ln_rstd)

            def row_root(g):
                return lin(g, per, 1) if not latent else own_count(g, "rows")

            def own_count(g, what):
                return lin(g, 3, {"rows": 1, "squares": 2, "lat": 3}[what])

            def squares(g):
                root(g, lambda: pool.wait_ge(sq_done, lin(g, GB, GB)), own_count(g, "squares"), ms[:], rr[:],
                     1.0 / D, RMS_EPS, rv[:], ms_done)

            def latents(g):
                root(g, lambda: pool.wait_ge(lat_agg, lin(g, GB, GB)), own_count(g, "lat"), laggr[:, :, 1], lrstd[:],
                     1.0, LN_EPS, lvar[:], lat_rstd)

            def rope(what, g):
                if what in ("qs", "ks"):
                    k = 0 if what == "qs" else 1
                    hi, lo = (qh, ql) if what == "qs" else (kh, kl)
                    pool.wait_ge(evac, use(g, what) + 1)
                    pool.tensor_tensor(t1[:, k, :], t1[:, k, :], t2[:, k, :], ALU.add).then_inc(rope_sum, 1)
                    pool.wait_ge(rope_sum, lin(g, 2, 1 + k))
                    pool.wait_ge(hi_made, hi_count(g, what))
                    stacked(pool, g)
                    pool.tensor_tensor(lo[:], t1[:, k, :], hi[:], ALU.subtract).then_inc(rope_lo, 1)
                elif what == "latT":
                    pool.wait_ge(evac, use(g, what) + 1)
                    pool.wait_ge(hi_made, hi_count(g, what))
                    pool.tensor_tensor(ll[:], lt, lh[:], ALU.subtract).then_inc(lat_lo, 1)
                elif what == "lat":
                    latents(g)

            def begin():
                for what, k in start:
                    if what == "x":
                        rows((None, k))
                        squares((None, k))
                    rope(what, (None, k))
                    if k == 0 and what in ("qs", "ks"):
                        stack(pool, (None, 0), 0, what[0], pool_sent)

            def step(g, p, b, nxt, nxt2):
                if b == 0 and nxt2:
                    rows(shift(g, 2))
                for half_ in (0, 1):
                    what, gw, far = slot(b, half_, g, nxt, nxt2)
                    if what:
                        rope(what, gw)
                if b == 0 and nxt:
                    stack(pool, shift(g, 1), 1 - p, "q", pool_sent)
                if b == 1 and nxt2:
                    squares(shift(g, 2))
                if b == 1 and nxt:
                    stack(pool, shift(g, 1), 1 - p, "k", pool_sent)

            pool.wait_ge(zeroed, 3)
            if latent:
                walk(pool, begin, step, lambda: None)
            else:
                rows((None, 0))
                rows((None, 1))
                stack(pool, (None, 0), 0, "k", pool_sent)

                def ahead(g, p, nxt, nxt2):
                    if nxt2:
                        rows(shift(g, 2))
                    if nxt:
                        stack(pool, shift(g, 1), 1 - p, "k", pool_sent)

                groups(pool, ahead)

        @block.sync
        def _(sp):
            sp.wait_ge(zeroed, 3)

            def begin():
                stack(sp, (None, 0), 0, "q", sync_sent)
                stack(sp, (None, 0), 0, "k", sync_sent)

            def step(g, p, b, nxt, nxt2):
                if b == 0 and nxt:
                    stack(sp, shift(g, 1), 1 - p, "q", sync_sent)
                    stack(sp, shift(g, 1), 1 - p, "k", sync_sent)

            walk(sp, begin, step, lambda: None)


def wide_attention(nc, c, X, late, late_hi, late_lo):
    CL = NLATE // NG
    W = c["parts"]
    HB = WH_ // 2
    with ExitStack() as ctx:
        def sb(name, shape, dt):
            return ctx.enter_context(nc.sbuf_tensor(f"w_{name}", shape, dt))

        def pb(name, shape, dt=F32):
            return ctx.enter_context(nc.psum_tensor(f"w_{name}", shape, dt))

        def sem(name):
            return ctx.enter_context(nc.semaphore(f"w_{name}"))

        stage = sb("stage", [P, CL], F32)
        late_loaded, late_hi_done, late_lo_done = sem("late_loaded"), sem("late_hi_done"), sem("late_lo_done")
        stats, aggr = sb("stats", [P, GB, 6], F32), sb("aggr", [P, GB, 2], F32)
        var, rstd = sb("var", [P, GB], F32), sb("rstd", [P, GB], F32)
        xn = sb("xn", [P, GB, D], F32)
        xh, xl = sb("xh", [P, TG], F16), sb("xl", [P, TG], F16)
        Qh, Ql = sb("Qh", [P, 2, HB, TG], F16), sb("Ql", [P, 2, HB, TG], F16)
        Kh, Kl = sb("Kh", [P, 2, HB, 2, GB * KC], F16), sb("Kl", [P, 2, HB, 2, GB * KC], F16)
        V = sb("V", [P, 2, WH_, WD + 1], F32)
        mx = sb("mx", [P, WH_], F32)
        ng = sb("ng", [P, WH_], F16)
        mT = sb("mT", [P, 2, P], F16)
        PT = sb("PT", [P, 2, WH_, P], F32)
        rec, O = sb("rec", [P, 2, HB, 1], F32), sb("O", [P, WHID], F32)
        oh, ol = sb("oh", [P, 2, HB, P], F16), sb("ol", [P, 2, HB, P], F16)

        pM = pb("pM", [P, WH_, P])
        pS = pb("pS", [P, WH_, P])
        pV = pb("pV", [P, 2, 512])
        heads_out = pV[:, :, :HB * (WD + 1)].rearrange("p b (h d) -> p b h d", d=WD + 1)
        pP = pb("pP", [P, 512])
        pT = pb("pT", [P, 512])

        zeroed, x_norm, ln_st, ln_agg, ln_rstd = (sem("zeroed"), sem("x_norm"), sem("ln_st"), sem("ln_agg"),
                                                  sem("ln_rstd"))
        own, used, hi_made, evac = sem("own"), sem("used"), sem("hi_made"), sem("evac")
        v_kept = sem("v_kept")
        m_ready, m_max, neg, mt_ready, mt_kept = (sem("m_ready"), sem("m_max"), sem("neg"), sem("mt_ready"),
                                                  sem("mt_kept"))
        s_ready, exp_done, pv_ready, rec_done, o_done = (sem("s_ready"), sem("exp_done"), sem("pv_ready"),
                                                         sem("rec_done"), sem("o_done"))
        o_turned = sem("o_turned")
        oh_done, ol_done, wo_ready, res_done = sem("oh_done"), sem("ol_done"), sem("wo_ready"), sem("res_done")
        block = ctx.enter_context(nc.Block())

        LEAD, USES = 2 + 2 * HB, 3 * GB + 1
        KEPT = 2 * GB + 1

        def is_start(g, what):
            return g[0] is None and (what == "x" and g[1] < 2 or what in "qk" and g[1] == 0)

        def is_last(g):
            return g[0] is None and g[1] == NG - 1

        def x_before_k(g, b):
            return int(b == GB - 1 and not is_last(g))

        def use(g, what, b=0):
            if is_start(g, what):
                return {"x": 0 if g[1] == 0 else LEAD - 1, "q": 1 + 2 * b, "k": 2 + 2 * b}[what]
            if what == "x":
                return lin(g, USES, LEAD - 2 * USES + 3 * GB - 1)
            if what == "v":
                return LEAD + USES * (NG - 1) - 1 + b if is_last(g) else lin(g, USES, LEAD + 3 * b + 1)
            if what == "q":
                return lin(g, USES, LEAD - USES + 3 * b)
            return lin(g, USES, LEAD - USES + 3 * b + 2 + x_before_k(g, b))

        def values_before(g, what, b):
            if is_start(g, what):
                return 0
            if what == "x":
                return lin(g, GB, -GB)
            return lin(g, GB, {"q": b - GB, "v": b, "k": b - GB + 1}[what])

        def by_vector(g, what, b=0):
            if is_start(g, what):
                return use(g, what, b) + 1
            if what == "x":
                return lin(g, KEPT, LEAD - 2 * KEPT + 2 * GB)
            if what == "v":
                return LEAD + KEPT * (NG - 1) - 1 if is_last(g) else lin(g, KEPT, LEAD + 2 * b + 1)
            if what == "q":
                return lin(g, KEPT, LEAD - KEPT + 2 * b + 1)
            return lin(g, KEPT, LEAD - KEPT + 2 * b + 2 + x_before_k(g, b))

        def earlier(g, b, by):
            if b >= by:
                return g, b - by
            return None if is_first(g) else (shift(g, -1), b - by + GB)

        def walk(engine, begin, step, finish):
            begin()
            groups(engine, lambda g, p, nxt, nxt2: [step(g, p, b, nxt, nxt2) for b in range(GB)])
            finish()

        start = [("x", 0, 0)] + [(w, 0, b) for b in range(HB) for w in "qk"] + [("x", 1, 0)]

        @block.tensor
        def _(pe):

            def project(what, g, b):
                wait(pe, evac, by_vector(g, what, b) - (what != "v"))
                wait(pe, v_kept, values_before(g, what, b))
                if what == "x":
                    pe.wait_ge(x_norm, lin(g, GB, GB))
                    for t in range(GB):
                        mm = pe.transpose(pP[:, t * P:(t + 1) * P], xn[:, t, :], c["ident"][:])
                elif what == "q":
                    wait(pe, evac, by_vector(g, "x"))
                    mm = product(pe, pP[:, :TG], W.of("w_q", b * P, P), (xh[:], xl[:]))
                elif what == "k":
                    mm = product(pe, pP[:, :GB * KC], W.of("w_k", b * P, P), W.of("ctx", lin(g, GB * KC), GB * KC))
                else:
                    mm = product(pe, pP[:KC, :], W.of("ctx", lin(g, GB * KC, b * KC), KC), W.of("w_v", 0, WHID))
                mm.then_inc(used, 1)

            def maxima(g, p, b):
                wait(pe, m_max, lin(g, GB, b))
                if b == 0:
                    pe.wait_ge(evac, by_vector(g, "k", HB - 1))
                for k in range(HB):
                    mm = pe.matmul(pM[:, 2 * k:2 * k + 2, :KC], Qh[:, p, k, b * P:(b + 1) * P],
                                   Kh[:, p, k, :, b * KC:(b + 1) * KC], start=True, stop=True)
                mm.then_inc(m_ready, 1)

            def max_transpose(g, b):
                pe.wait_ge(neg, lin(g, GB, b + 1))
                wait(pe, res_done, lin(g, GB, b - 2))
                pe.transpose(pT[:, :P // 2].bitcast(F16)[:WH_, :], ng[:], c["ident16"][:]).then_inc(mt_ready, 1)

            def scores(g, p, b):
                wait(pe, exp_done, lin(g, GB, b))
                q, k = slice(b * P, (b + 1) * P), slice(b * KC, (b + 1) * KC)
                for h in range(WH_):
                    product(pe, pS[:KC, h, :], (Kh[:, p, h // 2, h % 2, k], Kl[:, p, h // 2, h % 2, k]),
                            (Qh[:, p, h // 2, q], Ql[:, p, h // 2, q]), first=h % HB == 0, last=False, check=False)

            def shift_scores(g, b):
                pe.wait_ge(mt_kept, lin(g, GB, b + 1))
                for h in range(WH_):
                    mm = pe.matmul(pS[:KC, h, :], c["sel"][:, h, :KC], mT[:, b % 2, :],
                                   start=False, stop=h % HB == HB - 1, skip_group_check=True)
                mm.then_inc(s_ready, 1)

            def values(g, b):
                pe.wait_ge(exp_done, lin(g, GB, b + 1))
                wait(pe, ol_done, lin(g, GB, b))
                pe.wait_ge(v_kept, lin(g, GB, b + 1))
                for h in range(WH_):
                    mm = pe.matmul(heads_out[:, h // HB, h % HB, :], PT[:KC, b % 2, h, :], V[:KC, b % 2, h, :],
                                   start=True, stop=True)
                mm.then_inc(pv_ready, 1)

            def turn_output(g, b):
                pe.wait_ge(o_done, lin(g, GB, b + 1))
                for k in range(HB):
                    mm = pe.transpose(pV[:, 1, k * P:(k + 1) * P], O[:, k * P:(k + 1) * P], c["ident"][:])
                mm.then_inc(o_turned, 1)

            def project_output(g, b, maxima_before):
                pe.wait_ge(oh_done, lin(g, GB, b + 1))
                pe.wait_ge(ol_done, lin(g, GB, b + 1))
                pe.wait_ge(mt_kept, maxima_before)
                wait(pe, res_done, lin(g, GB, b))
                for k in range(HB):
                    product(pe, pT[:, :D], (oh[:, b % 2, k, :], ol[:, b % 2, k, :]), W.of("w_o", k * D, D),
                            first=k == 0, last=False)
                bh, bl = W.of("w_bo", 0, D)
                pe.matmul(pT[:, :D], c["row0"][:], bh, start=False, stop=False)
                pe.matmul(pT[:, :D], c["row0"][:], bl, start=False, stop=True).then_inc(wo_ready, 1)

            def begin():
                for what, k, b in start:
                    project(what, (None, k), b)
                pe.wait_ge(zeroed, 4)

            def step(g, p, b, nxt, nxt2):
                one, two = earlier(g, b, 1), earlier(g, b, 2)
                if one:
                    values(*one)
                maxima(g, p, b)
                if nxt:
                    project("q", shift(g, 1), b)
                scores(g, p, b)
                if one:
                    turn_output(*one)
                max_transpose(g, b)
                project("v", g, b)
                shift_scores(g, b)
                if b == GB - 1 and nxt2:
                    project("x", shift(g, 2), 0)
                if two:
                    project_output(*two, lin(g, GB, b + 1))
                if nxt:
                    project("k", shift(g, 1), b)

            def finish():
                g = (None, NG - 1)
                project_output(g, GB - 2, NB)
                values(g, GB - 1)
                turn_output(g, GB - 1)
                project_output(g, GB - 1, NB)

            walk(pe, begin, step, finish)

        @block.scalar
        def _(act):
            def part(what, g, p, b):
                act.wait_ge(used, use(g, what, b) + 1)
                if what == "x":
                    act.activation(xh[:], pP[:, :TG], ACT.Copy).then_inc(hi_made, 1)
                elif what == "q":
                    act.activation(Qh[:, p, b, :], pP[:, :TG], ACT.Copy).then_inc(hi_made, 1)
                elif what == "k":
                    act.activation(Kh[:WD, p, b, 0, :], pP[:WD, :GB * KC], ACT.Copy)
                    act.activation(Kh[WD:, p, b, 1, :], pP[WD:, :GB * KC], ACT.Copy).then_inc(hi_made, 1)
                else:
                    wait(act, pv_ready, lin(g, GB, b - 1))
                    act.activation(V[:KC, b % 2, :, :WD], pP[:KC, :].rearrange("k (h d) -> k h d", h=WH_),
                                   ACT.Copy).then_inc(v_kept, 1)

            def exps(g, b):
                act.wait_ge(s_ready, lin(g, GB, b + 1))
                wait(act, pv_ready, lin(g, GB, b - 1))
                act.activation(PT[:KC, b % 2, :, :], pS[:KC], ACT.Exp,
                               scale=float(WD) ** -0.5).then_inc(exp_done, 1)

            def output_hi(g, b):
                act.wait_ge(o_turned, lin(g, GB, b + 1))
                wait(act, wo_ready, lin(g, GB, b - 1))
                act.activation(oh[:, b % 2].rearrange("p k t -> p (k t)"), pV[:, 1, :], ACT.Copy).then_inc(oh_done, 1)

            def begin():
                for what, k, b in start:
                    if (what, b) == ("k", 0):
                        act.wait_ge(zeroed, 4)
                    part(what, (None, k), k, b)

            def step(g, p, b, nxt, nxt2):
                one = earlier(g, b, 1)
                if nxt:
                    part("q", shift(g, 1), 1 - p, b)
                if one:
                    output_hi(*one)
                part("v", g, p, b)
                exps(g, b)
                if b == GB - 1 and nxt2:
                    part("x", shift(g, 2), p, 0)
                if nxt:
                    part("k", shift(g, 1), 1 - p, b)

            walk(act, begin, step, lambda: output_hi((None, NG - 1), GB - 1))

        @block.vector
        def _(dve):
            def norm_stats(g, start=0, count=GB):
                for b in range(start, start + count):
                    dve.bn_stats(stats[:, b, :], X[:, bass.ds(lin(g, GB, b), 1), :]).then_inc(ln_st, 1)
                for b in range(start, start + count):
                    dve.wait_ge(ln_st, lin(g, GB, b + 1))
                    settle(dve, c)
                    dve.bn_aggr(aggr[:, b, :], stats[:, b, :]).then_inc(ln_agg, 1)

            def norm_rows(g, start=0, count=GB):
                dve.wait_ge(ln_rstd, lin(g, 1, 1))
                if not is_first(g):
                    dve.wait_ge(used, use(shift(g, -1), "x") + 1)
                for b in range(start, start + count):
                    dve.tensor_scalar(xn[:, b:b + 1, :], X[:, bass.ds(lin(g, GB, b), 1), :], aggr[:, b, 0:1],
                                      rstd[:, b:b + 1], ALU.subtract, ALU.mult).then_inc(x_norm, 1)

            def part(what, g, p, b):
                dve.wait_ge(hi_made, by_vector(g, what, b))
                if what == "x":
                    dve.tensor_tensor(xl[:], pP[:, :TG], xh[:], ALU.subtract).then_inc(evac, 1)
                elif what == "q":
                    dve.tensor_tensor(Ql[:, p, b, :], pP[:, :TG], Qh[:, p, b, :], ALU.subtract).then_inc(evac, 1)
                else:
                    for o in range(2):
                        half = slice(WD * o, WD * (o + 1))
                        tt = dve.tensor_tensor(Kl[half, p, b, o, :], pP[half, :GB * KC], Kh[half, p, b, o, :],
                                               ALU.subtract)
                    tt.then_inc(evac, 1)

            def take_max(g, b):
                dve.wait_ge(m_ready, lin(g, GB, b + 1))
                wait(dve, neg, lin(g, GB, b))
                dve.tensor_reduce(out=mx[:], in_=pM[:, :, :KC], op=ALU.max,
                                  axis=AX.X).then_inc(m_max, 1)
                dve.wait_ge(m_max, lin(g, GB, b + 1))
                wait(dve, mt_ready, lin(g, GB, b))
                dve.tensor_scalar(ng[:], mx[:], -1.0 / SHIFT, None, ALU.mult).then_inc(neg, 1)

            def keep_max(g, b):
                dve.wait_ge(mt_ready, lin(g, GB, b + 1))
                wait(dve, s_ready, lin(g, GB, b - 1))
                dve.tensor_copy(mT[:WH_, b % 2, :], pT[:, :P // 2].bitcast(F16)[:WH_, :]).then_inc(mt_kept, 1)

            def divide(g, b):
                dve.wait_ge(pv_ready, lin(g, GB, b + 1))
                dve.reciprocal(rec[:], heads_out[:, :, :, WD:]).then_inc(rec_done, 1)
                dve.wait_ge(rec_done, lin(g, GB, b + 1))
                wait(dve, o_turned, lin(g, GB, b))
                dve.tensor_tensor(O[:].rearrange("p (b h d) -> p b h d", b=2, h=HB), heads_out[:, :, :, :WD],
                                  rec[:].to_broadcast([P, 2, HB, WD]), ALU.mult).then_inc(o_done, 1)

            def output_lo(g, b):
                dve.wait_ge(oh_done, lin(g, GB, b + 1))
                dve.tensor_tensor(ol[:, b % 2].rearrange("p k t -> p (k t)"), pV[:, 1, :],
                                  oh[:, b % 2].rearrange("p k t -> p (k t)"), ALU.subtract).then_inc(ol_done, 1)

            def residual(g, b):
                n = bass.ds(lin(g, GB, b), 1)
                dve.wait_ge(wo_ready, lin(g, GB, b + 1))
                dve.tensor_tensor(X[:, n, :], pT[:, :D].rearrange("p (o d) -> p o d", o=1), X[:, n, :],
                                  ALU.add).then_inc(res_done, 1)

            def begin():
                dve.memset(mT[:].bitcast(F32), 0.0).then_inc(zeroed, 1)
                dve.memset(V[:], 1.0).then_inc(zeroed, 1)
                for what, k, b in start:
                    if what == "x":
                        norm_stats((None, k))
                        norm_rows((None, k))
                    if (what, b) == ("k", 0):
                        dve.wait_ge(zeroed, 4)
                    part(what, (None, k), k, b)

            def step(g, p, b, nxt, nxt2):
                one, two = earlier(g, b, 1), earlier(g, b, 2)
                if one:
                    divide(*one)
                take_max(g, b)
                if nxt:
                    part("q", shift(g, 1), 1 - p, b)
                keep_max(g, b)
                if one:
                    output_lo(*one)
                if b == 0 and nxt2:
                    norm_stats(shift(g, 2))
                elif b < GB - 1 and nxt2:
                    norm_rows(shift(g, 2), 2 * (b - 1), 2)
                if b == GB - 1 and nxt2:
                    part("x", shift(g, 2), p, 0)
                if two:
                    residual(*two)
                if nxt:
                    part("k", shift(g, 1), 1 - p, b)

            def finish():
                g = (None, NG - 1)
                residual(g, GB - 2)
                divide(g, GB - 1)
                output_lo(g, GB - 1)
                residual(g, GB - 1)

            walk(dve, begin, step, finish)

        @block.gpsimd
        def _(pool):
            def rows(g):
                pool.wait_ge(ln_agg, lin(g, GB, GB))
                wait(pool, x_norm, lin(g, GB, 0))
                settle(pool, c)
                pool.tensor_scalar(var[:], aggr[:, :, 1], 1.0, LN_EPS, ALU.mult, ALU.add).then_inc(own, 1)
                pool.wait_ge(own, lin(g, 1, 1))
                pool.tensor_tensor(rstd[:], var[:], c["mhalf"][:, 0:GB], ALU.pow).then_inc(ln_rstd, 1)

            def split_late(g):
                cols = bass.ds(lin(g, CL), CL)
                pool.wait_ge(late_loaded, lin(g, 16, 16))
                pool.tensor_tensor(late_hi[:, cols], stage[:], c["zero"][:].to_broadcast([P, CL]),
                                   ALU.add).then_inc(late_hi_done, 1)
                pool.wait_ge(late_hi_done, lin(g, 1, 1))
                pool.tensor_tensor(late_lo[:, cols], stage[:], late_hi[:, cols],
                                   ALU.subtract).then_inc(late_lo_done, 1)

            pool.memset(Kh[:].bitcast(F32), 0.0).then_inc(zeroed, 1)
            rows((None, 0))
            pool.memset(Kl[:].bitcast(F32), 0.0).then_inc(zeroed, 1)
            rows((None, 1))
            groups(pool, lambda g, p, nxt, nxt2: (rows(shift(g, 2)) if nxt2 else None, split_late(g)))
            pool.wait_ge(late_lo_done, NG)

        @block.sync
        def _(sp):
            def load_late(g, p, nxt, nxt2):
                wait(sp, late_lo_done, lin(g, 1, 0))
                sp.dma_start(stage[:], late[:, bass.ds(lin(g, CL), CL)]).then_inc(late_loaded, 16)

            groups(sp, load_late)
            sp.wait_ge(late_loaded, 16 * NG)


STATS_AT, NORM_AT, TURN_AT, SPLIT_AT, SCORE_AT, PICK_AT = 0, 6, 7, 9, 10, 13


def mixture(nc, c, X, S, second, parts, out=None):
    W, SM = c["parts"], c["small"]
    E = E1 if second else E0
    tag = "e1" if second else "e0"
    gate = "router" if second else "gate"
    U, LAG, NU, NA = E * FC, 2, 4, 2
    PICKS = 19 if second else 5
    DIFFERENCE = 12
    with ExitStack() as ctx:
        def sb(name, shape, dt):
            return ctx.enter_context(nc.sbuf_tensor(f"{tag}_{name}", shape, dt))

        def pb(name, shape):
            return ctx.enter_context(nc.psum_tensor(f"{tag}_{name}", shape, F32))

        def sem(name):
            return ctx.enter_context(nc.semaphore(f"{tag}_{name}"))

        XH, XL = sb("XH", [P, NB * P], F16), sb("XL", [P, NB * P], F16)
        WR = sb("WR", [P, NB, E], F32)
        stats, aggr = sb("stats", [P, GB, 6], F32), sb("aggr", [P, GB, 2], F32)
        ms, var, rstd = sb("ms", [P, GB], F32), sb("var", [P, GB], F32), sb("rstd", [P, GB], F32)
        sq, xn = sb("sq", [P, D], F32), sb("xn", [P, GB, D], F32)
        logits, marked = sb("logits", [P, GB, E], F32), sb("marked", [P, GB, E], F32)
        is_first_, is_second = sb("is_first", [P, GB, E], F32), sb("is_second", [P, GB, E], F32)
        v1, v2, d1, d2 = (sb(k, [P, GB], F32) for k in ("v1", "v2", "d1", "d2"))
        gh, gl, g32 = sb("gh", [P, NU, TG], F16), sb("gl", [P, NU, TG], F16), sb("g32", [P, NA, TG], F32)
        pU, pY = pb("pU", [P, NU, TG]), pb("pY", [P, 2, GB, D])
        pX, pL = pb("pX", [P, TG]), pb("pL", [P, 512])
        st, agg, root, rstd_done, rows = sem("st"), sem("agg"), sem("root"), sem("rstd_done"), sem("rows")
        turned, hi_made, lo_made = sem("turned"), sem("hi_made"), sem("lo_made")
        scored, kept = sem("scored"), sem("kept")
        picked, exp_done, joined, stored = sem("picked"), sem("exp_done"), sem("joined"), sem("stored")
        up, hi, full, lo, down, summed = (sem(k) for k in ("up", "hi", "full", "lo", "down", "summed"))
        block = ctx.enter_context(nc.Block())

        def every(engine, body):
            body(0, True)
            with engine.Fori(1, NG - 1, 1) as g:
                body(g, True)
            body(NG - 1, False)

        @block.tensor
        def _(pe):
            def turn(r):
                pe.wait_ge(rows, r + 1)
                wait(pe, lo_made, r)
                for t in range(GB):
                    mm = pe.transpose(pX[:, t * P:(t + 1) * P], xn[:, t, :], c["ident"][:])
                mm.then_inc(turned, 1)

            def score(r):
                pe.wait_ge(lo_made, r + 1)
                wait(pe, kept, r)
                for t in range(GB):
                    toks = bass.ds(r * TG + t * P, P)
                    out = pL[:, t * E:(t + 1) * E]
                    mm = product(pe, out, (XH[:, toks], XL[:, toks]), W.of(gate, 0, E), last=second)
                    if not second:
                        bh, bl = W.of("gate_b", 0, E)
                        pe.matmul(out, c["row0"][:], bh, start=False, stop=False)
                        mm = pe.matmul(out, c["row0"][:], bl, start=False, stop=True)
                mm.then_inc(scored, 1)

            def raise_(g, u):
                e, f = divmod(u, FC)
                wait(pe, full, g * U + (u - NU + 1))
                toks = bass.ds(g * TG, TG)
                product(pe, pU[:, u % NU, :], parts(0, e * FF + f * P, P), (XH[:, toks], XL[:, toks])).then_inc(up, 1)

            def lower(g, u):
                e, f = divmod(u, FC)
                pe.wait_ge(lo, g * U + (u + 1))
                if f == 0:
                    wait(pe, summed, g * E + (e - 1))
                for t in range(GB):
                    out = pY[:, e % 2, t, :]
                    ts = slice(t * P, (t + 1) * P)
                    mm = product(pe, out, (gh[:, u % NU, ts], gl[:, u % NU, ts]), parts(1, e * FF + f * D, D),
                                 first=f == 0 and t == 0, last=f == FC - 1 and second, check=False)
                    if f == FC - 1 and not second:
                        bh, bl = W.of("b2", e * D, D)
                        pe.matmul(out, c["row0"][:], bh, start=False, stop=False, skip_group_check=True)
                        mm = pe.matmul(out, c["row0"][:], bl, start=False, stop=True, skip_group_check=True)
                mm.then_inc(down, 1)

            def group(g, nxt):
                for u in range(U):
                    if u + LAG < U:
                        raise_(g, u + LAG)
                    elif nxt:
                        raise_(g + 1, u + LAG - U)
                    lower(g, u)
                    if nxt and u == TURN_AT:
                        turn(g + 1)
                    if nxt and u == SCORE_AT:
                        score(g + 1)

            turn(0)
            score(0)
            for u in range(LAG):
                raise_(0, u)
            every(pe, group)

        @block.scalar
        def _(act):
            def squares(r, t):
                wait(act, rstd_done, r)
                wait(act, agg, r * GB + t)
                act.activation(sq[:], S[:, bass.ds(r * GB + t, 1), :], ACT.Square,
                               accum_out=ms[:, t:t + 1]).then_inc(agg, 1)

            def split(r):
                act.wait_ge(turned, r + 1)
                scale = {} if second else {"scale": SM("n2")}
                act.activation(XH[:, bass.ds(r * TG, TG)], pX[:], ACT.Copy, **scale).then_inc(hi_made, 1)

            def unit(g, u):
                act.wait_ge(up, g * U + (u + 1))
                wait(act, down, g * U + (u - NU + 1))
                f = ACT.Gelu if second else ACT.Relu
                bias = 0.0 if second else SM("b1", P, u)
                act.activation(gh[:, u % NU, :], pU[:, u % NU, :], f, bias=bias).then_inc(hi, 1)
                wait(act, lo, g * U + (u - NA + 1))
                act.activation(g32[:, u % NA, :], pU[:, u % NU, :], f, bias=bias).then_inc(full, 1)

            def group(g, nxt):
                for u in range(U):
                    unit(g, u)
                    if nxt and 0 <= u - STATS_AT < GB and not second:
                        squares(g + 1, u - STATS_AT)
                    if nxt and u == SPLIT_AT:
                        split(g + 1)

            for t in range(0 if second else GB):
                squares(0, t)
            split(0)
            every(act, group)

        @block.gpsimd
        def _(pool):
            def roots(r):
                pool.wait_ge(agg, (r + 1) * GB)
                wait(pool, rows, r)
                settle(pool, c)
                src = aggr[:, :, 1] if second else ms[:]
                pool.tensor_scalar(var[:], src, 1.0 if second else 1.0 / D, LN_EPS if second else RMS_EPS,
                                   ALU.mult, ALU.add).then_inc(root, 1)
                pool.wait_ge(root, r + 1)
                pool.tensor_tensor(rstd[:], var[:], c["mhalf"][:, 0:GB], ALU.pow).then_inc(rstd_done, 1)
                if second:
                    pool.wait_ge(picked, r * PICKS + DIFFERENCE)
                    pool.tensor_tensor(d2[:], c["euler"][:, 0:GB], d1[:], ALU.pow).then_inc(exp_done, 1)

            roots(0)
            every(pool, lambda g, nxt: roots(g + 1) if nxt else None)

        @block.vector
        def _(dve):
            def statistics(r, t):
                dve.bn_stats(stats[:, t, :], S[:, bass.ds(r * GB + t, 1), :]).then_inc(st, 1)
                dve.wait_ge(st, r * GB + (t + 1))
                settle(dve, c)
                dve.bn_aggr(aggr[:, t, :], stats[:, t, :]).then_inc(agg, 1)

            def norm(r):
                dve.wait_ge(rstd_done, r + 1)
                wait(dve, turned, r)
                for t in range(GB):
                    src, dst = S[:, bass.ds(r * GB + t, 1), :], xn[:, t:t + 1, :]
                    if second:
                        ts = dve.tensor_scalar(dst, src, aggr[:, t, 0:1], rstd[:, t:t + 1], ALU.subtract, ALU.mult)
                    else:
                        ts = dve.tensor_scalar(dst, src, rstd[:, t:t + 1], None, ALU.mult)
                ts.then_inc(rows, 1)

            def split(r):
                dve.wait_ge(hi_made, r + 1)
                at = bass.ds(r * TG, TG)
                if second:
                    dve.tensor_tensor(XL[:, at], pX[:], XH[:, at], ALU.subtract).then_inc(lo_made, 1)
                else:
                    dve.scalar_tensor_tensor(XL[:, at], pX[:], SM("n2"), XH[:, at], ALU.mult,
                                             ALU.subtract).then_inc(lo_made, 1)

            def keep(r):
                dve.wait_ge(scored, r + 1)
                dve.tensor_copy(logits[:], pL[:, :GB * E].rearrange("p (t e) -> p t e", e=E)).then_inc(kept, 1)
                dve.wait_ge(kept, r + 1)

            def then(instruction, r, k):
                instruction.then_inc(picked, 1)
                dve.wait_ge(picked, r * PICKS + k)

            def over(v):
                return v[:].rearrange("p (n o) -> p n o", o=1).to_broadcast([P, GB, E])

            def first_max(r, k, value, onehot):
                then(dve.tensor_reduce(out=value[:], in_=logits[:], op=ALU.max, axis=AX.X), r, k + 1)
                then(dve.tensor_tensor(marked[:], logits[:], over(value), ALU.is_equal), r, k + 2)
                then(dve.tensor_tensor(marked[:], marked[:], c["first"][:, :, :E].to_broadcast([P, GB, E]), ALU.mult),
                     r, k + 3)
                then(dve.tensor_reduce(out=d1[:], in_=marked[:], op=ALU.max, axis=AX.X), r, k + 4)
                then(dve.tensor_tensor(onehot, marked[:], over(d1), ALU.is_equal), r, k + 5)

            def drop_first(r):
                then(dve.scalar_tensor_tensor(logits[:], is_first_[:], -3.0e38, logits[:], ALU.mult, ALU.add), r, 6)

            def weights(r):
                dve.wait_ge(exp_done, r + 1)
                then(dve.tensor_scalar(v1[:], d2[:], 1.0, None, ALU.add), r, 13)
                then(dve.reciprocal(v1[:], v1[:]), r, 14)
                then(dve.tensor_tensor(v2[:], v1[:], d2[:], ALU.mult), r, 15)
                then(dve.tensor_tensor(is_first_[:], is_first_[:], over(v1), ALU.mult), r, 16)
                then(dve.tensor_tensor(is_second[:], is_second[:], over(v2), ALU.mult), r, 17)
                then(dve.tensor_tensor(marked[:], is_first_[:], is_second[:], ALU.add), r, 18)
                then(dve.tensor_copy(WR[:, bass.ds(r * GB, GB), :], marked[:]), r, 19)

            def add(g, e, back=0):
                dve.wait_ge(down, g * U + ((e + 1) * FC - back * U))
                for t in range(GB):
                    n = bass.ds(g * GB + (t - back * GB), 1)
                    last = dve.scalar_tensor_tensor(X[:, n, :], pY[:, e % 2, t:t + 1, :], WR[:, n, e], X[:, n, :],
                                                    ALU.mult, ALU.add)
                last.then_inc(summed, 1)

            def pick(r, part):
                if part == 0:
                    keep(r)
                    first_max(r, 0, v1, is_first_[:] if second else WR[:, bass.ds(r * GB, GB), :])
                elif part == 1 and second:
                    drop_first(r)
                    first_max(r, 6, v2, is_second[:])
                elif part == 2 and second:
                    then(dve.tensor_tensor(d1[:], v2[:], v1[:], ALU.subtract), r, DIFFERENCE)
                elif part == 3 and second:
                    weights(r)

            def group(g, nxt):
                if not second:
                    rows_ = bass.ds(g * GB, GB)
                    dve.tensor_tensor(X[:, rows_, :], X[:, rows_, :], S[:, rows_, :], ALU.add).then_inc(joined, 1)
                    dve.wait_ge(joined, g + 1)
                for u in range(U):
                    dve.wait_ge(full, g * U + (u + 1))
                    dve.tensor_tensor(gl[:, u % NU, :], g32[:, u % NA, :], gh[:, u % NU, :],
                                      ALU.subtract).then_inc(lo, 1)
                    if u % FC == 1 and u > FC:
                        add(g, u // FC - 1)
                    elif u == 1 and not (isinstance(g, int) and g == 0):
                        add(g, E - 1, back=1)
                    if nxt and 0 <= u - STATS_AT < GB and second:
                        statistics(g + 1, u - STATS_AT)
                    if nxt and u == NORM_AT:
                        norm(g + 1)
                    if nxt and u == SPLIT_AT:
                        split(g + 1)
                    if nxt and u >= PICK_AT and (u - PICK_AT) % 2 == 0 and u < PICK_AT + 8:
                        pick(g + 1, (u - PICK_AT) // 2)

            for t in range(GB if second else 0):
                statistics(0, t)
            norm(0)
            split(0)
            for part in range(4):
                pick(0, part)
            every(dve, group)
            add(NG - 1, E - 1)

        if second:
            @block.sync
            def _(sp):
                def store(g, nxt):
                    sp.wait_ge(summed, g * E + E)
                    sp.dma_start(out.rearrange("n t d -> t n d")[:, bass.ds(g * GB, GB), :],
                                 X[:, bass.ds(g * GB, GB), :]).then_inc(stored, 16)

                every(sp, store)
                sp.wait_ge(stored, 16 * NG)


def build(nc, ins, out):
    ctx = ExitStack()
    with ctx:
        def sb(name, shape, dt):
            return ctx.enter_context(nc.sbuf_tensor(name, shape, dt))

        X = sb("X", [P, NB, D], F32)
        YW = sb("YW", [P, NB * D], F32)
        Y = YW[:].rearrange("p (n d) -> p n d", n=NB)
        SH, SL = sb("SH", [P, NSPLIT], F16), sb("SL", [P, NSPLIT], F16)
        small = sb("small", [P, NSMALL], F32)
        c = {
            "passed": ctx.enter_context(nc.semaphore("passed")),
            "parts": Parts(SH, SL),
            "small": lambda name, rows=P, k=0: small[:rows, SM_OFF[name] + k:SM_OFF[name] + k + 1],
            "ident": sb("ident", [P, P], F32), "ident16": sb("ident16", [P, P], F16), "id16": sb("identb", [P, P], U16),
            "maskM": sb("maskM", [P, HQ, P], U16), "maskS": sb("maskS", [P, HQ, P], U16),
            "sel": sb("sel", [P, H, P], F16), "row0": sb("row0", [P, P], F16),
            "cos": sb("cos", [P, P], F32), "sin": sb("sin", [P, P], F32), "mhalf": sb("mhalf", [P, 8], F32),
            "euler": sb("euler", [P, 8], F32), "zero": sb("zero", [P, 1], F32), "first": sb("first", [P, 1, E1], F32),
        }
        operands = ExitStack()

        def operand(name, shape, dt):
            c[name] = operands.enter_context(nc.sbuf_tensor(name, shape, dt))

        operand("Qd", [P, 2, HQ, HQ, TG], F16)
        operand("Ks", [P, 2, HQ, TG], F16)
        operand("V", [P, 2, GB, H, HD + 1], F32)
        operand("mT", [P, 2, P], F16)
        load_and_split(nc, c, ins["split"], [(X[:], ins["x"].rearrange("n t d -> t n d")), (small[:], ins["small"])]
                       + [(c[k][:], ins[k]) for k in CONSTANTS])
        narrow_attention(nc, c, X, Y, False)
        narrow_attention(nc, c, X, Y, True)
        operands.close()
        mixture(nc, c, X, Y, False, lambda k, a, n: c["parts"].of(("w1a", "w2a")[k], a, n))
        parts16 = YW[:].bitcast(F16)
        wide_attention(nc, c, X, ins["late"], parts16[:, :NLATE], parts16[:, NLATE:])
        mixture(nc, c, X, X, True, lambda k, a, n: tuple(
            parts16[:, start + k * E1 * FF + a:start + k * E1 * FF + a + n] for start in (0, NLATE)), out)


def shape_constants():
    f = np.float32
    b16 = lambda m: (np.ascontiguousarray(m, f).view(np.uint32) >> 16).astype(np.uint16)
    i = np.arange(P)
    sel = np.zeros((P, H, P), np.float16)
    sel[np.arange(H), np.arange(H), :] = SHIFT
    row0 = np.zeros((P, P), np.float16)
    row0[0] = 1
    maskM = np.where(i[None, :] > i[:, None], f(-1e30), f(0))
    half = HD // 2
    freq = f(1.0) / f(10000.0) ** (np.arange(half, dtype=f) / f(half))
    ang = i.astype(f)[None, :] * freq[:, None]
    d = (i % 32) // 4
    cos, sin = np.cos(ang).astype(f)[d % half], np.sin(ang).astype(f)[d % half]
    sin = np.where((d < half)[:, None], -sin, sin)
    tile4 = lambda m: b16(np.broadcast_to(m[:, None, :], (P, HQ, P)))
    return {"ident": np.eye(P, dtype=f), "ident16": np.eye(P, dtype=np.float16), "id16": b16(np.eye(P)),
            "maskM": tile4(maskM), "maskS": tile4(maskM.T), "sel": sel, "row0": row0,
            "cos": cos.astype(f), "sin": sin.astype(f), "mhalf": np.full((P, 8), -0.5, f),
            "euler": np.full((P, 8), np.e, f), "zero": np.zeros((P, 1), f),
            "first": np.ascontiguousarray(np.broadcast_to(f(E1) - np.arange(E1, dtype=f), (P, 1, E1)))}


def lay_out(a):
    f = np.float32
    r = np.arange(D)
    row_head, row_dim = HQ * (r % 4) + r // 32, (r % 32) // 4
    perm = row_head * HD + row_dim
    swap = row_head * HD + (row_dim + HD // 2) % HD
    full = lambda m: np.pad(m, ((0, P - m.shape[0]), (0, 0)))
    row = lambda v: full(v.reshape(1, -1))
    up = lambda w: w.transpose(2, 0, 1).reshape(D, -1)
    down = lambda w: w.reshape(w.shape[0], D, FC, P).transpose(3, 0, 2, 1).reshape(P, -1)
    cols = {
        "ctx": a["ctx_1024"].transpose(2, 0, 1).reshape(D, -1),
        "a_q": a["L0_xattn_Wq"][:, perm], "a_k": a["L0_xattn_Wk"][:, perm], "a_v": a["L0_xattn_Wv"],
        "a_o": a["L0_xattn_Wo"], "a_bo": row(a["L0_xattn_bo"]),
        "m_q": a["L0_ffn_Wq"].T[:, perm], "m_qs": a["L0_ffn_Wq"].T[:, swap], "m_kv": a["L0_ffn_Wdkv"].T,
        "m_k": full(a["L0_ffn_Wuk"].T[:, perm]), "m_ks": full(a["L0_ffn_Wuk"].T[:, swap]),
        "m_v": full(a["L0_ffn_Wuv"].T), "m_o": a["L0_ffn_Wo"].T,
        "w_q": a["L1_xattn_Wq"], "w_k": a["L1_xattn_Wk"], "w_v": a["L1_xattn_Wv"],
        "w_o": a["L1_xattn_Wo"].reshape(FC, P, D).transpose(1, 0, 2).reshape(P, -1), "w_bo": row(a["L1_xattn_bo"]),
        "gate": a["L0_ffn_gate_w"].T, "gate_b": row(a["L0_ffn_gate_b"]), "router": a["L1_ffn_router_w"].T,
        "b2": row(a["L0_ffn_b2"]), "w1a": up(a["L0_ffn_W1"]), "w2a": down(a["L0_ffn_W2"]),
    }
    split = np.zeros((P, NSPLIT), f)
    for name, width in SPLIT_COLS:
        split[:, OFF[name]:OFF[name] + width] = cols[name]
    late = np.concatenate([up(a["L1_ffn_expert_w1"]), down(a["L1_ffn_expert_w2"])], axis=1)
    small = np.zeros((P, NSMALL), f)
    for name, v in (("bq", a["L0_xattn_bq"][perm]), ("bk", a["L0_xattn_bk"][perm]), ("bv", a["L0_xattn_bv"]),
                    ("n1", a["L0_ffn_norm1_w"]), ("n2", a["L0_ffn_norm2_w"]), ("lg", a["L0_ffn_ln_g"]),
                    ("lb", a["L0_ffn_ln_b"])):
        small[:len(v), SM_OFF[name]] = v
    small[:, SM_OFF["b1"]:] = a["L0_ffn_b1"].reshape(E0 * FC, P).T
    return {"x": a["x"], "split": split, "late": np.ascontiguousarray(late), "small": small}


def kernel(**inputs):
    import concourse.bacc as bacc
    from concourse.bass_utils import run_bass_kernel_spmd

    a = {k: np.asarray(v) for k, v in inputs.items()}
    arrays = {f"in_{k}": np.ascontiguousarray(v) for k, v in (lay_out(a) | shape_constants()).items()}
    nc = bacc.Bacc("TRN2", target_bir_lowering=False, num_devices=1)
    ins = {k[3:]: nc.dram_tensor(k, v.shape, mybir.dt.from_np(v.dtype), kind="ExternalInput").ap()
           for k, v in arrays.items()}
    out = nc.dram_tensor("out", a["x"].shape, F32, kind="ExternalOutput").ap()
    build(nc, ins, out)
    return run_bass_kernel_spmd(nc, [arrays], core_ids=[0]).results[0]["out"]
```
